# Optimizing a Trainium2 kernel written in Bass

```python
import numpy as np
import jax
import jax.numpy as jnp

def _softmax(x, axis=-1):
    return jax.nn.softmax(x, axis=axis)

def _gelu(x):
    return jax.nn.gelu(x, approximate=True)

def _silu(x):
    return jax.nn.silu(x)

def _sigmoid(x):
    return jax.nn.sigmoid(x)

def _layernorm(x, axis=-1, eps=1e-05):
    m = jnp.mean(x, axis=axis, keepdims=True)
    v = jnp.var(x, axis=axis, keepdims=True)
    return (x - m) / jnp.sqrt(v + eps)

def _scatter_add(tgt, idx, src, axis=0):
    return tgt.at[idx].add(src)

def _segment_sum(src, seg, n):
    return jax.ops.segment_sum(src, seg, n)
kernel_name = 'mk_adaln_d1_jaxref_r8_50773b'

def setup_inputs(seed: int=0):
    np.random.seed(seed)
    _w = jnp.asarray

    def _L0_attn_setup():
        import jax, jax.numpy as jnp
        import numpy as np
        D_MODEL = 128
        D_INNER = 256
        D_STATE = 16
        DT_RANK = 64
        K_CONV = 4
        D_FF = 512
        EPS = 1e-06

        def _rms(x, w):
            return x * jax.lax.rsqrt(jnp.mean(x * x, axis=-1, keepdims=True) + EPS) * w

        def _reference_tuple_inner(hidden_states, in_proj_w, conv_w, conv_b, x_proj_w, dt_proj_w, dt_proj_b, dt_ln_w, b_ln_w, c_ln_w, A_log, D_skip, out_proj_w, input_ln_w, pre_moe_ln_w, gate_w, up_w, down_w):
            B, S, _ = hidden_states.shape
            residual = hidden_states
            h = _rms(hidden_states, input_ln_w)
            xz = h @ in_proj_w
            x, z = jnp.split(xz, 2, axis=-1)
            xt = jnp.transpose(x, (0, 2, 1))
            conv_state = xt[:, :, -K_CONV:]
            y = jax.lax.conv_general_dilated(xt, conv_w[:, None, :], window_strides=(1,), padding=[(K_CONV - 1, 0)], feature_group_count=D_INNER, dimension_numbers=('NCH', 'OIH', 'NCH'))
            y = y + conv_b[None, :, None]
            x = jax.nn.silu(jnp.transpose(y, (0, 2, 1)))
            proj = x @ x_proj_w
            dt_raw = proj[..., :DT_RANK]
            B_raw = proj[..., DT_RANK:DT_RANK + D_STATE]
            C_raw = proj[..., DT_RANK + D_STATE:]
            dt = jax.nn.softplus(_rms(dt_raw, dt_ln_w) @ dt_proj_w + dt_proj_b)
            Bm = _rms(B_raw, b_ln_w)
            Cm = _rms(C_raw, c_ln_w)
            A = -jnp.exp(A_log)

            def step(hstate, ins):
                x_t, dt_t, B_t, C_t = ins
                dA = jnp.exp(dt_t[..., None] * A)
                hstate = hstate * dA + (dt_t * x_t)[..., None] * B_t[:, None, :]
                y_t = jnp.einsum('bdn,bn->bd', hstate, C_t)
                return (hstate, y_t)
            h0 = jnp.zeros((B, D_INNER, D_STATE), x.dtype)
            xs = (jnp.swapaxes(x, 0, 1), jnp.swapaxes(dt, 0, 1), jnp.swapaxes(Bm, 0, 1), jnp.swapaxes(Cm, 0, 1))
            ssm_state, ys = jax.lax.scan(step, h0, xs)
            y = jnp.swapaxes(ys, 0, 1) + x * D_skip
            y = y * jax.nn.silu(z)
            mamba_out = y @ out_proj_w
            hidden = residual + mamba_out
            residual = hidden
            hn = _rms(hidden, pre_moe_ln_w)
            ff = jax.nn.silu(hn @ gate_w) * (hn @ up_w) @ down_w
            out = residual + ff
            return (out, conv_state, ssm_state)
        key = jax.random.key(seed)
        ks = jax.random.split(key, 20)
        s = lambda i, shape, scale: jax.random.normal(ks[i], shape, dtype=jnp.float32) * scale
        inp = {'hidden_states': s(0, (2, 256, D_MODEL), 1.0), 'in_proj_w': s(1, (D_MODEL, 2 * D_INNER), D_MODEL ** (-0.5)), 'conv_w': s(2, (D_INNER, K_CONV), 0.3), 'conv_b': jnp.zeros((D_INNER,), jnp.float32), 'x_proj_w': s(3, (D_INNER, DT_RANK + 2 * D_STATE), D_INNER ** (-0.5)), 'dt_proj_w': s(4, (DT_RANK, D_INNER), DT_RANK ** (-0.5)), 'dt_proj_b': jnp.full((D_INNER,), -2.0, jnp.float32), 'dt_ln_w': jnp.ones((DT_RANK,), jnp.float32), 'b_ln_w': jnp.ones((D_STATE,), jnp.float32), 'c_ln_w': jnp.ones((D_STATE,), jnp.float32), 'A_log': jnp.log(jnp.broadcast_to(jnp.arange(1, D_STATE + 1, dtype=jnp.float32), (D_INNER, D_STATE))), 'D_skip': jnp.ones((D_INNER,), jnp.float32), 'out_proj_w': s(5, (D_INNER, D_MODEL), D_INNER ** (-0.5)), 'input_ln_w': jnp.ones((D_MODEL,), jnp.float32), 'pre_moe_ln_w': jnp.ones((D_MODEL,), jnp.float32), 'gate_w': s(6, (D_MODEL, D_FF), D_MODEL ** (-0.5)), 'up_w': s(7, (D_MODEL, D_FF), D_MODEL ** (-0.5)), 'down_w': s(8, (D_FF, D_MODEL), D_FF ** (-0.5))}
        return inp
    _L0_attn_in = _L0_attn_setup()

    def _L0_ffn_setup():
        import jax, jax.numpy as jnp
        import numpy as np
        NUM_EXPERTS = 160
        TOP_K = 8
        ROUTED_SCALE = 2.5
        HIDDEN = 128
        INTER = 64
        key = jax.random.key(seed)
        ks = jax.random.split(key, 7)
        B, S = (1, 256)
        return {'hidden_states': jax.random.normal(ks[0], (B, S, HIDDEN), dtype=jnp.float32), 'router_w': jax.random.normal(ks[1], (NUM_EXPERTS, HIDDEN), dtype=jnp.float32) * 0.02, 'expert_bias': jnp.zeros((NUM_EXPERTS,), dtype=jnp.float32), 'w_gate': jax.random.normal(ks[2], (NUM_EXPERTS, INTER, HIDDEN), dtype=jnp.float32) * 0.02, 'w_down': jax.random.normal(ks[3], (NUM_EXPERTS, HIDDEN, INTER), dtype=jnp.float32) * 0.02, 'w_gate_shared': jax.random.normal(ks[4], (INTER, HIDDEN), dtype=jnp.float32) * 0.02, 'w_down_shared': jax.random.normal(ks[5], (HIDDEN, INTER), dtype=jnp.float32) * 0.02}
    _L0_ffn_in = _L0_ffn_setup()
    _L0_c = _w((lambda *s: np.random.randn(*s).astype(np.float32) * 0.05)(8, 128))
    _L0_wmod = _w((lambda *s: np.random.randn(*s).astype(np.float32) * 0.05)(128, 6 * 128) * 128 ** (-0.5))
    _d = {'L0_attn_hidden_states': _L0_attn_in['hidden_states'], 'L0_attn_in_proj_w': _L0_attn_in['in_proj_w'], 'L0_attn_conv_w': _L0_attn_in['conv_w'], 'L0_attn_conv_b': _L0_attn_in['conv_b'], 'L0_attn_x_proj_w': _L0_attn_in['x_proj_w'], 'L0_attn_dt_proj_w': _L0_attn_in['dt_proj_w'], 'L0_attn_dt_proj_b': _L0_attn_in['dt_proj_b'], 'L0_attn_dt_ln_w': _L0_attn_in['dt_ln_w'], 'L0_attn_b_ln_w': _L0_attn_in['b_ln_w'], 'L0_attn_c_ln_w': _L0_attn_in['c_ln_w'], 'L0_attn_A_log': _L0_attn_in['A_log'], 'L0_attn_D_skip': _L0_attn_in['D_skip'], 'L0_attn_out_proj_w': _L0_attn_in['out_proj_w'], 'L0_attn_input_ln_w': _L0_attn_in['input_ln_w'], 'L0_attn_pre_moe_ln_w': _L0_attn_in['pre_moe_ln_w'], 'L0_attn_gate_w': _L0_attn_in['gate_w'], 'L0_attn_up_w': _L0_attn_in['up_w'], 'L0_attn_down_w': _L0_attn_in['down_w'], 'L0_ffn_router_w': _L0_ffn_in['router_w'], 'L0_ffn_expert_bias': _L0_ffn_in['expert_bias'], 'L0_ffn_w_gate': _L0_ffn_in['w_gate'], 'L0_ffn_w_down': _L0_ffn_in['w_down'], 'L0_ffn_w_gate_shared': _L0_ffn_in['w_gate_shared'], 'L0_ffn_w_down_shared': _L0_ffn_in['w_down_shared'], 'L0_c': _L0_c, 'L0_wmod': _L0_wmod}
    _x0 = _d['L0_attn_hidden_states']
    _d['L0_attn_hidden_states'] = jax.random.normal(jax.random.fold_in(jax.random.key(seed), 1), (8, 512, 128), dtype=_x0.dtype)
    del _x0
    return _d

def reference(L0_attn_hidden_states, L0_attn_in_proj_w, L0_attn_conv_w, L0_attn_conv_b, L0_attn_x_proj_w, L0_attn_dt_proj_w, L0_attn_dt_proj_b, L0_attn_dt_ln_w, L0_attn_b_ln_w, L0_attn_c_ln_w, L0_attn_A_log, L0_attn_D_skip, L0_attn_out_proj_w, L0_attn_input_ln_w, L0_attn_pre_moe_ln_w, L0_attn_gate_w, L0_attn_up_w, L0_attn_down_w, L0_ffn_router_w, L0_ffn_expert_bias, L0_ffn_w_gate, L0_ffn_w_down, L0_ffn_w_gate_shared, L0_ffn_w_down_shared, L0_c, L0_wmod):

    def _L0_attn_ref(hidden_states, in_proj_w, conv_w, conv_b, x_proj_w, dt_proj_w, dt_proj_b, dt_ln_w, b_ln_w, c_ln_w, A_log, D_skip, out_proj_w, input_ln_w, pre_moe_ln_w, gate_w, up_w, down_w):
        import jax, jax.numpy as jnp
        import numpy as np
        D_MODEL = 128
        D_INNER = 256
        D_STATE = 16
        DT_RANK = 64
        K_CONV = 4
        D_FF = 512
        EPS = 1e-06

        def _rms(x, w):
            return x * jax.lax.rsqrt(jnp.mean(x * x, axis=-1, keepdims=True) + EPS) * w

        def _reference_tuple_inner(hidden_states, in_proj_w, conv_w, conv_b, x_proj_w, dt_proj_w, dt_proj_b, dt_ln_w, b_ln_w, c_ln_w, A_log, D_skip, out_proj_w, input_ln_w, pre_moe_ln_w, gate_w, up_w, down_w):
            B, S, _ = hidden_states.shape
            residual = hidden_states
            h = _rms(hidden_states, input_ln_w)
            xz = h @ in_proj_w
            x, z = jnp.split(xz, 2, axis=-1)
            xt = jnp.transpose(x, (0, 2, 1))
            conv_state = xt[:, :, -K_CONV:]
            y = jax.lax.conv_general_dilated(xt, conv_w[:, None, :], window_strides=(1,), padding=[(K_CONV - 1, 0)], feature_group_count=D_INNER, dimension_numbers=('NCH', 'OIH', 'NCH'))
            y = y + conv_b[None, :, None]
            x = jax.nn.silu(jnp.transpose(y, (0, 2, 1)))
            proj = x @ x_proj_w
            dt_raw = proj[..., :DT_RANK]
            B_raw = proj[..., DT_RANK:DT_RANK + D_STATE]
            C_raw = proj[..., DT_RANK + D_STATE:]
            dt = jax.nn.softplus(_rms(dt_raw, dt_ln_w) @ dt_proj_w + dt_proj_b)
            Bm = _rms(B_raw, b_ln_w)
            Cm = _rms(C_raw, c_ln_w)
            A = -jnp.exp(A_log)

            def step(hstate, ins):
                x_t, dt_t, B_t, C_t = ins
                dA = jnp.exp(dt_t[..., None] * A)
                hstate = hstate * dA + (dt_t * x_t)[..., None] * B_t[:, None, :]
                y_t = jnp.einsum('bdn,bn->bd', hstate, C_t)
                return (hstate, y_t)
            h0 = jnp.zeros((B, D_INNER, D_STATE), x.dtype)
            xs = (jnp.swapaxes(x, 0, 1), jnp.swapaxes(dt, 0, 1), jnp.swapaxes(Bm, 0, 1), jnp.swapaxes(Cm, 0, 1))
            ssm_state, ys = jax.lax.scan(step, h0, xs)
            y = jnp.swapaxes(ys, 0, 1) + x * D_skip
            y = y * jax.nn.silu(z)
            mamba_out = y @ out_proj_w
            hidden = residual + mamba_out
            residual = hidden
            hn = _rms(hidden, pre_moe_ln_w)
            ff = jax.nn.silu(hn @ gate_w) * (hn @ up_w) @ down_w
            out = residual + ff
            return (out, conv_state, ssm_state)
        return _reference_tuple_inner(hidden_states, in_proj_w, conv_w, conv_b, x_proj_w, dt_proj_w, dt_proj_b, dt_ln_w, b_ln_w, c_ln_w, A_log, D_skip, out_proj_w, input_ln_w, pre_moe_ln_w, gate_w, up_w, down_w)[0]

    def _L0_ffn_ref(hidden_states, router_w, expert_bias, w_gate, w_down, w_gate_shared, w_down_shared):
        import jax, jax.numpy as jnp
        import numpy as np
        NUM_EXPERTS = 160
        TOP_K = 8
        ROUTED_SCALE = 2.5
        HIDDEN = 128
        INTER = 64
        B, S, H = hidden_states.shape
        x = hidden_states.reshape(-1, H)
        T = x.shape[0]
        logits = x @ router_w.T + expert_bias[None, :]
        probs = jax.nn.sigmoid(logits)
        top_w, top_idx = jax.lax.top_k(probs, TOP_K)
        top_w = top_w / (jnp.sum(top_w, axis=-1, keepdims=True) + 1e-09)
        top_w = top_w * ROUTED_SCALE
        combine = jnp.zeros((T, NUM_EXPERTS), dtype=x.dtype)
        combine = combine.at[jnp.arange(T)[:, None], top_idx].set(top_w)
        h1 = jax.nn.silu(jnp.einsum('th,eih->eti', x, w_gate))
        h1w = h1 * combine.T[:, :, None]
        routed = jnp.einsum('eti,ehi->th', h1w, w_down)
        shared = jax.nn.silu(x @ w_gate_shared.T) @ w_down_shared.T
        return (routed + shared).reshape(B, S, H)
    x = L0_attn_hidden_states
    mod = (_silu(L0_c) @ L0_wmod).reshape(L0_c.shape[0], 6, 1, -1)
    sa, ca, ga, sb, cb, gb = (mod[:, 0], mod[:, 1], mod[:, 2], mod[:, 3], mod[:, 4], mod[:, 5])
    ga = (2 * (ga >= 0) - 1) * jnp.maximum(jnp.abs(ga), 0.25)
    gb = (2 * (gb >= 0) - 1) * jnp.maximum(jnp.abs(gb), 0.25)
    h = _layernorm(x, axis=-1) * (1 + ca) + sa
    x = x + ga * _L0_attn_ref(h, L0_attn_in_proj_w, L0_attn_conv_w, L0_attn_conv_b, L0_attn_x_proj_w, L0_attn_dt_proj_w, L0_attn_dt_proj_b, L0_attn_dt_ln_w, L0_attn_b_ln_w, L0_attn_c_ln_w, L0_attn_A_log, L0_attn_D_skip, L0_attn_out_proj_w, L0_attn_input_ln_w, L0_attn_pre_moe_ln_w, L0_attn_gate_w, L0_attn_up_w, L0_attn_down_w)
    h = _layernorm(x, axis=-1) * (1 + cb) + sb
    x = x + gb * _L0_ffn_ref(h, L0_ffn_router_w, L0_ffn_expert_bias, L0_ffn_w_gate, L0_ffn_w_down, L0_ffn_w_gate_shared, L0_ffn_w_down_shared)
    return x

_drawn_inputs = setup_inputs


def setup_inputs(seed=0):
    import zlib

    import numpy as np

    out = dict(_drawn_inputs(seed))
    spreads = {'L0_attn_conv_b': (0.0, 0.1),
     'L0_attn_dt_proj_b': (-2.0, 0.6),
     'L0_attn_dt_ln_w': (1.0, 0.6),
     'L0_attn_b_ln_w': (1.0, 0.6),
     'L0_attn_c_ln_w': (1.0, 0.6),
     'L0_attn_D_skip': (1.0, 0.6),
     'L0_attn_input_ln_w': (1.0, 0.2),
     'L0_attn_pre_moe_ln_w': (1.0, 0.2),
     'L0_ffn_expert_bias': (0.0, 0.8)}
    factors = {'L0_ffn_router_w': 8.0,
     'L0_ffn_w_gate': 8.0,
     'L0_ffn_w_down': 8.0,
     'L0_ffn_w_gate_shared': 8.0,
     'L0_ffn_w_down_shared': 8.0}
    for name, (base, spread) in spreads.items():
        noise = np.random.default_rng([zlib.crc32(name.encode()), seed]).standard_normal(out[name].shape)
        drawn = base * np.exp(spread * noise) if base else spread * noise
        out[name] = jnp.asarray(drawn.astype(out[name].dtype))
    for name, factor in factors.items():
        out[name] = (out[name] * factor).astype(out[name].dtype)
    return out
```

```python
from contextlib import ExitStack

import concourse.bass as bass
from concourse import mybir

ALU = mybir.AluOpType
ACT = mybir.ActivationFunctionType
BF16 = mybir.dt.bfloat16
F32 = mybir.dt.float32
F32R = mybir.dt.float32r
AX_X = mybir.AxisListType.X

P = 128
DM = 128
DI = 256
HALVES = DI // P
NS = 16
RANK = 64
TAPS = 4
FF = 512
FB = FF // P
EXPERTS = 160
TOPK = 8
INTER = 64
SCALE = 2.5
PROJ = RANK + 2 * NS
SEQ = 512
TILES = SEQ // P
EPS_LN = 1e-5
EPS_RMS = 1e-6

PAIRS = EXPERTS // 2
GROUPS = EXPERTS // 32
GP = 16
RING = 10
HRING = 5
BLOCKS = PAIRS + 1
LAG = 3
LOOP_PAIRS = 8
BEFORE = 3
STATES_PER_TURN = 4
TURNS = NS // STATES_PER_TURN
PER_TURN = LOOP_PAIRS * GROUPS // TURNS
FIRST_LOOP = BEFORE * GROUPS
FIRST_AFTER = FIRST_LOOP + LOOP_PAIRS * GROUPS
SPLIT = 2
CUTS = PAIRS // SPLIT // TURNS
OUTS = RING // SPLIT
TURN_SHARE = [0, 3, 5, 8, 10]
FFN_BANKS = [(0, 2), (1, 0), (2, 1), (0, 2)]
assert PER_TURN == RING and RING % 2 == 0 and RING % HRING == 0 and FIRST_LOOP % HRING == 0
assert CUTS == PER_TURN == HRING * SEQ // (SPLIT * P) and CUTS % OUTS == 0

A_POINTS = {f"a{i + 1}": i for i in range(FIRST_LOOP)}
C_POINTS = {f"c{i + 1}": FIRST_AFTER + i for i in range(BLOCKS - FIRST_AFTER)}
POINTS = {**A_POINTS, **C_POINTS}


class Block:

    def __init__(self, q, slot, pair, lap):
        self.q, self.slot, self.pair, self.lap = q, slot, pair, lap
        self.group, self.h_slot, self.two = slot % GROUPS, slot % HRING, slot % 2

    def before(self, n):
        return Block(self.q - n, (self.slot - n) % RING, None, None)


def block_at(q):
    return Block(q, q % RING, q // GROUPS if q < PAIRS else None, q // RING)


def block_in_turn(turn, k):
    at = FIRST_LOOP + k
    return Block(PER_TURN * turn + at, at % RING, PER_TURN // GROUPS * turn + at // GROUPS, turn + at // RING)


def block_in_lap(lap, k):
    return Block(RING * lap + k, k, RING // GROUPS * lap + k // GROUPS, lap)


class Signal:

    def __init__(self, sem, per_row, credit):
        self.sem, self.per_row, self.credit = sem, per_row, credit

    def by(self, row, k=None):
        return row * self.per_row + (self.per_row if k is None else k) + self.credit


def build(nc, A, out, rows):
    with ExitStack() as ctx:
        def sb(name, shape, dt=F32):
            return ctx.enter_context(nc.sbuf_tensor(name, shape, dt))

        def bank(name, dt=F32):
            return ctx.enter_context(nc.psum_tensor(name, [P, 2048 // (4 if dt == F32 else 2)], dt))

        def sig(name, per_row=1, credit=0):
            return Signal(ctx.enter_context(nc.semaphore(name)), per_row, credit)

        ident = sb("ident", [P, P])
        identb = sb("identb", [P, P], BF16)
        pair_sel = sb("pair_sel", [96, GP, P], BF16)
        row_sel = sb("row_sel", [96, 2 * NS, P], BF16)
        neg_half = sb("neg_half", [P, 16])
        raised = sb("raised", [1, 7 + OUTS])
        in_w = sb("in_w", [P, 2 * DI])
        conv_w = sb("conv_w", [P, HALVES, TAPS])
        cols = sb("cols", [P, 9])
        xproj_w = sb("xproj_w", [P, HALVES, PROJ])
        dtproj_w = sb("dtproj_w", [RANK, DI])
        a_neg = sb("a_neg", [P, HALVES, NS])
        out_w = sb("out_w", [P, HALVES, DM])
        gate_w = sb("gate_w", [P, FF])
        up_w = sb("up_w", [P, FF])
        down_w = sb("down_w", [P, FB, DM])
        bc_w = sb("bc_w", [P, 2, NS])
        bias_w = sb("bias_w", [P, EXPERTS])
        router_w = sb("router_w", [P, EXPERTS])
        shared_up = sb("shared_up", [P, INTER])
        shared_parts = sb("shared_parts", [P, 2, INTER], F32R)
        shared_down = sb("shared_down", [INTER, DM])
        c_cm = sb("c_cm", [P, rows])
        c_th = sb("c_th", [P, rows])
        c_sl = sb("c_sl", [P, rows])
        mod_w = sb("mod_w", [P, 6 * DM])
        mod_all = sb("mod_all", [rows, 6, DM])
        mod_abs = sb("mod_abs", [rows, 2, DM])
        mod_sgn = sb("mod_sgn", [rows, 2, DM])
        CONV_B, DT_B, D_HALF, IN_LN, PRE_LN, DT_LN = 0, 2, 4, 6, 7, 8

        mod = sb("mod", [P, 6, DM])
        SH1, SC1, G1, SH2, SC2, G2 = range(6)
        x_tm = sb("x_tm", [P, TILES, DM])
        stats = sb("stats", [P, TILES, 6])
        mv = sb("mv", [P, TILES, 2])
        var1 = sb("var1", [P, TILES])
        rstd1 = sb("rstd1", [P, TILES])
        xn_tm = sb("xn_tm", [P, TILES, DM])
        hs_tm = sb("hs_tm", [P, TILES, DM])
        h_tm = sb("h_tm", [P, TILES, DM])
        junk = sb("junk", [P, TILES, DM])
        ss1 = sb("ss1", [P, TILES])
        ms1 = sb("ms1", [P, TILES])
        r1 = sb("r1", [P, TILES])
        hn_tm = sb("hn_tm", [P, TILES, DM])
        h_cm = sb("h_cm", [P, SEQ])
        conv = [sb(f"conv{h}", [P, SEQ]) for h in range(HALVES)]
        conv_th = [sb(f"conv_th{h}", [P, SEQ]) for h in range(HALVES)]
        x2 = [sb(f"x2_{h}", [P, SEQ]) for h in range(HALVES)]
        z_th = [sb(f"z_th{h}", [P, SEQ]) for h in range(HALVES)]
        z2 = [sb(f"z2_{h}", [P, SEQ]) for h in range(HALVES)]
        proj_sq = sb("proj_sq", [P, TILES, PROJ])
        ss3 = sb("ss3", [P, TILES, 3])
        ms3 = sb("ms3", [P, TILES, 3])
        r3 = sb("r3", [P, TILES, 3])
        dtn_tm = sb("dtn_tm", [P, TILES, RANK])
        bcn = sb("bcn", [P, TILES, 2 * NS])
        bcs = sb("bcs", [P, TILES, 2 * NS])
        bc_rem = sb("bc_rem", [P, TILES, 2 * NS])
        bc_parts = sb("bc_parts", [P, TILES, 3, 2 * NS], BF16)
        dtn_cm = sb("dtn_cm", [RANK, SEQ])
        bc_cm = sb("bc_cm", [96, SEQ], BF16)
        dt_min = conv
        dt_exp = conv_th
        dt_ln = z_th
        dt = [sb(f"dt{h}", [P, SEQ]) for h in range(HALVES)]
        dtx = [sb(f"dtx{h}", [P, SEQ]) for h in range(HALVES)]
        c_sb = [sb(f"c_sb{i}", [P, SEQ]) for i in range(2)]
        dbx = [sb(f"dbx{h}", [P, SEQ]) for h in range(HALVES)]
        state = [[sb(f"state{i}{h}", [P, SEQ]) for h in range(HALVES)] for i in range(2)]
        read = [sb(f"read{h}", [P, SEQ]) for h in range(HALVES)]
        y = [sb(f"y{h}", [P, SEQ]) for h in range(HALVES)]
        yz = [sb(f"yz{h}", [P, SEQ]) for h in range(HALVES)]
        hid_tm = sb("hid_tm", [P, TILES, DM])
        ss2 = sb("ss2", [P, TILES])
        ms2 = sb("ms2", [P, TILES])
        r2 = sb("r2", [P, TILES])
        f_th, f_v, f_act = read, dbx, dt + dtx
        att_tm = sb("att_tm", [P, TILES, DM])
        gat_tm = sb("gat_tm", [P, TILES, DM])
        x1_tm = sb("x1_tm", [P, TILES, DM])
        stats2 = sb("stats2", [P, TILES, 6])
        mv2 = sb("mv2", [P, TILES, 2])
        var2 = sb("var2", [P, TILES])
        rstd2 = sb("rstd2", [P, TILES])
        xn2_tm, hs2_tm = xn_tm, hs_tm
        h2_tm = sb("h2_tm", [P, TILES, DM])
        h2_cm = sb("h2_cm", [P, SEQ])
        logits = sb("logits", [P, TILES, EXPERTS])
        l_exp = sb("l_exp", [P, TILES, EXPERTS])
        l_one = logits
        probs = sb("probs", [P, TILES, EXPERTS])
        top = sb("top", [P, TILES, TOPK])
        rest = sb("rest", [P, TILES, EXPERTS])
        chosen = sb("chosen", [P, TILES, EXPERTS])
        top_sum = sb("top_sum", [P, TILES])
        top_inv = sb("top_inv", [P, TILES])
        top_fac = sb("top_fac", [P, TILES])
        comb = sb("comb", [P, TILES, EXPERTS])
        comb_rem = sb("comb_rem", [P, TILES, EXPERTS])
        comb_parts = sb("comb_parts", [P, TILES, GROUPS, 3, 32], BF16)

        h2_live = [sb(f"h2_live{i}", [P, SEQ], F32R) for i in range(2)]
        comb_live = sb("comb_live", [96, GROUPS, SEQ], BF16)
        x1_live = sb("x1_live", [P, TILES, DM])
        g2_live = sb("g2_live", [P, DM])
        up_ring = sb("up_ring", [P, RING, 2, P])
        up_exact = up_ring[:, :, :, :].bitcast(F32R)
        down_ring = sb("down_ring", [P, RING, P])
        e_th = [sb(f"e_th{i}", [P, SEQ]) for i in range(2)]
        e_h = sb("e_h", [P, HRING, SEQ])
        e_out = sb("e_out", [P, SEQ])
        raw_up = e_h[:, :, :].rearrange("p h s -> p (h s)").rearrange("p (k i n) -> p k i n", i=SPLIT, n=P)
        e_gat = sb("e_gat", [P, TILES, DM])
        o_tm = sb("o_tm", [P, TILES, DM])

        up_bank = [bank("up_bank0"), bank("up_bank1")]
        comb_bank = [bank("comb_bank0"), bank("comb_bank1")]
        acc_bank = bank("acc_bank")
        M = [bank("m0"), bank("m1"), bank("m2")]
        b_bank, c_bank, da_bank = M
        Mb = [b[:, :].bitcast(BF16) for b in M]

        c_loaded = [sig(f"c_loaded{i}") for i in range(3)]
        ident_zero, ident_done = sig("ident_zero"), sig("ident_done")
        sel_done = sig("sel_done")
        prep = sig("prep")
        c_tanh, c_silu, mod_mm, mod_raw, mod_half, mod_done, mod_out = (
            sig(n) for n in ("c_tanh", "c_silu", "mod_mm", "mod_raw", "mod_half", "mod_done", "mod_out"))
        a_exp = sig("a_exp")
        x_in, mod_in = sig("x_in", 16), sig("mod_in", 16)
        ln1_st, ln1_mv, ln1_var, ln1_rs = sig("ln1_st", 4), sig("ln1_mv", 4), sig("ln1_var"), sig("ln1_rs")
        xn_done, hs_done, h_done = sig("xn_done", 4), sig("hs_done"), sig("h_done")
        ss1_done, ms1_done, r1_done, hn_done = sig("ss1_done", 4), sig("ms1_done"), sig("r1_done"), sig("hn_done", 4)
        hT_mm, hT_done = sig("hT_mm"), sig("hT_done")
        in_mm = sig("in_mm", 4)
        conv_done = sig("conv_done", 2 * TAPS)
        convth_done, x2_done = sig("convth_done", 2), sig("x2_done", 2)
        zth_done, z2_done = sig("zth_done", 2), sig("z2_done", 2)
        proj_mm, sq3_done, ss3_done, ms3_done, r3_done = (
            sig("proj_mm"), sig("sq3_done"), sig("ss3_done", 2), sig("ms3_done", 2), sig("r3_done"))
        dtn_done, bcn_done, bcs_done, bcp_done = sig("dtn_done"), sig("bcn_done"), sig("bcs_done"), sig("bcp_done", 4)
        dtT_mm, bcT_mm, dtT_done, bcT_done = sig("dtT_mm"), sig("bcT_mm"), sig("dtT_done"), sig("bcT_done")
        dt_mm, dtmin_done, dtexp_done, dtln_done, dt_done = (
            sig("dt_mm", 2), sig("dtmin_done", 2), sig("dtexp_done", 2), sig("dtln_done", 2), sig("dt_done", 2))
        dtx_done, y0_done = sig("dtx_done", 2), sig("y0_done", 2)
        b_mm, cn_mm, c_copied = sig("b_mm", NS), sig("cn_mm", NS), sig("c_copied", NS, credit=1)
        da_done, dbx_done, scan_done = sig("da_done", 2 * NS), sig("dbx_done", 2 * NS, credit=1), sig("scan_done", 2 * NS, credit=1)
        read_done, y_done = sig("read_done", 2 * NS, credit=4), sig("y_done", 2 * NS, credit=2)
        yz_done, outp_mm, hid_done = sig("yz_done", 2), sig("outp_mm"), sig("hid_done")
        ss2_done, ms2_done, r2_done, hn2_done = sig("ss2_done", 4), sig("ms2_done"), sig("r2_done"), sig("hn2_done", 4)
        hT2_mm, hT2_done = sig("hT2_mm"), sig("hT2_done")
        fg_mm, fu_mm, fth_done, fv_done, fa_done = (
            sig("fg_mm", FB), sig("fu_mm", FB), sig("fth_done", FB), sig("fv_done", FB), sig("fa_done", FB))
        down_mm, att_done, gat_done, x1_done = sig("down_mm"), sig("att_done"), sig("gat_done"), sig("x1_done")
        ln2_st, ln2_mv, ln2_var, ln2_rs = sig("ln2_st", 4), sig("ln2_mv", 4), sig("ln2_var"), sig("ln2_rs")
        xn2_done, hs2_done, h2_done = sig("xn2_done", 4), sig("hs2_done"), sig("h2_done")
        h2T_mm, h2T_done = sig("h2T_mm"), sig("h2T_done")
        rt_mm, lg_done, lexp_done, lone_done, probs_done = (
            sig("rt_mm"), sig("lg_done", 2), sig("lexp_done"), sig("lone_done"), sig("probs_done", 4))
        top_done, rest_done, chosen_done = sig("top_done", 4), sig("rest_done", 4), sig("chosen_done", 4)
        tops_done, comb_done, combp_done = sig("tops_done", 3), sig("comb_done", 4), sig("combp_done", 4)
        combT_mm = sig("combT_mm")
        live_h2, live_comb, live_x1 = sig("live_h2"), sig("live_comb", 3), sig("live_x1", 2)
        raw_in = [sig(f"raw_in{k}") for k in range(CUTS)]
        hi_done, lo_done = sig("hi_done"), sig("lo_done")
        split_out = [sig(f"split_out{k}", credit=16) for k in range(OUTS)]
        shared_split, live_lo = sig("shared_split"), sig("live_lo")
        w_in = [sig(f"w_in{k}", 32 * PAIRS // RING) for k in range(RING)]
        e_up, e_c, e_tanh, e_vd, e_hd, e_down = (
            sig(n, BLOCKS) for n in ("e_up", "e_c", "e_tanh", "e_vd", "e_hd", "e_down"))
        e_c.per_row = e_hd.per_row = PAIRS
        eo_done, eT_mm, eg_done, o_done, o_out = sig("eo_done", credit=1), sig("eT_mm"), sig("eg_done"), sig("o_done"), sig("o_out", 16, credit=1)

        up_parts = nc.dram_tensor("up_parts", (PAIRS, P, 2, P), F32, kind="Internal").ap()
        mod_dram = nc.dram_tensor("mod_rows", (rows, 6 * DM), F32, kind="Internal").ap()
        x_dram = A["x"].rearrange("b (t p) d -> b p t d", p=P)
        out_dram = out.rearrange("b (t p) d -> b p t d", p=P)

        def tiles_of(ap, row):
            return ap[bass.ds(row, 1)].rearrange("o p t d -> p (o t) d")

        LOADS = [
            (1, c_cm[:, :], A["c_cm"]), (1, mod_w[:, :], A["mod_w"]),
            (1, in_w[:, :], A["in_w"]), (1, conv_w[:, :, :], A["conv_w"].rearrange("(h p) k -> p h k", p=P)),
            (1, cols[:, :], A["cols"]),
            (1, xproj_w[:, :, :], A["xproj_w"].rearrange("(h p) n -> p h n", p=P)),
            (1, dtproj_w[:, :], A["dtproj_w"]),
            (1, a_neg[:, :, :], A["a_log"].rearrange("(h p) n -> p h n", p=P)),
            (2, bc_w[:, 0, :], A["b_ln"].rearrange("(o n) -> o n", o=1).to_broadcast([P, NS])),
            (2, bc_w[:, 1, :], A["c_ln"].rearrange("(o n) -> o n", o=1).to_broadcast([P, NS])),
            (2, bias_w[:, :], A["bias"].rearrange("(o n) -> o n", o=1).to_broadcast([P, EXPERTS])),
            (2, out_w[:, :, :], A["out_w"].rearrange("(h p) n -> p h n", p=P)),
            (2, gate_w[:, :], A["gate_w"]), (2, up_w[:, :], A["up_w"]),
            (2, down_w[:, :, :], A["down_w"].rearrange("(f p) n -> p f n", p=P)),
            (2, router_w[:, :], A["router_cm"]), (2, shared_up[:, :], A["shared_up"]),
            (2, shared_down[:, :], A["shared_down"]),
        ]
        N_LOADS = [16 * sum(q == k for q, _, _ in LOADS) for k in range(3)]
        N_PREP = 11

        block = ctx.enter_context(nc.Block())

        @block.sync
        def _(sp):
            for q, dst, src in LOADS:
                if q == 1:
                    sp.dma_start(dst, src).then_inc(c_loaded[1].sem, 16)
            def load_raw(k, cut):
                sp.dma_start(raw_up[:, k, :, :], A["up"][bass.ds(cut * SPLIT, SPLIT)].rearrange("i p n -> p i n"))\
                    .then_inc(raw_in[k].sem, 16)

            def store_parts(k, cut):
                sp.wait_ge(lo_done.sem, cut + 1)
                sp.dma_start(up_parts[bass.ds(cut * SPLIT, SPLIT)].rearrange("i p a n -> p i a n"),
                             up_ring[:, k % OUTS * SPLIT:(k % OUTS + 1) * SPLIT, :, :])\
                    .then_inc(split_out[k % OUTS].sem, 16)

            def load(k, source):
                sp.dma_start(up_ring[:, k, :, :], up_parts[bass.ds(source, 1)].rearrange("o p a n -> p (o a) n"))\
                    .then_inc(w_in[k].sem, 16)
                sp.dma_start(down_ring[:, k, :], A["down"][bass.ds(source, 1)].rearrange("o p n -> p (o n)"))\
                    .then_inc(w_in[k].sem, 16)

            for k in range(CUTS):
                load_raw(k, k)
            with sp.Fori(0, TURNS - 1) as turn:
                for k in range(CUTS):
                    store_parts(k, CUTS * turn + k)
                    load_raw(k, CUTS * turn + k + CUTS)
            for k in range(CUTS):
                store_parts(k, CUTS * (TURNS - 1) + k)
            for k in range(OUTS):
                sp.wait_ge(split_out[k].sem, split_out[k].credit + 16 * TURNS * CUTS // OUTS)
            for k in range(RING):
                load(k, k)

            def refill(row, turn, source):
                for k in range(RING):
                    sp.wait_ge(e_down.sem, e_down.by(row, RING * turn + k + 1))
                    load(k, source + k)

            with sp.Fori(0, rows - 1) as row:
                with sp.Fori(0, PAIRS // RING - 1) as turn:
                    refill(row, turn, RING * turn + RING)
                refill(row, PAIRS // RING - 1, 0)
            with sp.Fori(0, PAIRS // RING - 1) as turn:
                refill(rows - 1, turn, RING * turn + RING)

        @block.gpsimd
        def _(pool):
            for q, dst, src in LOADS:
                if q == 2:
                    pool.dma_start(dst, src).then_inc(c_loaded[2].sem, 16)
            nc.gpsimd.memset(ident[:, :], 0.0).then_inc(ident_zero.sem, 1)
            nc.gpsimd.memset(identb[:, :], 0.0).then_inc(ident_zero.sem, 1)
            nc.gpsimd.memset(pair_sel[:, :, :], 0.0).then_inc(ident_zero.sem, 1)
            nc.gpsimd.memset(row_sel[:, :, :], 0.0).then_inc(ident_zero.sem, 1)
            nc.gpsimd.memset(neg_half[:, :], -0.5).then_inc(ident_zero.sem, 1)
            for i, s in enumerate((read_done, scan_done, dbx_done, c_copied, y_done, eo_done, o_out, *split_out)):
                nc.gpsimd.memset(raised[:, i:i + 1], 0.0).then_inc(s.sem, s.credit)
            pool.wait_ge(ident_zero.sem, 5)
            for t in (ident, identb):
                nc.gpsimd.affine_select(out=t[:, :], in_=t[:, :], compare_op=ALU.not_equal, fill=1.0, base=0,
                                        pattern=[[-1, P]], channel_multiplier=1).then_inc(ident_done.sem, 1)
            sel_v = pair_sel[:, :, :].rearrange("p j (e i) -> p j e i", e=2)
            for part in range(3):
                if part:
                    pool.wait_ge(sel_done.sem, 2 * part)
                nc.gpsimd.affine_select(out=sel_v, in_=sel_v, compare_op=ALU.not_equal, fill=1.0, base=-32 * part,
                                        pattern=[[-2, GP], [-1, 2], [0, INTER]], channel_multiplier=1)\
                    .then_inc(sel_done.sem, 1)
                nc.gpsimd.affine_select(out=row_sel[:, :, :], in_=row_sel[:, :, :], compare_op=ALU.not_equal,
                                        fill=1.0, base=-32 * part, pattern=[[-1, 2 * NS], [0, P]],
                                        channel_multiplier=1).then_inc(sel_done.sem, 1)

            def spread(slot):
                return mod[:, slot:slot + 1, :].to_broadcast([P, TILES, DM])

            def root(dst, src, n):
                return nc.gpsimd.tensor_tensor(dst, src, neg_half[:, 0:n], ALU.pow)

            def row_stages(m):
                pool.wait_ge(ln1_var.sem, ln1_var.by(m))
                root(rstd1[:, :], var1[:, :], TILES).then_inc(ln1_rs.sem, 1)
                pool.wait_ge(xn_done.sem, xn_done.by(m))
                pool.wait_ge(mod_in.sem, mod_in.by(m))
                nc.gpsimd.tensor_tensor(hs_tm[:, :, :], xn_tm[:, :, :], spread(SC1), ALU.mult).then_inc(hs_done.sem, 1)
                pool.wait_ge(hs_done.sem, hs_done.by(m))
                nc.gpsimd.tensor_tensor(h_tm[:, :, :], hs_tm[:, :, :], spread(SH1), ALU.add).then_inc(h_done.sem, 1)
                pool.wait_ge(ms1_done.sem, ms1_done.by(m))
                root(r1[:, :], ms1[:, :], TILES).then_inc(r1_done.sem, 1)
                pool.wait_ge(ms3_done.sem, ms3_done.by(m))
                root(r3[:, :, :].rearrange("p t k -> p (t k)"), ms3[:, :, :].rearrange("p t k -> p (t k)"), 3 * TILES)\
                    .then_inc(r3_done.sem, 1)
                for h in range(HALVES):
                    pool.wait_ge(y0_done.sem, y0_done.by(m, h + 1))
                    pool.wait_ge(dt_done.sem, dt_done.by(m, h + 1))
                    nc.gpsimd.tensor_tensor(dtx[h][:, :], dt[h][:, :], x2[h][:, :], ALU.mult).then_inc(dtx_done.sem, 1)
                with pool.Fori(0, TURNS) as turn:
                    for s in range(STATES_PER_TURN):
                        for h in range(HALVES):
                            k = STATES_PER_TURN * HALVES * turn + HALVES * s + h
                            pool.wait_ge(scan_done.sem, scan_done.by(m, k + 1))
                            pool.wait_ge(y_done.sem, y_done.by(m, k - 1))
                            if h == 0:
                                pool.wait_ge(c_copied.sem, c_copied.by(m, STATES_PER_TURN * turn + s + 1))
                            nc.gpsimd.tensor_tensor(read[h][:, :], state[s % 2][h][:, :], c_sb[s % 2][:, :], ALU.mult)\
                                .then_inc(read_done.sem, 1)
                        for h in range(HALVES):
                            k = STATES_PER_TURN * HALVES * turn + HALVES * s + h
                            pool.wait_ge(read_done.sem, read_done.by(m, k + 1))
                            nc.gpsimd.tensor_tensor(y[h][:, :], y[h][:, :], read[h][:, :], ALU.add)\
                                .then_inc(y_done.sem, 1)
                for h in range(HALVES):
                    pool.wait_ge(y_done.sem, y_done.by(m, 2 * NS - 1 + h))
                    nc.gpsimd.tensor_tensor(yz[h][:, :], y[h][:, :], z2[h][:, :], ALU.mult).then_inc(yz_done.sem, 1)
                pool.wait_ge(ms2_done.sem, ms2_done.by(m))
                root(r2[:, :], ms2[:, :], TILES).then_inc(r2_done.sem, 1)
                pool.wait_ge(att_done.sem, att_done.by(m))
                nc.gpsimd.tensor_tensor(gat_tm[:, :, :], att_tm[:, :, :], spread(G1), ALU.mult).then_inc(gat_done.sem, 1)
                pool.wait_ge(gat_done.sem, gat_done.by(m))
                nc.gpsimd.tensor_tensor(x1_tm[:, :, :], gat_tm[:, :, :], x_tm[:, :, :], ALU.add).then_inc(x1_done.sem, 1)
                pool.wait_ge(ln2_var.sem, ln2_var.by(m))
                root(rstd2[:, :], var2[:, :], TILES).then_inc(ln2_rs.sem, 1)
                pool.wait_ge(xn2_done.sem, xn2_done.by(m))
                nc.gpsimd.tensor_tensor(hs2_tm[:, :, :], xn2_tm[:, :, :], spread(SC2), ALU.mult).then_inc(hs2_done.sem, 1)
                pool.wait_ge(hs2_done.sem, hs2_done.by(m))
                nc.gpsimd.tensor_tensor(h2_tm[:, :, :], hs2_tm[:, :, :], spread(SH2), ALU.add).then_inc(h2_done.sem, 1)

            row_stages(0)
            with pool.Fori(0, rows - 1) as row:
                row_stages(row + 1)

        @block.tensor
        def _(pe):
            def transposed(dst, src, width, idn):
                for t in range(TILES):
                    last = nc.tensor.transpose(dst[0:width, t * P:(t + 1) * P], src(t), idn[:, :])
                return last

            def up(row, e, steady):
                shared = e.pair is None
                if steady:
                    pe.wait_ge(e_vd.sem, e_vd.by(row, e.q - 1))
                if not shared:
                    pe.wait_ge(w_in[e.slot].sem, w_in[e.slot].by(row, 32 * (e.lap + 1)))
                for w, h in ((0, 0), (0, 1), (1, 0)):
                    last = nc.tensor.matmul(up_bank[e.two][0:INTER if shared else P, :],
                                            shared_parts[:, w, :] if shared else up_exact[:, e.slot, w, :],
                                            h2_live[h][:, :], start=(w + h == 0), stop=(w == 1))
                last.then_inc(e_up.sem, 1)

            def spread_weights(row, e, steady):
                if e.pair is None:
                    return
                if steady:
                    pe.wait_ge(e_hd.sem, e_hd.by(row, e.q - 1))
                nc.tensor.matmul(comb_bank[e.two][:, :], pair_sel[:, e.pair, :] if isinstance(e.pair, int) else
                                 pair_sel[:, bass.ds(e.pair, 1), :].rearrange("p o n -> p (o n)"),
                                 comb_live[:, e.group, :], start=True, stop=True).then_inc(e_c.sem, 1)

            def down(row, e, first=False, shared=False):
                if shared:
                    pe.wait_ge(e_vd.sem, e_vd.by(row))
                    nc.tensor.matmul(acc_bank[:, :], shared_down[:, :], e_h[0:INTER, e.h_slot, :], start=False,
                                     stop=True).then_inc(e_down.sem, 1)
                else:
                    pe.wait_ge(e_hd.sem, e_hd.by(row, e.q + 1))
                    nc.tensor.matmul(acc_bank[:, :], down_ring[:, e.slot, :], e_h[:, e.h_slot, :], start=first,
                                     stop=False).then_inc(e_down.sem, 1)

            def experts(row, q):
                if q == 0:
                    pe.wait_ge(live_h2.sem, live_h2.by(row))
                    pe.wait_ge(live_lo.sem, live_lo.by(row))
                    pe.wait_ge(live_comb.sem, live_comb.by(row))
                up(row, block_at(q), steady=q >= 2)
                if q == LAG:
                    pe.wait_ge(eo_done.sem, eo_done.by(row, 0))
                if q >= LAG:
                    down(row, block_at(q - LAG), first=q == LAG)
                spread_weights(row, block_at(q), steady=q >= 2)

            def finish_experts(row):
                for back in range(LAG - 1, 0, -1):
                    down(row, block_at(PAIRS - back))
                down(row, block_at(PAIRS), shared=True)

            def turn_out(row):
                pe.wait_ge(eo_done.sem, eo_done.by(row))
                transposed(M[0], lambda t: e_out[:, t * P:(t + 1) * P], P, ident).then_inc(eT_mm.sem, 1)

            def row_stages(m, at, scan_experts):
                for p in ("a1", "a2", "a3", "a4", "a5"):
                    at(p)
                pe.wait_ge(hn_done.sem, hn_done.by(m))
                transposed(M[0], lambda t: hn_tm[:, t, :], P, ident).then_inc(hT_mm.sem, 1)
                at("a6")
                pe.wait_ge(hT_done.sem, hT_done.by(m))
                for h in range(HALVES):
                    nc.tensor.matmul(M[1 + h][:, :], in_w[:, h * P:(h + 1) * P], h_cm[:, :], start=True, stop=True)\
                        .then_inc(in_mm.sem, 1)
                nc.tensor.matmul(M[0][:, :], in_w[:, DI:DI + P], h_cm[:, :], start=True, stop=True)\
                    .then_inc(in_mm.sem, 1)
                at("a7")
                at("a8")
                pe.wait_ge(conv_done.sem, conv_done.by(m, TAPS))
                nc.tensor.matmul(M[1][:, :], in_w[:, DI + P:], h_cm[:, :], start=True, stop=True)\
                    .then_inc(in_mm.sem, 1)
                at("a9")
                pe.wait_ge(x2_done.sem, x2_done.by(m))
                for t in range(TILES):
                    for h in range(HALVES):
                        last = nc.tensor.matmul(M[2][:, t * PROJ:(t + 1) * PROJ], x2[h][:, t * P:(t + 1) * P],
                                                xproj_w[:, h, :], start=(h == 0), stop=(h == HALVES - 1))
                last.then_inc(proj_mm.sem, 1)
                for p in ("a10", "a11", "a12", "a13"):
                    at(p)
                pe.wait_ge(dtn_done.sem, dtn_done.by(m))
                pe.wait_ge(z2_done.sem, z2_done.by(m))
                pe.wait_ge(bcp_done.sem, bcp_done.by(m))
                transposed(Mb[1], lambda t: bc_parts[:, t, :, :].rearrange("p s n -> p (s n)"), 96, identb)\
                    .then_inc(bcT_mm.sem, 1)
                transposed(M[0], lambda t: dtn_tm[:, t, :], RANK, ident).then_inc(dtT_mm.sem, 1)
                at("a14")
                pe.wait_ge(dtT_done.sem, dtT_done.by(m))
                for h in range(HALVES):
                    nc.tensor.matmul(M[2 * (1 - h)][:, :], dtproj_w[:, h * P:(h + 1) * P], dtn_cm[:, :], start=True,
                                     stop=True).then_inc(dt_mm.sem, 1)
                at("a15")
                with pe.Fori(0, TURNS) as turn:
                    pe.wait_ge(bcT_done.sem, bcT_done.by(m))
                    pe.wait_ge(dt_done.sem, dt_done.by(m))
                    for s in range(STATES_PER_TURN):
                        n = STATES_PER_TURN * turn + s
                        pe.wait_ge(dbx_done.sem, dbx_done.by(m, HALVES * n))
                        nc.tensor.matmul(b_bank[:, :], row_sel[:, bass.ds(n, 1), :].rearrange("p o n -> p (o n)"),
                                         bc_cm[:, :], start=True, stop=True).then_inc(b_mm.sem, 1)
                        pe.wait_ge(c_copied.sem, c_copied.by(m, n))
                        nc.tensor.matmul(c_bank[:, :], row_sel[:, bass.ds(n + NS, 1), :].rearrange("p o n -> p (o n)"),
                                         bc_cm[:, :], start=True, stop=True).then_inc(cn_mm.sem, 1)
                        for k in range(TURN_SHARE[s], TURN_SHARE[s + 1]):
                            scan_experts(turn, k)
                at("c1")
                at("c2")
                pe.wait_ge(yz_done.sem, yz_done.by(m))
                for t in range(TILES):
                    for h in range(HALVES):
                        last = nc.tensor.matmul(M[0][:, t * P:(t + 1) * P], yz[h][:, t * P:(t + 1) * P], out_w[:, h, :],
                                                start=(h == 0), stop=(h == HALVES - 1))
                last.then_inc(outp_mm.sem, 1)
                for p in ("c3", "c4", "c5", "c6"):
                    at(p)
                pe.wait_ge(hn2_done.sem, hn2_done.by(m))
                transposed(M[1], lambda t: hn_tm[:, t, :], P, ident).then_inc(hT2_mm.sem, 1)
                at("c7")
                pe.wait_ge(hT2_done.sem, hT2_done.by(m))
                for f in range(FB):
                    g, u = FFN_BANKS[f]
                    if f:
                        pe.wait_ge(fv_done.sem, fv_done.by(m, f))
                    if f >= 2:
                        pe.wait_ge(fa_done.sem, fa_done.by(m, f - 1))
                    nc.tensor.matmul(M[g][:, :], gate_w[:, f * P:(f + 1) * P], h_cm[:, :], start=True, stop=True)\
                        .then_inc(fg_mm.sem, 1)
                    nc.tensor.matmul(M[u][:, :], up_w[:, f * P:(f + 1) * P], h_cm[:, :], start=True, stop=True)\
                        .then_inc(fu_mm.sem, 1)
                    at(f"c{8 + f}")
                at("c12")
                pe.wait_ge(fa_done.sem, fa_done.by(m))
                for t in range(TILES):
                    for f in range(FB):
                        last = nc.tensor.matmul(M[1][:, t * P:(t + 1) * P], f_act[f][:, t * P:(t + 1) * P],
                                                down_w[:, f, :], start=(f == 0), stop=(f == FB - 1))
                last.then_inc(down_mm.sem, 1)
                for p in ("c13", "c14", "c15", "c16", "c17", "c18"):
                    at(p)
                pe.wait_ge(h2_done.sem, h2_done.by(m))
                transposed(M[0], lambda t: h2_tm[:, t, :], P, ident).then_inc(h2T_mm.sem, 1)
                at("c19")
                pe.wait_ge(h2T_done.sem, h2T_done.by(m))
                for t in range(TILES):
                    last = nc.tensor.matmul(M[1 + t // 3][:, t % 3 * EXPERTS:(t % 3 + 1) * EXPERTS],
                                            h2_cm[:, t * P:(t + 1) * P], router_w[:, :], start=True, stop=True)
                last.then_inc(rt_mm.sem, 1)
                for p in ("c20", "c21", "c22", "c23", "c24", "c25", "c26"):
                    at(p)
                pe.wait_ge(combp_done.sem, combp_done.by(m))
                for g in range(GROUPS):
                    half = g % 2 * SEQ
                    last = transposed(Mb[g // 2][:, half:half + SEQ],
                                      lambda t: comb_parts[:, t, g, :, :].rearrange("p s e -> p (s e)"), 96, identb)
                last.then_inc(combT_mm.sem, 1)

            pe.wait_ge(ident_done.sem, 2)
            pe.wait_ge(sel_done.sem, 6)
            pe.wait_ge(c_silu.sem, 1)
            nc.tensor.matmul(M[0][0:rows, :], c_sl[:, :], mod_w[:, 0:512], start=True, stop=True)
            nc.tensor.matmul(M[1][0:rows, 0:256], c_sl[:, :], mod_w[:, 512:768], start=True, stop=True)\
                .then_inc(mod_mm.sem, 1)
            pe.wait_ge(prep.sem, N_PREP)
            pe.wait_ge(shared_split.sem, 2)
            pe.wait_ge(c_loaded[2].sem, N_LOADS[2])
            row_stages(0, lambda p: None, lambda turn, k: None)
            with pe.Fori(0, rows - 1) as row:
                def in_scan(turn, k):
                    e = block_in_turn(turn, k)
                    up(row, e, True)
                    down(row, e.before(LAG))
                    spread_weights(row, e, True)
                row_stages(row + 1, lambda p: experts(row, POINTS[p]), in_scan)
                finish_experts(row)
                pe.wait_ge(live_comb.sem, live_comb.by(row + 1))
                turn_out(row)
            for q in range(RING):
                experts(rows - 1, q)
            with pe.Fori(1, PAIRS // RING) as lap:
                for k in range(RING):
                    e = block_in_lap(lap, k)
                    up(rows - 1, e, True)
                    down(rows - 1, e.before(LAG))
                    spread_weights(rows - 1, e, True)
            experts(rows - 1, PAIRS)
            finish_experts(rows - 1)
            turn_out(rows - 1)

        @block.scalar
        def _(act):
            for q, dst, src in LOADS:
                if q == 0:
                    act.dma_start(dst, src).then_inc(c_loaded[0].sem, 16)

            def load_row(m):
                act.dma_start(x_tm[:, :, :], tiles_of(x_dram, m)).then_inc(x_in.sem, 16)
                act.dma_start(mod[:, :, :].rearrange("p s d -> p (s d)"),
                              mod_dram[bass.ds(m, 1), :].to_broadcast([P, 6 * DM])).then_inc(mod_in.sem, 16)

            def experts(row, e):
                act.wait_ge(e_up.sem, e_up.by(row, e.q + 1))
                n = INTER if e.pair is None else P
                nc.scalar.activation(e_th[e.two][0:n, :], up_bank[e.two][0:n, :], ACT.Tanh, scale=0.5)\
                    .then_inc(e_tanh.sem, 1)

            def square_sums(src, dst, done):
                for t in range(TILES):
                    nc.scalar.activation(junk[:, t, :], src[:, t, :], ACT.Square, accum_out=dst[:, t:t + 1])\
                        .then_inc(done.sem, 1)

            def row_stages(m, at, scan_experts):
                for p in ("a1", "a2"):
                    at(p)
                act.wait_ge(h_done.sem, h_done.by(m))
                square_sums(h_tm, ss1, ss1_done)
                for p in ("a3", "a4", "a5"):
                    at(p)
                act.wait_ge(hT_mm.sem, hT_mm.by(m))
                nc.scalar.activation(h_cm[:, :], M[0][:, :], ACT.Copy).then_inc(hT_done.sem, 1)
                at("a6")
                at("a7")
                for h in range(HALVES):
                    act.wait_ge(conv_done.sem, conv_done.by(m, TAPS * (h + 1)))
                    nc.scalar.activation(conv_th[h][:, :], conv[h][:, :], ACT.Tanh, scale=0.5)\
                        .then_inc(convth_done.sem, 1)
                act.wait_ge(in_mm.sem, in_mm.by(m, 3))
                nc.scalar.activation(z_th[0][:, :], M[0][:, :], ACT.Tanh, scale=0.5).then_inc(zth_done.sem, 1)
                at("a8")
                at("a9")
                act.wait_ge(in_mm.sem, in_mm.by(m, 4))
                nc.scalar.activation(z_th[1][:, :], M[1][:, :], ACT.Tanh, scale=0.5).then_inc(zth_done.sem, 1)
                at("a10")
                act.wait_ge(proj_mm.sem, proj_mm.by(m))
                nc.scalar.activation(proj_sq[:, :, :].rearrange("p t n -> p (t n)"), M[2][:, 0:TILES * PROJ], ACT.Square)\
                    .then_inc(sq3_done.sem, 1)
                for p in ("a11", "a12", "a13"):
                    at(p)
                act.wait_ge(dtT_mm.sem, dtT_mm.by(m))
                nc.scalar.activation(dtn_cm[:, :], M[0][0:RANK, :], ACT.Copy).then_inc(dtT_done.sem, 1)
                act.wait_ge(bcT_mm.sem, bcT_mm.by(m))
                nc.scalar.activation(bc_cm[:, :], Mb[1][0:96, 0:SEQ], ACT.Copy).then_inc(bcT_done.sem, 1)
                at("a14")
                for h in range(HALVES):
                    act.wait_ge(dtmin_done.sem, dtmin_done.by(m, h + 1))
                    nc.scalar.activation(dt_exp[h][:, :], dt_min[h][:, :], ACT.Exp).then_inc(dtexp_done.sem, 1)
                for h in range(HALVES):
                    act.wait_ge(dtexp_done.sem, dtexp_done.by(m, h + 1))
                    nc.scalar.activation(dt_ln[h][:, :], dt_exp[h][:, :], ACT.Ln, bias=1.0).then_inc(dtln_done.sem, 1)
                for h in range(HALVES):
                    act.wait_ge(x2_done.sem, x2_done.by(m))
                    nc.scalar.activation(y[h][:, :], x2[h][:, :], ACT.Copy, scale=cols[:, D_HALF + h:D_HALF + h + 1])\
                        .then_inc(y0_done.sem, 1)
                at("a15")
                act.wait_ge(dt_done.sem, dt_done.by(m))
                with act.Fori(0, TURNS) as turn:
                    for s in range(STATES_PER_TURN):
                        n = STATES_PER_TURN * turn + s
                        k = HALVES * n
                        act.wait_ge(cn_mm.sem, cn_mm.by(m, n + 1))
                        act.wait_ge(read_done.sem, read_done.by(m, k - HALVES))
                        nc.scalar.activation(c_sb[s % 2][:, :], c_bank[:, :], ACT.Copy).then_inc(c_copied.sem, 1)
                        cut = TURN_SHARE[s], TURN_SHARE[s] + 1, TURN_SHARE[s + 1]
                        for h in range(HALVES):
                            act.wait_ge(scan_done.sem, scan_done.by(m, k + h))
                            nc.scalar.activation(da_bank[:, :], dt[h][:, :], ACT.Exp,
                                                 scale=a_neg[:, h, bass.ds(n, 1)]).then_inc(da_done.sem, 1)
                            for b in range(cut[h], cut[h + 1]):
                                scan_experts(turn, b)
                for p in ("c1", "c2", "c3"):
                    at(p)
                act.wait_ge(hid_done.sem, hid_done.by(m))
                square_sums(hid_tm, ss2, ss2_done)
                for p in ("c4", "c5", "c6"):
                    at(p)
                act.wait_ge(hT2_mm.sem, hT2_mm.by(m))
                nc.scalar.activation(h_cm[:, :], M[1][:, :], ACT.Copy).then_inc(hT2_done.sem, 1)
                at("c7")
                for f in range(FB):
                    act.wait_ge(fg_mm.sem, fg_mm.by(m, f + 1))
                    nc.scalar.activation(f_th[f % 2][:, :], M[FFN_BANKS[f][0]][:, :], ACT.Tanh, scale=0.5)\
                        .then_inc(fth_done.sem, 1)
                    at(f"c{8 + f}")
                for p in ("c12", "c13", "c14", "c15", "c16", "c17", "c18"):
                    at(p)
                act.wait_ge(h2T_mm.sem, h2T_mm.by(m))
                nc.scalar.activation(h2_cm[:, :], M[0][:, :], ACT.Copy).then_inc(h2T_done.sem, 1)
                at("c19")
                at("c20")
                act.wait_ge(lg_done.sem, lg_done.by(m))
                nc.scalar.activation(l_exp[:, :, :], logits[:, :, :], ACT.Exp, scale=-1.0).then_inc(lexp_done.sem, 1)
                for p in ("c21", "c22", "c23", "c24", "c25", "c26"):
                    at(p)

            def take_live(m):
                act.wait_ge(h2T_done.sem, h2T_done.by(m))
                nc.scalar.activation(h2_live[0][:, :], h2_cm[:, :], ACT.Copy).then_inc(live_h2.sem, 1)

            def take_sum(row):
                act.wait_ge(e_down.sem, e_down.by(row))
                nc.scalar.activation(e_out[:, :], acc_bank[:, :], ACT.Copy).then_inc(eo_done.sem, 1)

            def store(row):
                act.wait_ge(o_done.sem, o_done.by(row))
                act.dma_start(tiles_of(out_dram, row), o_tm[:, :, :]).then_inc(o_out.sem, 16)

            act.wait_ge(c_loaded[1].sem, N_LOADS[1])
            act.wait_ge(c_loaded[2].sem, N_LOADS[2])
            nc.scalar.activation(c_th[:, :], c_cm[:, :], ACT.Tanh, scale=0.5).then_inc(c_tanh.sem, 1)
            nc.scalar.activation(a_neg[:, :, :], a_neg[:, :, :], ACT.Exp).then_inc(a_exp.sem, 1)
            act.wait_ge(mod_done.sem, mod_done.by(0, 3))
            act.dma_start(mod_dram, mod_all[:, :, :].rearrange("b s d -> b (s d)")).then_inc(mod_out.sem, 16)
            act.wait_ge(mod_out.sem, 16)
            load_row(0)
            nc.scalar.activation(shared_parts[:, 0, :], shared_up[:, :], ACT.Copy).then_inc(shared_split.sem, 1)

            def cut_hi(turn, k):
                out = split_out[k % OUTS]
                act.wait_ge(raw_in[k].sem, 16 * (turn + 1))
                act.wait_ge(out.sem, out.credit + 16 * (CUTS // OUTS * turn + k // OUTS))
                nc.scalar.activation(up_exact[:, k % OUTS * SPLIT:(k % OUTS + 1) * SPLIT, 0, :], raw_up[:, k, :, :],
                                     ACT.Copy).then_inc(hi_done.sem, 1)

            row_stages(0, lambda p: None, cut_hi)
            take_live(0)
            with act.Fori(0, rows - 1) as row:
                act.wait_ge(live_x1.sem, live_x1.by(row))
                load_row(row + 1)
                row_stages(row + 1, lambda p: experts(row, block_at(POINTS[p])),
                           lambda turn, k: experts(row, block_in_turn(turn, k)))
                act.wait_ge(e_up.sem, e_up.by(row))
                take_live(row + 1)
                take_sum(row)
                store(row)
            for k in range(RING):
                experts(rows - 1, block_at(k))
            with act.Fori(1, PAIRS // RING) as lap:
                for k in range(RING):
                    experts(rows - 1, block_in_lap(lap, k))
            experts(rows - 1, block_at(PAIRS))
            take_sum(rows - 1)
            store(rows - 1)
            act.wait_ge(o_out.sem, o_out.by(rows - 1))

        @block.vector
        def _(dve):
            def experts(row, e):
                n = INTER if e.pair is None else P
                if not (isinstance(e.q, int) and e.q < HRING):
                    dve.wait_ge(e_down.sem, e_down.by(row, e.q - HRING + 1))
                dve.wait_ge(e_tanh.sem, e_tanh.by(row, e.q + 1))
                nc.vector.scalar_tensor_tensor(out=e_h[0:n, e.h_slot, :], in0=e_th[e.two][0:n, :], scalar=1.0,
                                               in1=up_bank[e.two][0:n, :], op0=ALU.add, op1=ALU.mult)\
                    .then_inc(e_vd.sem, 1)
                if not (isinstance(e.q, int) and e.q == 0):
                    w = e.before(1)
                    dve.wait_ge(e_vd.sem, e_vd.by(row, w.q + 1))
                    dve.wait_ge(e_c.sem, e_c.by(row, w.q + 1))
                    nc.vector.tensor_tensor(e_h[:, w.h_slot, :], e_h[:, w.h_slot, :], comb_bank[w.two][:, :],
                                            ALU.mult).then_inc(e_hd.sem, 1)

            def count_of(done, m):
                return done.by(m) if isinstance(m, int) else dve.snap(dve.to_reg(done.by(m)))

            def wait_apart(done, count):
                dve.wait_ge(prep.sem, N_PREP)
                dve.wait_ge(done.sem, count)

            def norm_stats(m, count, src, st, st_done, agg, agg_done, var, var_done):
                for t in range(TILES):
                    nc.vector.bn_stats(st[:, t, :], src[:, t, :]).then_inc(st_done.sem, 1)
                wait_apart(st_done, count)
                for t in range(TILES):
                    nc.vector.bn_aggr(agg[:, t, :], st[:, t, :]).then_inc(agg_done.sem, 1)
                dve.wait_ge(agg_done.sem, agg_done.by(m))
                nc.vector.tensor_scalar(var[:, :], agg[:, :, 1], EPS_LN, None, ALU.add).then_inc(var_done.sem, 1)

            def centred(dst, src, agg, rs, done):
                for t in range(TILES):
                    nc.vector.tensor_scalar(dst[:, t, :], src[:, t, :], agg[:, t, 0:1], rs[:, t:t + 1],
                                            ALU.subtract, ALU.mult).then_inc(done.sem, 1)

            def scaled(dst, src, r, done):
                for t in range(TILES):
                    nc.vector.tensor_scalar(dst[:, t, :], src[:, t, :], r[:, t:t + 1], None, ALU.mult)\
                        .then_inc(done.sem, 1)

            def gated(th, src, dst, done):
                nc.vector.scalar_tensor_tensor(out=dst, in0=th, scalar=1.0, in1=src, op0=ALU.add, op1=ALU.mult)\
                    .then_inc(done.sem, 1)

            def convolve(m, h):
                src = M[1 + h]
                dve.wait_ge(in_mm.sem, in_mm.by(m, h + 1))
                nc.vector.tensor_scalar(conv[h][:, :], src[:, :], conv_w[:, h, TAPS - 1:TAPS],
                                        cols[:, CONV_B + h:CONV_B + h + 1], ALU.mult, ALU.add)\
                    .then_inc(conv_done.sem, 1)
                for back in range(1, TAPS):
                    dve.wait_ge(conv_done.sem, conv_done.by(m, TAPS * h + back))
                    nc.vector.scalar_tensor_tensor(out=conv[h][:, back:], in0=src[:, 0:SEQ - back],
                                                   scalar=conv_w[:, h, TAPS - 1 - back:TAPS - back],
                                                   in1=conv[h][:, back:], op0=ALU.mult, op1=ALU.add)\
                        .then_inc(conv_done.sem, 1)

            def thirds(m, src, rem, parts, done):
                nc.vector.tensor_copy(parts(0), src).then_inc(done.sem, 1)
                dve.wait_ge(done.sem, done.by(m, 1))
                nc.vector.tensor_tensor(rem, src, parts(0), ALU.subtract).then_inc(done.sem, 1)
                dve.wait_ge(done.sem, done.by(m, 2))
                nc.vector.tensor_copy(parts(1), rem).then_inc(done.sem, 1)
                dve.wait_ge(done.sem, done.by(m, 3))
                nc.vector.tensor_tensor(parts(2), rem, parts(1), ALU.subtract).then_inc(done.sem, 1)

            def row_stages(m, at, scan_experts):
                counts = {d: count_of(d, m) for d in (ln1_st, ln2_st, probs_done, top_done)}
                dve.wait_ge(x_in.sem, x_in.by(m))
                norm_stats(m, counts[ln1_st], x_tm, stats, ln1_st, mv, ln1_mv, var1, ln1_var)
                at("a1")
                dve.wait_ge(ln1_rs.sem, ln1_rs.by(m))
                centred(xn_tm, x_tm, mv, rstd1, xn_done)
                at("a2")
                at("a3")
                dve.wait_ge(ss1_done.sem, ss1_done.by(m))
                nc.vector.tensor_scalar(ms1[:, :], ss1[:, :], 1.0 / DM, EPS_RMS, ALU.mult, ALU.add)\
                    .then_inc(ms1_done.sem, 1)
                at("a4")
                dve.wait_ge(r1_done.sem, r1_done.by(m))
                scaled(hn_tm, h_tm, r1, hn_done)
                at("a5")
                at("a6")
                convolve(m, 0)
                at("a7")
                convolve(m, 1)
                at("a8")
                for h in range(HALVES):
                    dve.wait_ge(convth_done.sem, convth_done.by(m, h + 1))
                    gated(conv_th[h][:, :], conv[h][:, :], x2[h][:, :], x2_done)
                dve.wait_ge(zth_done.sem, zth_done.by(m, 1))
                gated(z_th[0][:, :], M[0][:, :], z2[0][:, :], z2_done)
                at("a9")
                dve.wait_ge(zth_done.sem, zth_done.by(m, 2))
                gated(z_th[1][:, :], M[1][:, :], z2[1][:, :], z2_done)
                at("a10")
                at("a11")
                dve.wait_ge(sq3_done.sem, sq3_done.by(m))
                nc.vector.tensor_reduce(ss3[:, :, 0], proj_sq[:, :, 0:RANK], AX_X, ALU.add).then_inc(ss3_done.sem, 1)
                nc.vector.tensor_reduce(ss3[:, :, 1:3], proj_sq[:, :, RANK:].rearrange("p t (k n) -> p t k n", k=2),
                                        AX_X, ALU.add).then_inc(ss3_done.sem, 1)
                dve.wait_ge(ss3_done.sem, ss3_done.by(m))
                nc.vector.tensor_scalar(ms3[:, :, 0], ss3[:, :, 0], 1.0 / RANK, EPS_RMS, ALU.mult, ALU.add)\
                    .then_inc(ms3_done.sem, 1)
                nc.vector.tensor_scalar(ms3[:, :, 1:3], ss3[:, :, 1:3], 1.0 / NS, EPS_RMS, ALU.mult, ALU.add)\
                    .then_inc(ms3_done.sem, 1)
                at("a12")
                at("a13")
                dve.wait_ge(r3_done.sem, r3_done.by(m))
                proj = M[2][:, 0:TILES * PROJ].rearrange("p (t n) -> p t n", t=TILES)
                nc.vector.tensor_tensor(dtn_tm[:, :, :], proj[:, :, 0:RANK],
                                        r3[:, :, 0:1].to_broadcast([P, TILES, RANK]), ALU.mult).then_inc(dtn_done.sem, 1)
                nc.vector.tensor_tensor(bcn[:, :, :].rearrange("p t (k n) -> p t k n", k=2),
                                        proj[:, :, RANK:].rearrange("p t (k n) -> p t k n", k=2),
                                        r3[:, :, 1:3].rearrange("p t (k o) -> p t k o", o=1)
                                        .to_broadcast([P, TILES, 2, NS]), ALU.mult).then_inc(bcn_done.sem, 1)
                dve.wait_ge(bcn_done.sem, bcn_done.by(m))
                nc.vector.tensor_tensor(bcs[:, :, :], bcn[:, :, :],
                                        bc_w[:, :, :].rearrange("p (o k) n -> p o (k n)", o=1)
                                        .to_broadcast([P, TILES, 2 * NS]), ALU.mult).then_inc(bcs_done.sem, 1)
                dve.wait_ge(bcs_done.sem, bcs_done.by(m))
                thirds(m, bcs[:, :, :], bc_rem[:, :, :], lambda i: bc_parts[:, :, i, :], bcp_done)
                at("a14")
                for h in range(HALVES):
                    dve.wait_ge(dt_mm.sem, dt_mm.by(m, h + 1))
                    nc.vector.tensor_scalar(dt_min[h][:, :], M[2 * (1 - h)][:, :], cols[:, DT_B + h:DT_B + h + 1], 30.0,
                                            ALU.add, ALU.min).then_inc(dtmin_done.sem, 1)
                at("a15")
                for h in range(HALVES):
                    dve.wait_ge(dtln_done.sem, dtln_done.by(m, h + 1))
                    nc.vector.scalar_tensor_tensor(out=dt[h][:, :], in0=M[2 * (1 - h)][:, :],
                                                   scalar=cols[:, DT_B + h:DT_B + h + 1], in1=dt_ln[h][:, :],
                                                   op0=ALU.add, op1=ALU.max).then_inc(dt_done.sem, 1)
                with dve.Fori(0, TURNS) as turn:
                    dve.wait_ge(dtx_done.sem, dtx_done.by(m))
                    for s in range(STATES_PER_TURN):
                        n = STATES_PER_TURN * turn + s
                        cut = TURN_SHARE[s], TURN_SHARE[s] + 1, TURN_SHARE[s + 1]
                        dve.wait_ge(b_mm.sem, b_mm.by(m, n + 1))
                        dve.wait_ge(scan_done.sem, scan_done.by(m, HALVES * n))
                        for h in range(HALVES):
                            nc.vector.tensor_tensor(dbx[h][:, :], dtx[h][:, :], b_bank[:, :], ALU.mult)\
                                .then_inc(dbx_done.sem, 1)
                        for h in range(HALVES):
                            k = HALVES * n + h
                            dve.wait_ge(dbx_done.sem, dbx_done.by(m, k + 1))
                            dve.wait_ge(da_done.sem, da_done.by(m, k + 1))
                            dve.wait_ge(read_done.sem, read_done.by(m, k - 3))
                            nc.vector.tensor_tensor_scan(state[s % 2][h][:, :], da_bank[:, :], dbx[h][:, :], 0.0,
                                                         ALU.mult, ALU.add).then_inc(scan_done.sem, 1)
                            for b in range(cut[h], cut[h + 1]):
                                scan_experts(turn, b)
                for p in ("c1", "c2", "c3"):
                    at(p)
                dve.wait_ge(outp_mm.sem, outp_mm.by(m))
                nc.vector.tensor_tensor(hid_tm[:, :, :], M[0][:, :].rearrange("p (t d) -> p t d", t=TILES),
                                        h_tm[:, :, :], ALU.add).then_inc(hid_done.sem, 1)
                at("c4")
                dve.wait_ge(ss2_done.sem, ss2_done.by(m))
                nc.vector.tensor_scalar(ms2[:, :], ss2[:, :], 1.0 / DM, EPS_RMS, ALU.mult, ALU.add)\
                    .then_inc(ms2_done.sem, 1)
                at("c5")
                dve.wait_ge(r2_done.sem, r2_done.by(m))
                scaled(hn_tm, hid_tm, r2, hn2_done)
                at("c6")
                at("c7")
                for f in range(FB):
                    g, u = FFN_BANKS[f]
                    dve.wait_ge(fth_done.sem, fth_done.by(m, f + 1))
                    gated(f_th[f % 2][:, :], M[g][:, :], f_v[f % 2][:, :], fv_done)
                    dve.wait_ge(fv_done.sem, fv_done.by(m, f + 1))
                    dve.wait_ge(fu_mm.sem, fu_mm.by(m, f + 1))
                    nc.vector.tensor_tensor(f_act[f][:, :], f_v[f % 2][:, :], M[u][:, :], ALU.mult)\
                        .then_inc(fa_done.sem, 1)
                    at(f"c{8 + f}")
                at("c12")
                at("c13")
                dve.wait_ge(down_mm.sem, down_mm.by(m))
                nc.vector.tensor_tensor(att_tm[:, :, :], M[1][:, :].rearrange("p (t d) -> p t d", t=TILES),
                                        hid_tm[:, :, :], ALU.add).then_inc(att_done.sem, 1)
                at("c14")
                at("c15")
                dve.wait_ge(x1_done.sem, x1_done.by(m))
                norm_stats(m, counts[ln2_st], x1_tm, stats2, ln2_st, mv2, ln2_mv, var2, ln2_var)
                at("c16")
                dve.wait_ge(ln2_rs.sem, ln2_rs.by(m))
                centred(xn2_tm, x1_tm, mv2, rstd2, xn2_done)
                for p in ("c17", "c18", "c19", "c20"):
                    at(p)
                dve.wait_ge(rt_mm.sem, rt_mm.by(m))
                nc.vector.tensor_tensor(logits[:, 0:3, :], M[1][:, 0:3 * EXPERTS].rearrange("p (t e) -> p t e", t=3),
                                        bias_w[:, :].rearrange("p (o e) -> p o e", o=1)
                                        .to_broadcast([P, 3, EXPERTS]), ALU.add).then_inc(lg_done.sem, 1)
                nc.vector.tensor_tensor(logits[:, 3, :], M[2][:, 0:EXPERTS], bias_w[:, :], ALU.add)\
                    .then_inc(lg_done.sem, 1)
                at("c21")
                dve.wait_ge(lexp_done.sem, lexp_done.by(m))
                nc.vector.tensor_scalar(l_one[:, :, :], l_exp[:, :, :], 1.0, None, ALU.add).then_inc(lone_done.sem, 1)
                dve.wait_ge(lone_done.sem, lone_done.by(m))

                for t in range(TILES):
                    nc.vector.reciprocal(probs[:, t, :], l_one[:, t, :]).then_inc(probs_done.sem, 1)
                at("c22")
                wait_apart(probs_done, counts[probs_done])
                for t in range(TILES):
                    nc.vector.max(top[:, t, :], probs[:, t, :]).then_inc(top_done.sem, 1)
                at("c23")
                wait_apart(top_done, counts[top_done])
                for t in range(TILES):
                    nc.vector.match_replace(rest[:, t, :], in_to_replace=top[:, t, :], in_values=probs[:, t, :],
                                            imm_value=-1.0).then_inc(rest_done.sem, 1)
                at("c24")
                dve.wait_ge(rest_done.sem, rest_done.by(m))
                for t in range(TILES):
                    nc.vector.scalar_tensor_tensor(out=chosen[:, t, :], in0=rest[:, t, :], scalar=0.0,
                                                   in1=probs[:, t, :], op0=ALU.max, op1=ALU.subtract)\
                        .then_inc(chosen_done.sem, 1)
                at("c25")
                nc.vector.tensor_reduce(top_sum[:, :], top[:, :, :], AX_X, ALU.add).then_inc(tops_done.sem, 1)
                dve.wait_ge(tops_done.sem, tops_done.by(m, 1))
                nc.vector.tensor_scalar(top_inv[:, :], top_sum[:, :], 1e-9, None, ALU.add).then_inc(tops_done.sem, 1)
                dve.wait_ge(tops_done.sem, tops_done.by(m, 2))
                nc.vector.reciprocal(top_fac[:, :], top_inv[:, :]).then_inc(tops_done.sem, 1)
                dve.wait_ge(tops_done.sem, tops_done.by(m, 3))
                dve.wait_ge(chosen_done.sem, chosen_done.by(m))
                for t in range(TILES):
                    nc.vector.tensor_scalar(comb[:, t, :], chosen[:, t, :], top_fac[:, t:t + 1], -SCALE / 2,
                                            ALU.mult, ALU.mult).then_inc(comb_done.sem, 1)
                dve.wait_ge(comb_done.sem, comb_done.by(m))
                as_groups = "p t (g e) -> p t g e"
                thirds(m, comb[:, :, :].rearrange(as_groups, g=GROUPS), comb_rem[:, :, :].rearrange(as_groups, g=GROUPS),
                       lambda i: comb_parts[:, :, :, i, :], combp_done)
                at("c26")

            def take_live(m):
                dve.wait_ge(live_h2.sem, live_h2.by(m))
                nc.vector.tensor_tensor(h2_live[1][:, :], h2_cm[:, :], h2_live[0][:, :].bitcast(F32), ALU.subtract)\
                    .then_inc(live_lo.sem, 1)
                dve.wait_ge(combT_mm.sem, combT_mm.by(m))
                for b in range(3):
                    g = min(2, GROUPS - 2 * b)
                    nc.vector.tensor_copy(comb_live[:, 2 * b:2 * b + g, :],
                                          Mb[b][0:96, 0:g * SEQ].rearrange("p (g t) -> p g t", g=g))\
                        .then_inc(live_comb.sem, 1)

            def take_residual(m):
                nc.vector.tensor_copy(x1_live[:, :, :], x1_tm[:, :, :]).then_inc(live_x1.sem, 1)
                nc.vector.tensor_copy(g2_live[:, :], mod[:, G2, :]).then_inc(live_x1.sem, 1)

            def finish_row(row, first):
                dve.wait_ge(eT_mm.sem, eT_mm.by(row))
                nc.vector.tensor_tensor(e_gat[:, :, :], M[0][:, :].rearrange("p (t d) -> p t d", t=TILES),
                                        g2_live[:, :].rearrange("p (o d) -> p o d", o=1)
                                        .to_broadcast([P, TILES, DM]), ALU.mult).then_inc(eg_done.sem, 1)
                dve.wait_ge(eg_done.sem, eg_done.by(row))
                dve.wait_ge(o_out.sem, o_out.by(row, 0))
                nc.vector.tensor_tensor(o_tm[:, :, :], e_gat[:, :, :], x1_live[:, :, :], ALU.add)\
                    .then_inc(o_done.sem, 1)

            dve.wait_ge(c_tanh.sem, 1)
            gated(c_th[:, :], c_cm[:, :], c_sl[:, :], c_silu)
            dve.wait_ge(mod_mm.sem, 1)
            flat = mod_all[:, :, :].rearrange("b s d -> b (s d)")
            nc.vector.tensor_scalar(flat[:, 0:512], M[0][0:rows, :], 0.5, None, ALU.mult).then_inc(mod_half.sem, 1)
            nc.vector.tensor_scalar(flat[:, 512:768], M[1][0:rows, 0:256], 0.5, None, ALU.mult).then_inc(mod_half.sem, 1)
            dve.wait_ge(mod_half.sem, 2)
            nc.vector.tensor_scalar(mod_all[:, SC1::3, :], mod_all[:, SC1::3, :], 1.0, None, ALU.add)\
                .then_inc(mod_done.sem, 1)
            for i, slot in enumerate((G1, G2)):
                nc.vector.scalar_tensor_tensor(out=mod_abs[:, i, :], in0=mod_all[:, slot, :], scalar=-1.0,
                                               in1=mod_all[:, slot, :], op0=ALU.mult, op1=ALU.max)\
                    .then_inc(mod_raw.sem, 1)
            nc.vector.tensor_scalar(mod_sgn[:, :, :], mod_all[:, G1::3, :], 0.0, 2.0, ALU.is_ge, ALU.mult)\
                .then_inc(mod_raw.sem, 1)
            dve.wait_ge(mod_raw.sem, 3)
            nc.vector.tensor_scalar(mod_abs[:, :, :], mod_abs[:, :, :], 0.25, None, ALU.max).then_inc(mod_raw.sem, 1)
            dve.wait_ge(mod_raw.sem, 4)
            for i, slot in enumerate((G1, G2)):
                nc.vector.scalar_tensor_tensor(out=mod_all[:, slot, :], in0=mod_sgn[:, i, :], scalar=-1.0,
                                               in1=mod_abs[:, i, :], op0=ALU.add, op1=ALU.mult)\
                    .then_inc(mod_done.sem, 1)
            dve.wait_ge(c_loaded[1].sem, N_LOADS[1])
            dve.wait_ge(c_loaded[2].sem, N_LOADS[2])
            dve.wait_ge(a_exp.sem, 1)
            for t, scale in ((in_w[:, :], cols[:, IN_LN:IN_LN + 1]), (gate_w[:, :], cols[:, PRE_LN:PRE_LN + 1]),
                             (up_w[:, :], cols[:, PRE_LN:PRE_LN + 1]),
                             (dtproj_w[:, :], cols[0:RANK, DT_LN:DT_LN + 1]), (xproj_w[:, :, :], 0.5),
                             (out_w[:, :, :], 0.5), (down_w[:, :, :], 0.5), (shared_down[:, :], 0.5),
                             (bc_w[:, 0, :], 0.5), (cols[:, D_HALF:D_HALF + 2], 0.5), (a_neg[:, :, :], -1.0)):
                nc.vector.tensor_scalar(t, t, scale, None, ALU.mult).then_inc(prep.sem, 1)
            dve.wait_ge(prep.sem, N_PREP)
            dve.wait_ge(shared_split.sem, 1)
            nc.vector.tensor_tensor(shared_parts[:, 1, :], shared_up[:, :], shared_parts[:, 0, :].bitcast(F32), ALU.subtract)\
                .then_inc(shared_split.sem, 1)

            def cut_lo(turn, k):
                dve.wait_ge(hi_done.sem, CUTS * turn + k + 1)
                at = slice(k % OUTS * SPLIT, (k % OUTS + 1) * SPLIT)
                nc.vector.tensor_tensor(up_exact[:, at, 1, :], raw_up[:, k, :, :], up_ring[:, at, 0, :], ALU.subtract)\
                    .then_inc(lo_done.sem, 1)

            row_stages(0, lambda p: None, cut_lo)
            take_live(0)
            take_residual(0)
            with dve.Fori(0, rows - 1) as row:
                row_stages(row + 1, lambda p: experts(row, block_at(POINTS[p])),
                           lambda turn, k: experts(row, block_in_turn(turn, k)))
                dve.wait_ge(e_c.sem, e_c.by(row))
                take_live(row + 1)
                finish_row(row, False)
                dve.wait_ge(o_done.sem, o_done.by(row))
                take_residual(row + 1)
            for k in range(RING):
                experts(rows - 1, block_at(k))
            with dve.Fori(1, PAIRS // RING) as lap:
                for k in range(RING):
                    experts(rows - 1, block_in_lap(lap, k))
            experts(rows - 1, block_at(PAIRS))
            finish_row(rows - 1, True)


def kernel(**inputs):
    import numpy as np
    import concourse.bacc as bacc
    from concourse.bass_utils import run_bass_kernel_spmd as run

    i = {k.replace("L0_", ""): np.asarray(v) for k, v in inputs.items()}
    rows = i["attn_hidden_states"].shape[0]

    def lay(a):
        return np.ascontiguousarray(a)

    up = i["ffn_w_gate"].reshape(GROUPS, GP, 2, INTER, DM).transpose(1, 0, 4, 2, 3).reshape(PAIRS, P, P)
    down = i["ffn_w_down"].reshape(GROUPS, GP, 2, DM, INTER).transpose(1, 0, 2, 4, 3).reshape(PAIRS, P, P)
    cols = np.zeros((P, 9), np.float32)
    for at, name in ((0, "attn_conv_b"), (2, "attn_dt_proj_b"), (4, "attn_D_skip"), (6, "attn_input_ln_w"),
                     (7, "attn_pre_moe_ln_w")):
        v = i[name].reshape(-1, P)
        cols[:, at:at + len(v)] = v.T
    cols[:RANK, 8] = i["attn_dt_ln_w"]
    arrays = {
        "x": lay(i["attn_hidden_states"]), "in_w": lay(i["attn_in_proj_w"]), "conv_w": lay(i["attn_conv_w"]),
        "cols": cols, "xproj_w": lay(i["attn_x_proj_w"]), "dtproj_w": lay(i["attn_dt_proj_w"]),
        "b_ln": lay(i["attn_b_ln_w"]),
        "c_ln": lay(i["attn_c_ln_w"]), "a_log": lay(i["attn_A_log"]),
        "out_w": lay(i["attn_out_proj_w"]),
        "gate_w": lay(i["attn_gate_w"]), "up_w": lay(i["attn_up_w"]), "down_w": lay(i["attn_down_w"]),
        "router_cm": lay(i["ffn_router_w"].T), "bias": lay(i["ffn_expert_bias"]),
        "up": lay(up), "down": lay(down),
        "shared_up": lay(i["ffn_w_gate_shared"].T), "shared_down": lay(i["ffn_w_down_shared"].T),
        "c_cm": lay(i["c"].T), "mod_w": lay(i["wmod"]),
    }
    nc = bacc.Bacc("TRN2", target_bir_lowering=False, num_devices=1)
    args = {n: nc.dram_tensor(f"in_{n}", a.shape, F32, kind="ExternalInput").ap() for n, a in arrays.items()}
    out = nc.dram_tensor("out_0", (rows, SEQ, DM), F32, kind="ExternalOutput").ap()
    build(nc, args, out, rows)
    r = run(nc, [{f"in_{n}": a for n, a in arrays.items()}], core_ids=[0])
    return r.results[0]["out_0"]
```

```python
from contextlib import ExitStack

import concourse.bass as bass
from concourse import mybir

ALU = mybir.AluOpType
ACT = mybir.ActivationFunctionType
BF16 = mybir.dt.bfloat16
F32 = mybir.dt.float32
F32R = mybir.dt.float32r
AX_X = mybir.AxisListType.X

P = 128
DM = 128
DI = 256
HALVES = DI // P
NS = 16
RANK = 64
TAPS = 4
FF = 512
FB = FF // P
EXPERTS = 160
TOPK = 8
INTER = 64
SCALE = 2.5
PROJ = RANK + 2 * NS
SEQ = 512
TILES = SEQ // P
EPS_LN = 1e-5
EPS_RMS = 1e-6

PAIRS = EXPERTS // 2
GROUPS = EXPERTS // 32
GP = 16
RING = 10
HRING = 5
BLOCKS = PAIRS + 1
LAG = 3
LOOP_PAIRS = 8
BEFORE = 4
STATES_PER_TURN = 4
TURNS = NS // STATES_PER_TURN
PER_TURN = LOOP_PAIRS * GROUPS // TURNS
FIRST_LOOP = BEFORE * GROUPS
FIRST_AFTER = FIRST_LOOP + LOOP_PAIRS * GROUPS
SPLIT = 2
CUTS = PAIRS // SPLIT // TURNS
OUTS = RING // SPLIT
TURN_SHARE = [0, 3, 5, 8, 10]
FFN_BANKS = [(0, 2), (1, 0), (2, 1), (0, 2)]
assert PER_TURN == RING and RING % 2 == 0 and RING % HRING == 0 and FIRST_LOOP % HRING == 0
assert CUTS == PER_TURN == HRING * SEQ // (SPLIT * P) and CUTS % OUTS == 0

A_POINTS = {f"a{i + 1}": i for i in range(FIRST_LOOP)}
C_POINTS = {f"c{i + 1}": FIRST_AFTER + i for i in range(BLOCKS - FIRST_AFTER)}
POINTS = {**A_POINTS, **C_POINTS}


class Block:

    def __init__(self, q, slot, pair, lap):
        self.q, self.slot, self.pair, self.lap = q, slot, pair, lap
        self.group, self.h_slot, self.two = slot % GROUPS, slot % HRING, slot % 2

    def before(self, n):
        return Block(self.q - n, (self.slot - n) % RING, None, None)


def block_at(q):
    return Block(q, q % RING, q // GROUPS if q < PAIRS else None, q // RING)


def block_in_turn(turn, k):
    at = FIRST_LOOP + k
    return Block(PER_TURN * turn + at, at % RING, PER_TURN // GROUPS * turn + at // GROUPS, turn + at // RING)


def block_in_lap(lap, k):
    return Block(RING * lap + k, k, RING // GROUPS * lap + k // GROUPS, lap)


class Signal:

    def __init__(self, sem, per_row, credit):
        self.sem, self.per_row, self.credit = sem, per_row, credit

    def by(self, row, k=None):
        return row * self.per_row + (self.per_row if k is None else k) + self.credit


def build(nc, A, out, rows):
    with ExitStack() as ctx:
        def sb(name, shape, dt=F32):
            return ctx.enter_context(nc.sbuf_tensor(name, shape, dt))

        def bank(name, dt=F32):
            return ctx.enter_context(nc.psum_tensor(name, [P, 2048 // (4 if dt == F32 else 2)], dt))

        def sig(name, per_row=1, credit=0):
            return Signal(ctx.enter_context(nc.semaphore(name)), per_row, credit)

        ident = sb("ident", [P, P])
        identb = sb("identb", [P, P], BF16)
        pair_sel = sb("pair_sel", [96, GP, P], BF16)
        row_sel = sb("row_sel", [96, 2 * NS, P], BF16)
        neg_half = sb("neg_half", [P, 16])
        raised = sb("raised", [1, 7 + OUTS])
        in_w = sb("in_w", [P, 2 * DI])
        conv_w = sb("conv_w", [P, HALVES, TAPS])
        cols = sb("cols", [P, 9])
        xproj_w = sb("xproj_w", [P, HALVES, PROJ])
        dtproj_w = sb("dtproj_w", [RANK, DI])
        a_neg = sb("a_neg", [P, HALVES, NS])
        out_w = sb("out_w", [P, HALVES, DM])
        gate_w = sb("gate_w", [P, FF])
        up_w = sb("up_w", [P, FF])
        down_w = sb("down_w", [P, FB, DM])
        bc_w = sb("bc_w", [P, 2, NS])
        bias_w = sb("bias_w", [P, EXPERTS])
        router_w = sb("router_w", [P, EXPERTS])
        shared_up = sb("shared_up", [P, INTER])
        shared_parts = sb("shared_parts", [P, 2, INTER], F32R)
        shared_down = sb("shared_down", [INTER, DM])
        c_cm = sb("c_cm", [P, rows])
        c_th = sb("c_th", [P, rows])
        c_sl = sb("c_sl", [P, rows])
        mod_w = sb("mod_w", [P, 6 * DM])
        mod_all = sb("mod_all", [rows, 6, DM])
        mod_abs = sb("mod_abs", [rows, 2, DM])
        mod_sgn = sb("mod_sgn", [rows, 2, DM])
        CONV_B, DT_B, D_HALF, IN_LN, PRE_LN, DT_LN = 0, 2, 4, 6, 7, 8

        mod = sb("mod", [P, 5, DM])
        SH1, SC1, G1, SH2, SC2, G2 = range(6)
        x_tm = sb("x_tm", [P, TILES, DM])
        stats = sb("stats", [P, TILES, 6])
        mv = sb("mv", [P, TILES, 2])
        var1 = sb("var1", [P, TILES])
        rstd1 = sb("rstd1", [P, TILES])
        hs_tm = sb("hs_tm", [P, TILES, DM])
        h_tm = sb("h_tm", [P, TILES, DM])
        junk = sb("junk", [P, TILES, DM])
        ss1 = sb("ss1", [P, TILES])
        ms1 = sb("ms1", [P, TILES])
        r1 = sb("r1", [P, TILES])
        hn_tm = sb("hn_tm", [P, TILES, DM])
        h_cm = sb("h_cm", [P, SEQ])
        conv = [sb(f"conv{h}", [P, SEQ]) for h in range(HALVES)]
        conv_th = [sb(f"conv_th{h}", [P, SEQ]) for h in range(HALVES)]
        x2 = [sb(f"x2_{h}", [P, SEQ]) for h in range(HALVES)]
        z_th = [sb(f"z_th{h}", [P, SEQ]) for h in range(HALVES)]
        z2 = [sb(f"z2_{h}", [P, SEQ]) for h in range(HALVES)]
        proj_sq = sb("proj_sq", [P, TILES, PROJ])
        ss3 = sb("ss3", [P, TILES, 3])
        ms3 = sb("ms3", [P, TILES, 3])
        r3 = sb("r3", [P, TILES, 3])
        dtn_tm = sb("dtn_tm", [P, TILES, RANK])
        bcn = sb("bcn", [P, TILES, 2 * NS])
        bcs = sb("bcs", [P, TILES, 2 * NS])
        bc_rem = sb("bc_rem", [P, TILES, 2 * NS])
        bc_parts = sb("bc_parts", [P, TILES, 3, 2 * NS], BF16)
        dtn_cm = sb("dtn_cm", [RANK, SEQ])
        bc_cm = sb("bc_cm", [96, SEQ], BF16)
        dt_min = conv
        dt_exp = conv_th
        dt_ln = z_th
        dt = [sb(f"dt{h}", [P, SEQ]) for h in range(HALVES)]
        dtx = [sb(f"dtx{h}", [P, SEQ]) for h in range(HALVES)]
        c_sb = [sb(f"c_sb{i}", [P, SEQ]) for i in range(2)]
        dbx = [sb(f"dbx{h}", [P, SEQ]) for h in range(HALVES)]
        state = [[sb(f"state{i}{h}", [P, SEQ]) for h in range(HALVES)] for i in range(2)]
        read = [sb(f"read{h}", [P, SEQ]) for h in range(HALVES)]
        y = [sb(f"y{h}", [P, SEQ]) for h in range(HALVES)]
        yz = [sb(f"yz{h}", [P, SEQ]) for h in range(HALVES)]
        hid_tm = sb("hid_tm", [P, TILES, DM])
        ss2 = sb("ss2", [P, TILES])
        ms2 = sb("ms2", [P, TILES])
        r2 = sb("r2", [P, TILES])
        f_th, f_v, f_act = read, dbx, dt + dtx
        att_tm = sb("att_tm", [P, TILES, DM])
        gat_tm = sb("gat_tm", [P, TILES, DM])
        x1_tm = sb("x1_tm", [P, TILES, DM])
        stats2 = sb("stats2", [P, TILES, 6])
        mv2 = sb("mv2", [P, TILES, 2])
        var2 = sb("var2", [P, TILES])
        rstd2 = sb("rstd2", [P, TILES])
        hs2_tm = hs_tm
        h2_tm = sb("h2_tm", [P, TILES, DM])
        h2_cm = sb("h2_cm", [P, SEQ])
        logits = sb("logits", [P, TILES, EXPERTS])
        l_exp = sb("l_exp", [P, TILES, EXPERTS])
        l_one = logits
        probs = sb("probs", [P, TILES, EXPERTS])
        top = sb("top", [P, TILES, TOPK])
        rest = sb("rest", [P, TILES, EXPERTS])
        chosen = sb("chosen", [P, TILES, EXPERTS])
        top_sum = sb("top_sum", [P, TILES])
        top_inv = sb("top_inv", [P, TILES])
        top_fac = sb("top_fac", [P, TILES])
        comb = sb("comb", [P, TILES, EXPERTS])
        comb_rem = sb("comb_rem", [P, TILES, EXPERTS])
        comb_parts = sb("comb_parts", [P, TILES, GROUPS, 3, 32], BF16)

        h2_live = [sb(f"h2_live{i}", [P, SEQ], F32R) for i in range(2)]
        comb_live = sb("comb_live", [96, GROUPS, SEQ], BF16)
        x1_live = sb("x1_live", [P, TILES, DM])
        g2_live = sb("g2_live", [P, DM])
        up_ring = sb("up_ring", [P, RING, 2, P])
        up_exact = up_ring[:, :, :, :].bitcast(F32R)
        down_ring = sb("down_ring", [P, RING, P])
        e_th = [sb(f"e_th{i}", [P, SEQ]) for i in range(2)]
        e_h = sb("e_h", [P, HRING, SEQ])
        e_out = sb("e_out", [P, SEQ])
        raw_up = e_h[:, :, :].rearrange("p h s -> p (h s)").rearrange("p (k i n) -> p k i n", i=SPLIT, n=P)
        e_gat = sb("e_gat", [P, TILES, DM])
        o_tm = sb("o_tm", [P, TILES, DM])

        up_bank = [bank("up_bank0"), bank("up_bank1")]
        comb_bank = [bank("comb_bank0"), bank("comb_bank1")]
        acc_bank = bank("acc_bank")
        M = [bank("m0"), bank("m1"), bank("m2")]
        b_bank, c_bank, da_bank = M
        Mb = [b[:, :].bitcast(BF16) for b in M]

        c_loaded = [sig(f"c_loaded{i}") for i in range(3)]
        ident_zero, ident_done = sig("ident_zero"), sig("ident_done")
        sel_done = sig("sel_done")
        prep = sig("prep")
        c_tanh, c_silu, mod_mm, mod_raw, mod_half, mod_done, mod_out = (
            sig(n) for n in ("c_tanh", "c_silu", "mod_mm", "mod_raw", "mod_half", "mod_done", "mod_out"))
        a_exp = sig("a_exp")
        x_in, mod_in, g2_in = sig("x_in", 16), sig("mod_in", 16), sig("g2_in", 16)
        ln1_st, ln1_mv, ln1_var, ln1_rs = sig("ln1_st", 4), sig("ln1_mv", 4), sig("ln1_var"), sig("ln1_rs")
        hs_done, h_done = sig("hs_done", 4), sig("h_done", 4)
        ss1_done, ms1_done, r1_done, hn_done = sig("ss1_done", 4), sig("ms1_done"), sig("r1_done"), sig("hn_done", 4)
        hT_mm, hT_done = sig("hT_mm"), sig("hT_done")
        in_mm = sig("in_mm", 4)
        conv_done = sig("conv_done", 2 * TAPS)
        convth_done, x2_done = sig("convth_done", 2), sig("x2_done", 2)
        zth_done, z2_done = sig("zth_done", 2), sig("z2_done", 2)
        proj_mm, sq3_done, ss3_done, ms3_done, r3_done = (
            sig("proj_mm"), sig("sq3_done"), sig("ss3_done", 2), sig("ms3_done", 2), sig("r3_done"))
        dtn_done, bcn_done, bcs_done, bcp_done = sig("dtn_done"), sig("bcn_done"), sig("bcs_done"), sig("bcp_done", 4)
        dtT_mm, bcT_mm, dtT_done, bcT_done = sig("dtT_mm"), sig("bcT_mm"), sig("dtT_done"), sig("bcT_done")
        dt_mm, dtmin_done, dtexp_done, dtln_done, dt_done = (
            sig("dt_mm", 2), sig("dtmin_done", 2), sig("dtexp_done", 2), sig("dtln_done", 2), sig("dt_done", 2))
        dtx_done, y0_done = sig("dtx_done", 2), sig("y0_done", 2)
        b_mm, cn_mm, c_copied = sig("b_mm", NS), sig("cn_mm", NS), sig("c_copied", NS, credit=1)
        da_done, dbx_done, scan_done = sig("da_done", 2 * NS), sig("dbx_done", 2 * NS, credit=1), sig("scan_done", 2 * NS, credit=1)
        read_done, y_done = sig("read_done", 2 * NS, credit=4), sig("y_done", 2 * NS, credit=2)
        yz_done, outp_mm, hid_done = sig("yz_done", 2), sig("outp_mm"), sig("hid_done")
        ss2_done, ms2_done, r2_done, hn2_done = sig("ss2_done", 4), sig("ms2_done"), sig("r2_done"), sig("hn2_done", 4)
        hT2_mm, hT2_done = sig("hT2_mm"), sig("hT2_done")
        fg_mm, fu_mm, fth_done, fv_done, fa_done = (
            sig("fg_mm", FB), sig("fu_mm", FB), sig("fth_done", FB), sig("fv_done", FB), sig("fa_done", FB))
        down_mm, att_done, gat_done, x1_done = sig("down_mm"), sig("att_done"), sig("gat_done"), sig("x1_done")
        ln2_st, ln2_mv, ln2_var, ln2_rs = sig("ln2_st", 4), sig("ln2_mv", 4), sig("ln2_var"), sig("ln2_rs")
        hs2_done, h2_done = sig("hs2_done", 4), sig("h2_done", 4)
        h2T_mm, h2T_done = sig("h2T_mm"), sig("h2T_done")
        rt_mm, lg_done, lexp_done, lone_done, probs_done = (
            sig("rt_mm"), sig("lg_done", 2), sig("lexp_done"), sig("lone_done"), sig("probs_done", 4))
        top_done, rest_done, chosen_done = sig("top_done", 4), sig("rest_done", 4), sig("chosen_done", 4)
        tops_done, comb_done, combp_done = sig("tops_done", 3), sig("comb_done", 4), sig("combp_done", 4)
        combT_mm = sig("combT_mm")
        live_h2, live_comb, live_x1 = sig("live_h2"), sig("live_comb", 3), sig("live_x1")
        raw_in = [sig(f"raw_in{k}") for k in range(CUTS)]
        hi_done, lo_done = sig("hi_done"), sig("lo_done")
        split_out = [sig(f"split_out{k}", credit=16) for k in range(OUTS)]
        shared_split, live_lo = sig("shared_split"), sig("live_lo")
        w_in = [sig(f"w_in{k}", 32 * PAIRS // RING) for k in range(RING)]
        e_up, e_c, e_tanh, e_vd, e_hd, e_down = (
            sig(n, BLOCKS) for n in ("e_up", "e_c", "e_tanh", "e_vd", "e_hd", "e_down"))
        e_c.per_row = e_hd.per_row = PAIRS
        eo_done, eT_mm, eg_done, o_done, o_out = sig("eo_done", credit=1), sig("eT_mm"), sig("eg_done"), sig("o_done"), sig("o_out", 16, credit=1)

        up_parts = nc.dram_tensor("up_parts", (PAIRS, P, 2, P), F32, kind="Internal").ap()
        mod_dram = nc.dram_tensor("mod_rows", (rows + 1, 6 * DM), F32, kind="Internal").ap()
        x_dram = A["x"].rearrange("b (t p) d -> b p t d", p=P)
        out_dram = out.rearrange("b (t p) d -> b p t d", p=P)

        def tiles_of(ap, row):
            return ap[bass.ds(row, 1)].rearrange("o p t d -> p (o t) d")

        LOADS = [
            (0, c_cm[:, :], A["c_cm"]), (0, mod_w[:, :], A["mod_w"]),
            (1, in_w[:, :], A["in_w"]), (1, conv_w[:, :, :], A["conv_w"].rearrange("(h p) k -> p h k", p=P)),
            (1, cols[:, :], A["cols"]),
            (1, xproj_w[:, :, :], A["xproj_w"].rearrange("(h p) n -> p h n", p=P)),
            (1, dtproj_w[:, :], A["dtproj_w"]),
            (1, a_neg[:, :, :], A["a_log"].rearrange("(h p) n -> p h n", p=P)),
            (2, bc_w[:, 0, :], A["b_ln"].rearrange("(o n) -> o n", o=1).to_broadcast([P, NS])),
            (2, bc_w[:, 1, :], A["c_ln"].rearrange("(o n) -> o n", o=1).to_broadcast([P, NS])),
            (2, bias_w[:, :], A["bias"].rearrange("(o n) -> o n", o=1).to_broadcast([P, EXPERTS])),
            (2, out_w[:, :, :], A["out_w"].rearrange("(h p) n -> p h n", p=P)),
            (2, gate_w[:, :], A["gate_w"]), (2, up_w[:, :], A["up_w"]),
            (2, down_w[:, :, :], A["down_w"].rearrange("(f p) n -> p f n", p=P)),
            (2, router_w[:, :], A["router_cm"]), (2, shared_up[:, :], A["shared_up"]),
            (2, shared_down[:, :], A["shared_down"]),
        ]
        N_LOADS = [16 * sum(q == k for q, _, _ in LOADS) for k in range(3)]
        N_PREP = 11

        block = ctx.enter_context(nc.Block())

        @block.sync
        def _(sp):
            for q, dst, src in LOADS:
                if q:
                    sp.dma_start(dst, src).then_inc(c_loaded[q].sem, 16)
            def load_raw(k, cut):
                sp.dma_start(raw_up[:, k, :, :], A["up"][bass.ds(cut * SPLIT, SPLIT)].rearrange("i p n -> p i n"))\
                    .then_inc(raw_in[k].sem, 16)

            def store_parts(k, cut):
                sp.wait_ge(lo_done.sem, cut + 1)
                sp.dma_start(up_parts[bass.ds(cut * SPLIT, SPLIT)].rearrange("i p a n -> p i a n"),
                             up_ring[:, k % OUTS * SPLIT:(k % OUTS + 1) * SPLIT, :, :])\
                    .then_inc(split_out[k % OUTS].sem, 16)

            def load(k, source):
                sp.dma_start(up_ring[:, k, :, :], up_parts[bass.ds(source, 1)].rearrange("o p a n -> p (o a) n"))\
                    .then_inc(w_in[k].sem, 16)
                sp.dma_start(down_ring[:, k, :], A["down"][bass.ds(source, 1)].rearrange("o p n -> p (o n)"))\
                    .then_inc(w_in[k].sem, 16)

            for k in range(CUTS):
                load_raw(k, k)
            with sp.Fori(0, TURNS - 1) as turn:
                for k in range(CUTS):
                    store_parts(k, CUTS * turn + k)
                    load_raw(k, CUTS * turn + k + CUTS)
            for k in range(CUTS):
                store_parts(k, CUTS * (TURNS - 1) + k)
            for k in range(OUTS):
                sp.wait_ge(split_out[k].sem, split_out[k].credit + 16 * TURNS * CUTS // OUTS)
            for k in range(RING):
                load(k, k)

            def refill(row, turn, source):
                for k in range(RING):
                    sp.wait_ge(e_down.sem, e_down.by(row, RING * turn + k + 1))
                    load(k, source + k)

            with sp.Fori(0, rows - 1) as row:
                with sp.Fori(0, PAIRS // RING - 1) as turn:
                    refill(row, turn, RING * turn + RING)
                refill(row, PAIRS // RING - 1, 0)
            with sp.Fori(0, PAIRS // RING - 1) as turn:
                refill(rows - 1, turn, RING * turn + RING)

        @block.gpsimd
        def _(pool):
            def root(dst, src, n):
                return nc.gpsimd.tensor_tensor(dst, src, neg_half[:, 0:n], ALU.pow)

            def norm_root(m):
                pool.wait_ge(ln1_var.sem, ln1_var.by(m))
                root(rstd1[:, :], var1[:, :], TILES).then_inc(ln1_rs.sem, 1)

            nc.gpsimd.memset(ident[:, :], 0.0).then_inc(ident_zero.sem, 1)
            nc.gpsimd.memset(identb[:, :], 0.0).then_inc(ident_zero.sem, 1)
            nc.gpsimd.memset(neg_half[:, :], -0.5).then_inc(ident_zero.sem, 1)
            for i, s in enumerate((read_done, scan_done, dbx_done, c_copied, y_done, eo_done, o_out, *split_out)):
                nc.gpsimd.memset(raised[:, i:i + 1], 0.0).then_inc(s.sem, s.credit)
            pool.wait_ge(ident_zero.sem, 3)
            for t in (ident, identb):
                nc.gpsimd.affine_select(out=t[:, :], in_=t[:, :], compare_op=ALU.not_equal, fill=1.0, base=0,
                                        pattern=[[-1, P]], channel_multiplier=1).then_inc(ident_done.sem, 1)
            nc.gpsimd.memset(pair_sel[:, :, :], 0.0).then_inc(ident_zero.sem, 1)
            nc.gpsimd.memset(row_sel[:, :, :], 0.0).then_inc(ident_zero.sem, 1)
            norm_root(0)
            pool.wait_ge(ident_zero.sem, 5)
            sel_v = pair_sel[:, :, :].rearrange("p j (e i) -> p j e i", e=2)
            for part in range(3):
                if part:
                    pool.wait_ge(sel_done.sem, 2 * part)
                nc.gpsimd.affine_select(out=sel_v, in_=sel_v, compare_op=ALU.not_equal, fill=1.0, base=-32 * part,
                                        pattern=[[-2, GP], [-1, 2], [0, INTER]], channel_multiplier=1)\
                    .then_inc(sel_done.sem, 1)
                nc.gpsimd.affine_select(out=row_sel[:, :, :], in_=row_sel[:, :, :], compare_op=ALU.not_equal,
                                        fill=1.0, base=-32 * part, pattern=[[-1, 2 * NS], [0, P]],
                                        channel_multiplier=1).then_inc(sel_done.sem, 1)

            def row_stages(m):
                pool.wait_ge(ms1_done.sem, ms1_done.by(m))
                root(r1[:, :], ms1[:, :], TILES).then_inc(r1_done.sem, 1)
                pool.wait_ge(ms3_done.sem, ms3_done.by(m))
                root(r3[:, :, :].rearrange("p t k -> p (t k)"), ms3[:, :, :].rearrange("p t k -> p (t k)"), 3 * TILES)\
                    .then_inc(r3_done.sem, 1)
                pool.wait_ge(x2_done.sem, x2_done.by(m))
                for h in range(HALVES):
                    nc.gpsimd.tensor_tensor(y[h][:, :], x2[h][:, :], cols[:, D_HALF + h:D_HALF + h + 1]
                                            .to_broadcast([P, SEQ]), ALU.mult).then_inc(y0_done.sem, 1)
                with pool.Fori(0, TURNS) as turn:
                    pool.wait_ge(y0_done.sem, y0_done.by(m))
                    for s in range(STATES_PER_TURN):
                        for h in range(HALVES):
                            k = STATES_PER_TURN * HALVES * turn + HALVES * s + h
                            pool.wait_ge(scan_done.sem, scan_done.by(m, k + 1))
                            pool.wait_ge(y_done.sem, y_done.by(m, k - 1))
                            if h == 0:
                                pool.wait_ge(c_copied.sem, c_copied.by(m, STATES_PER_TURN * turn + s + 1))
                            nc.gpsimd.tensor_tensor(read[h][:, :], state[s % 2][h][:, :], c_sb[s % 2][:, :], ALU.mult)\
                                .then_inc(read_done.sem, 1)
                        for h in range(HALVES):
                            k = STATES_PER_TURN * HALVES * turn + HALVES * s + h
                            pool.wait_ge(read_done.sem, read_done.by(m, k + 1))
                            nc.gpsimd.tensor_tensor(y[h][:, :], y[h][:, :], read[h][:, :], ALU.add)\
                                .then_inc(y_done.sem, 1)
                pool.wait_ge(ms2_done.sem, ms2_done.by(m))
                root(r2[:, :], ms2[:, :], TILES).then_inc(r2_done.sem, 1)
                pool.wait_ge(ln2_var.sem, ln2_var.by(m))
                root(rstd2[:, :], var2[:, :], TILES).then_inc(ln2_rs.sem, 1)

            row_stages(0)
            with pool.Fori(0, rows - 1) as row:
                norm_root(row + 1)
                row_stages(row + 1)

        @block.tensor
        def _(pe):
            def transposed(dst, src, width, idn):
                for t in range(TILES):
                    last = nc.tensor.transpose(dst[0:width, t * P:(t + 1) * P], src(t), idn[:, :])
                return last

            def up(row, e, steady):
                shared = e.pair is None
                if steady:
                    pe.wait_ge(e_vd.sem, e_vd.by(row, e.q - 1))
                if not shared:
                    pe.wait_ge(w_in[e.slot].sem, w_in[e.slot].by(row, 32 * (e.lap + 1)))
                for w, h in ((0, 0), (0, 1), (1, 0)):
                    last = nc.tensor.matmul(up_bank[e.two][0:INTER if shared else P, :],
                                            shared_parts[:, w, :] if shared else up_exact[:, e.slot, w, :],
                                            h2_live[h][:, :], start=(w + h == 0), stop=(w == 1))
                last.then_inc(e_up.sem, 1)

            def spread_weights(row, e, steady):
                if e.pair is None:
                    return
                if steady:
                    pe.wait_ge(e_hd.sem, e_hd.by(row, e.q - 1))
                nc.tensor.matmul(comb_bank[e.two][:, :], pair_sel[:, e.pair, :] if isinstance(e.pair, int) else
                                 pair_sel[:, bass.ds(e.pair, 1), :].rearrange("p o n -> p (o n)"),
                                 comb_live[:, e.group, :], start=True, stop=True).then_inc(e_c.sem, 1)

            def down(row, e, first=False, shared=False):
                if shared:
                    pe.wait_ge(e_vd.sem, e_vd.by(row))
                    nc.tensor.matmul(acc_bank[:, :], shared_down[:, :], e_h[0:INTER, e.h_slot, :], start=False,
                                     stop=True).then_inc(e_down.sem, 1)
                else:
                    pe.wait_ge(e_hd.sem, e_hd.by(row, e.q + 1))
                    nc.tensor.matmul(acc_bank[:, :], down_ring[:, e.slot, :], e_h[:, e.h_slot, :], start=first,
                                     stop=False).then_inc(e_down.sem, 1)

            def experts(row, q):
                if q == 0:
                    pe.wait_ge(live_comb.sem, live_comb.by(row))
                if q >= 2:
                    up(row, block_at(q), steady=True)
                if q == LAG:
                    pe.wait_ge(eo_done.sem, eo_done.by(row, 0))
                if q >= LAG:
                    down(row, block_at(q - LAG), first=q == LAG)
                spread_weights(row, block_at(q), steady=q >= 2)

            def first_ups(row):
                pe.wait_ge(live_h2.sem, live_h2.by(row))
                pe.wait_ge(live_lo.sem, live_lo.by(row))
                if not isinstance(row, int):
                    pe.wait_ge(e_vd.sem, e_vd.by(row - 1))
                for q in range(2):
                    up(row, block_at(q), steady=False)

            def finish_experts(row):
                for back in range(LAG - 1, 0, -1):
                    down(row, block_at(PAIRS - back))
                down(row, block_at(PAIRS), shared=True)

            def turn_out(row):
                pe.wait_ge(eo_done.sem, eo_done.by(row))
                transposed(M[0], lambda t: e_out[:, t * P:(t + 1) * P], P, ident).then_inc(eT_mm.sem, 1)

            def row_stages(m, at, scan_experts):
                for p in ("a1", "a2", "a3", "a4", "a5", "a6", "a7"):
                    at(p)
                pe.wait_ge(hn_done.sem, hn_done.by(m))
                transposed(M[0], lambda t: hn_tm[:, t, :], P, ident).then_inc(hT_mm.sem, 1)
                at("a8")
                pe.wait_ge(hT_done.sem, hT_done.by(m))
                for h in range(HALVES):
                    nc.tensor.matmul(M[1 + h][:, :], in_w[:, h * P:(h + 1) * P], h_cm[:, :], start=True, stop=True)\
                        .then_inc(in_mm.sem, 1)
                nc.tensor.matmul(M[0][:, :], in_w[:, DI:DI + P], h_cm[:, :], start=True, stop=True)\
                    .then_inc(in_mm.sem, 1)
                at("a9")
                at("a10")
                pe.wait_ge(conv_done.sem, conv_done.by(m, TAPS))
                nc.tensor.matmul(M[1][:, :], in_w[:, DI + P:], h_cm[:, :], start=True, stop=True)\
                    .then_inc(in_mm.sem, 1)
                at("a11")
                at("a12")
                pe.wait_ge(x2_done.sem, x2_done.by(m))
                for t in range(TILES):
                    for h in range(HALVES):
                        last = nc.tensor.matmul(M[2][:, t * PROJ:(t + 1) * PROJ], x2[h][:, t * P:(t + 1) * P],
                                                xproj_w[:, h, :], start=(h == 0), stop=(h == HALVES - 1))
                last.then_inc(proj_mm.sem, 1)
                for p in ("a13", "a14", "a15", "a16"):
                    at(p)
                pe.wait_ge(dtn_done.sem, dtn_done.by(m))
                pe.wait_ge(z2_done.sem, z2_done.by(m))
                pe.wait_ge(bcp_done.sem, bcp_done.by(m))
                transposed(Mb[1], lambda t: bc_parts[:, t, :, :].rearrange("p s n -> p (s n)"), 96, identb)\
                    .then_inc(bcT_mm.sem, 1)
                transposed(M[0], lambda t: dtn_tm[:, t, :], RANK, ident).then_inc(dtT_mm.sem, 1)
                at("a17")
                pe.wait_ge(dtT_done.sem, dtT_done.by(m))
                for h in range(HALVES):
                    nc.tensor.matmul(M[2 * (1 - h)][:, :], dtproj_w[:, h * P:(h + 1) * P], dtn_cm[:, :], start=True,
                                     stop=True).then_inc(dt_mm.sem, 1)
                for p in ("a18", "a19", "a20"):
                    at(p)
                with pe.Fori(0, TURNS) as turn:
                    pe.wait_ge(sel_done.sem, 6)
                    pe.wait_ge(bcT_done.sem, bcT_done.by(m))
                    pe.wait_ge(dt_done.sem, dt_done.by(m))
                    for s in range(STATES_PER_TURN):
                        n = STATES_PER_TURN * turn + s
                        pe.wait_ge(dbx_done.sem, dbx_done.by(m, HALVES * n))
                        nc.tensor.matmul(b_bank[:, :], row_sel[:, bass.ds(n, 1), :].rearrange("p o n -> p (o n)"),
                                         bc_cm[:, :], start=True, stop=True).then_inc(b_mm.sem, 1)
                        pe.wait_ge(c_copied.sem, c_copied.by(m, n))
                        nc.tensor.matmul(c_bank[:, :], row_sel[:, bass.ds(n + NS, 1), :].rearrange("p o n -> p (o n)"),
                                         bc_cm[:, :], start=True, stop=True).then_inc(cn_mm.sem, 1)
                        for k in range(TURN_SHARE[s], TURN_SHARE[s + 1]):
                            scan_experts(turn, k)
                at("c1")
                at("c2")
                pe.wait_ge(yz_done.sem, yz_done.by(m))
                for t in range(TILES):
                    for h in range(HALVES):
                        last = nc.tensor.matmul(M[0][:, t * P:(t + 1) * P], yz[h][:, t * P:(t + 1) * P], out_w[:, h, :],
                                                start=(h == 0), stop=(h == HALVES - 1))
                last.then_inc(outp_mm.sem, 1)
                for p in ("c3", "c4", "c5"):
                    at(p)
                pe.wait_ge(hn2_done.sem, hn2_done.by(m))
                transposed(M[1], lambda t: hn_tm[:, t, :], P, ident).then_inc(hT2_mm.sem, 1)
                at("c6")
                pe.wait_ge(hT2_done.sem, hT2_done.by(m))
                for f in range(FB):
                    g, u = FFN_BANKS[f]
                    if f:
                        pe.wait_ge(fv_done.sem, fv_done.by(m, f))
                    if f >= 2:
                        pe.wait_ge(fa_done.sem, fa_done.by(m, f - 1))
                    nc.tensor.matmul(M[g][:, :], gate_w[:, f * P:(f + 1) * P], h_cm[:, :], start=True, stop=True)\
                        .then_inc(fg_mm.sem, 1)
                    nc.tensor.matmul(M[u][:, :], up_w[:, f * P:(f + 1) * P], h_cm[:, :], start=True, stop=True)\
                        .then_inc(fu_mm.sem, 1)
                    at(f"c{7 + f}")
                pe.wait_ge(fa_done.sem, fa_done.by(m))
                for t in range(TILES):
                    for f in range(FB):
                        last = nc.tensor.matmul(M[1][:, t * P:(t + 1) * P], f_act[f][:, t * P:(t + 1) * P],
                                                down_w[:, f, :], start=(f == 0), stop=(f == FB - 1))
                last.then_inc(down_mm.sem, 1)
                for p in ("c11", "c12", "c13", "c14", "c15"):
                    at(p)
                pe.wait_ge(h2_done.sem, h2_done.by(m))
                transposed(M[0], lambda t: h2_tm[:, t, :], P, ident).then_inc(h2T_mm.sem, 1)
                at("c16")
                pe.wait_ge(h2T_done.sem, h2T_done.by(m))
                for t in range(TILES):
                    last = nc.tensor.matmul(M[1 + t // 3][:, t % 3 * EXPERTS:(t % 3 + 1) * EXPERTS],
                                            h2_cm[:, t * P:(t + 1) * P], router_w[:, :], start=True, stop=True)
                last.then_inc(rt_mm.sem, 1)
                for p in ("c17", "c18", "c19", "c20", "c21"):
                    at(p)

            def turn_weights(m):
                pe.wait_ge(combp_done.sem, combp_done.by(m))
                for g in range(GROUPS):
                    half = g % 2 * SEQ
                    last = transposed(Mb[g // 2][:, half:half + SEQ],
                                      lambda t: comb_parts[:, t, g, :, :].rearrange("p s e -> p (s e)"), 96, identb)
                last.then_inc(combT_mm.sem, 1)

            pe.wait_ge(c_silu.sem, 1)
            nc.tensor.matmul(M[0][0:rows, :], c_sl[:, :], mod_w[:, 0:512], start=True, stop=True)
            nc.tensor.matmul(M[1][0:rows, 0:256], c_sl[:, :], mod_w[:, 512:768], start=True, stop=True)\
                .then_inc(mod_mm.sem, 1)
            pe.wait_ge(ident_done.sem, 2)
            pe.wait_ge(prep.sem, N_PREP)
            pe.wait_ge(c_loaded[2].sem, N_LOADS[2])
            row_stages(0, lambda p: None, lambda turn, k: None)
            pe.wait_ge(shared_split.sem, 2)
            first_ups(0)
            turn_weights(0)
            with pe.Fori(0, rows - 1) as row:
                def in_scan(turn, k):
                    e = block_in_turn(turn, k)
                    up(row, e, True)
                    down(row, e.before(LAG))
                    spread_weights(row, e, True)
                row_stages(row + 1, lambda p: experts(row, POINTS[p]), in_scan)
                finish_experts(row)
                first_ups(row + 1)
                turn_weights(row + 1)
                pe.wait_ge(live_comb.sem, live_comb.by(row + 1))
                turn_out(row)
            for q in range(RING):
                experts(rows - 1, q)
            with pe.Fori(1, PAIRS // RING) as lap:
                for k in range(RING):
                    e = block_in_lap(lap, k)
                    up(rows - 1, e, True)
                    down(rows - 1, e.before(LAG))
                    spread_weights(rows - 1, e, True)
            experts(rows - 1, PAIRS)
            finish_experts(rows - 1)
            turn_out(rows - 1)

        @block.scalar
        def _(act):
            for q, dst, src in LOADS:
                if q == 0:
                    act.dma_start(dst, src).then_inc(c_loaded[0].sem, 16)

            def load_x(m):
                act.dma_start(x_tm[:, :, :], tiles_of(x_dram, m)).then_inc(x_in.sem, 16)

            def load_mod(m):
                act.dma_start(mod[:, :, :].rearrange("p s d -> p (s d)"),
                              mod_dram[bass.ds(m, 1), 0:5 * DM].to_broadcast([P, 5 * DM])).then_inc(mod_in.sem, 16)

            def load_g2(m):
                act.dma_start(g2_live[:, :], mod_dram[bass.ds(m, 1), 5 * DM:].to_broadcast([P, DM]))\
                    .then_inc(g2_in.sem, 16)

            def experts(row, e):
                act.wait_ge(e_up.sem, e_up.by(row, e.q + 1))
                n = INTER if e.pair is None else P
                nc.scalar.activation(e_th[e.two][0:n, :], up_bank[e.two][0:n, :], ACT.Tanh, scale=0.5)\
                    .then_inc(e_tanh.sem, 1)

            def square_sums(src, dst, done):
                for t in range(TILES):
                    nc.scalar.activation(junk[:, t, :], src[:, t, :], ACT.Square, accum_out=dst[:, t:t + 1])\
                        .then_inc(done.sem, 1)

            def row_stages(m, at, scan_experts):
                for p in ("a3",):
                    at(p)
                act.wait_ge(h_done.sem, h_done.by(m))
                square_sums(h_tm, ss1, ss1_done)
                for p in ("a4", "a5", "a6", "a7"):
                    at(p)
                act.wait_ge(hT_mm.sem, hT_mm.by(m))
                nc.scalar.activation(h_cm[:, :], M[0][:, :], ACT.Copy).then_inc(hT_done.sem, 1)
                at("a8")
                at("a9")
                for h in range(HALVES):
                    act.wait_ge(conv_done.sem, conv_done.by(m, TAPS * (h + 1)))
                    nc.scalar.activation(conv_th[h][:, :], conv[h][:, :], ACT.Tanh, scale=0.5)\
                        .then_inc(convth_done.sem, 1)
                    at(f"a{10 + h}")
                act.wait_ge(in_mm.sem, in_mm.by(m, 3))
                nc.scalar.activation(z_th[0][:, :], M[0][:, :], ACT.Tanh, scale=0.5).then_inc(zth_done.sem, 1)
                act.wait_ge(in_mm.sem, in_mm.by(m, 4))
                nc.scalar.activation(z_th[1][:, :], M[1][:, :], ACT.Tanh, scale=0.5).then_inc(zth_done.sem, 1)
                at("a12")
                act.wait_ge(proj_mm.sem, proj_mm.by(m))
                nc.scalar.activation(proj_sq[:, :, :].rearrange("p t n -> p (t n)"), M[2][:, 0:TILES * PROJ], ACT.Square)\
                    .then_inc(sq3_done.sem, 1)
                for p in ("a13", "a14", "a15", "a16"):
                    at(p)
                act.wait_ge(dtT_mm.sem, dtT_mm.by(m))
                nc.scalar.activation(dtn_cm[:, :], M[0][0:RANK, :], ACT.Copy).then_inc(dtT_done.sem, 1)
                act.wait_ge(bcT_mm.sem, bcT_mm.by(m))
                nc.scalar.activation(bc_cm[:, :], Mb[1][0:96, 0:SEQ], ACT.Copy).then_inc(bcT_done.sem, 1)
                at("a17")
                for h in range(HALVES):
                    act.wait_ge(dtmin_done.sem, dtmin_done.by(m, h + 1))
                    nc.scalar.activation(dt_exp[h][:, :], dt_min[h][:, :], ACT.Exp).then_inc(dtexp_done.sem, 1)
                at("a18")
                for h in range(HALVES):
                    act.wait_ge(dtexp_done.sem, dtexp_done.by(m, h + 1))
                    nc.scalar.activation(dt_ln[h][:, :], dt_exp[h][:, :], ACT.Ln, bias=1.0).then_inc(dtln_done.sem, 1)
                at("a19")
                at("a20")
                act.wait_ge(dt_done.sem, dt_done.by(m))
                with act.Fori(0, TURNS) as turn:
                    for s in range(STATES_PER_TURN):
                        n = STATES_PER_TURN * turn + s
                        k = HALVES * n
                        act.wait_ge(cn_mm.sem, cn_mm.by(m, n + 1))
                        act.wait_ge(read_done.sem, read_done.by(m, k - HALVES))
                        nc.scalar.activation(c_sb[s % 2][:, :], c_bank[:, :], ACT.Copy).then_inc(c_copied.sem, 1)
                        cut = TURN_SHARE[s], TURN_SHARE[s] + 1, TURN_SHARE[s + 1]
                        for h in range(HALVES):
                            act.wait_ge(scan_done.sem, scan_done.by(m, k + h))
                            nc.scalar.activation(da_bank[:, :], dt[h][:, :], ACT.Exp,
                                                 scale=a_neg[:, h, bass.ds(n, 1)]).then_inc(da_done.sem, 1)
                            for b in range(cut[h], cut[h + 1]):
                                scan_experts(turn, b)
                for p in ("c1", "c2", "c3"):
                    at(p)
                act.wait_ge(hid_done.sem, hid_done.by(m))
                square_sums(hid_tm, ss2, ss2_done)
                for p in ("c4", "c5"):
                    at(p)
                act.wait_ge(hT2_mm.sem, hT2_mm.by(m))
                nc.scalar.activation(h_cm[:, :], M[1][:, :], ACT.Copy).then_inc(hT2_done.sem, 1)
                at("c6")
                for f in range(FB):
                    act.wait_ge(fg_mm.sem, fg_mm.by(m, f + 1))
                    nc.scalar.activation(f_th[f % 2][:, :], M[FFN_BANKS[f][0]][:, :], ACT.Tanh, scale=0.5)\
                        .then_inc(fth_done.sem, 1)
                    at(f"c{7 + f}")
                for p in ("c11", "c12", "c13", "c14", "c15"):
                    at(p)
                act.wait_ge(h2T_mm.sem, h2T_mm.by(m))
                nc.scalar.activation(h2_cm[:, :], M[0][:, :], ACT.Copy).then_inc(h2T_done.sem, 1)
                act.wait_ge(x1_done.sem, x1_done.by(m))
                load_x(m + 1)
                act.wait_ge(h2_done.sem, h2_done.by(m))
                load_mod(m + 1)
                at("c16")
                act.wait_ge(lg_done.sem, lg_done.by(m))
                nc.scalar.activation(l_exp[:, :, :], logits[:, :, :], ACT.Exp, scale=-1.0).then_inc(lexp_done.sem, 1)
                for p in ("c17", "c18", "c19", "c20", "c21"):
                    at(p)

            def take_live(m):
                act.wait_ge(h2T_done.sem, h2T_done.by(m))
                nc.scalar.activation(h2_live[0][:, :], h2_cm[:, :], ACT.Copy).then_inc(live_h2.sem, 1)

            def first_tanhs(row):
                experts(row, block_at(0))
                experts(row, block_at(1))

            def take_sum(row):
                act.wait_ge(e_down.sem, e_down.by(row))
                nc.scalar.activation(e_out[:, :], acc_bank[:, :], ACT.Copy).then_inc(eo_done.sem, 1)

            def store(row):
                act.wait_ge(o_done.sem, o_done.by(row))
                act.dma_start(tiles_of(out_dram, row), o_tm[:, :, :]).then_inc(o_out.sem, 16)

            load_x(0)
            act.wait_ge(c_loaded[0].sem, N_LOADS[0])
            nc.scalar.activation(c_th[:, :], c_cm[:, :], ACT.Tanh, scale=0.5).then_inc(c_tanh.sem, 1)
            act.wait_ge(c_loaded[1].sem, N_LOADS[1])
            act.wait_ge(c_loaded[2].sem, N_LOADS[2])
            nc.scalar.activation(a_neg[:, :, :], a_neg[:, :, :], ACT.Exp).then_inc(a_exp.sem, 1)
            act.wait_ge(mod_done.sem, mod_done.by(0, 3))
            act.dma_start(mod_dram[0:rows], mod_all[:, :, :].rearrange("b s d -> b (s d)")).then_inc(mod_out.sem, 16)
            act.dma_start(mod_dram[rows:], mod_all[0:1, :, :].rearrange("b s d -> b (s d)")).then_inc(mod_out.sem, 16)
            act.wait_ge(mod_out.sem, 32)
            load_mod(0)
            load_g2(0)
            nc.scalar.activation(shared_parts[:, 0, :], shared_up[:, :], ACT.Copy).then_inc(shared_split.sem, 1)

            def cut_hi(turn, k):
                out = split_out[k % OUTS]
                act.wait_ge(raw_in[k].sem, 16 * (turn + 1))
                act.wait_ge(out.sem, out.credit + 16 * (CUTS // OUTS * turn + k // OUTS))
                nc.scalar.activation(up_exact[:, k % OUTS * SPLIT:(k % OUTS + 1) * SPLIT, 0, :], raw_up[:, k, :, :],
                                     ACT.Copy).then_inc(hi_done.sem, 1)

            row_stages(0, lambda p: None, cut_hi)
            take_live(0)
            first_tanhs(0)
            with act.Fori(0, rows - 1) as row:
                row_stages(row + 1, lambda p: experts(row, block_at(POINTS[p])),
                           lambda turn, k: experts(row, block_in_turn(turn, k)))
                act.wait_ge(e_up.sem, e_up.by(row))
                take_live(row + 1)
                first_tanhs(row + 1)
                take_sum(row)
                store(row)
                load_g2(row + 1)
            for k in range(2, RING):
                experts(rows - 1, block_at(k))
            with act.Fori(1, PAIRS // RING) as lap:
                for k in range(RING):
                    experts(rows - 1, block_in_lap(lap, k))
            experts(rows - 1, block_at(PAIRS))
            take_sum(rows - 1)
            store(rows - 1)
            act.wait_ge(x_in.sem, x_in.by(rows))
            act.wait_ge(mod_in.sem, mod_in.by(rows))
            act.wait_ge(o_out.sem, o_out.by(rows - 1))

        @block.vector
        def _(dve):
            def gate(row, e):
                n = INTER if e.pair is None else P
                if not (isinstance(e.q, int) and e.q < HRING):
                    dve.wait_ge(e_down.sem, e_down.by(row, e.q - HRING + 1))
                dve.wait_ge(e_tanh.sem, e_tanh.by(row, e.q + 1))
                nc.vector.scalar_tensor_tensor(out=e_h[0:n, e.h_slot, :], in0=e_th[e.two][0:n, :], scalar=1.0,
                                               in1=up_bank[e.two][0:n, :], op0=ALU.add, op1=ALU.mult)\
                    .then_inc(e_vd.sem, 1)

            def weigh(row, w):
                dve.wait_ge(e_vd.sem, e_vd.by(row, w.q + 1))
                dve.wait_ge(e_c.sem, e_c.by(row, w.q + 1))
                nc.vector.tensor_tensor(e_h[:, w.h_slot, :], e_h[:, w.h_slot, :], comb_bank[w.two][:, :],
                                        ALU.mult).then_inc(e_hd.sem, 1)

            def experts(row, e):
                if isinstance(e.q, int) and e.q == 0:
                    return
                if not (isinstance(e.q, int) and e.q == 1):
                    gate(row, e)
                weigh(row, e.before(1))

            def count_of(done, m):
                return done.by(m) if isinstance(m, int) else dve.snap(dve.to_reg(done.by(m)))

            def wait_apart(done, count):
                if not isinstance(count, int):
                    dve.wait_ge(prep.sem, N_PREP)
                dve.wait_ge(done.sem, count)

            def norm_stats(m, count, src, st, st_done, agg, agg_done, var, var_done):
                for t in range(TILES):
                    nc.vector.bn_stats(st[:, t, :], src[:, t, :]).then_inc(st_done.sem, 1)
                wait_apart(st_done, count)
                for t in range(TILES):
                    nc.vector.bn_aggr(agg[:, t, :], st[:, t, :]).then_inc(agg_done.sem, 1)
                dve.wait_ge(agg_done.sem, agg_done.by(m))
                nc.vector.tensor_scalar(var[:, :], agg[:, :, 1], EPS_LN, None, ALU.add).then_inc(var_done.sem, 1)

            def modulated(m, src, agg, rs, rs_done, scale, shift, mid, mid_done, dst, done):
                for t in range(TILES):
                    nc.vector.scalar_tensor_tensor(out=mid[:, t, :], in0=src[:, t, :], scalar=agg[:, t, 0:1],
                                                   in1=mod[:, scale, :], op0=ALU.subtract, op1=ALU.mult)\
                        .then_inc(mid_done.sem, 1)
                dve.wait_ge(mid_done.sem, mid_done.by(m))
                dve.wait_ge(rs_done.sem, rs_done.by(m))
                for t in range(TILES):
                    nc.vector.scalar_tensor_tensor(out=dst[:, t, :], in0=mid[:, t, :], scalar=rs[:, t:t + 1],
                                                   in1=mod[:, shift, :], op0=ALU.mult, op1=ALU.add)\
                        .then_inc(done.sem, 1)

            def scaled(dst, src, r, done):
                for t in range(TILES):
                    nc.vector.tensor_scalar(dst[:, t, :], src[:, t, :], r[:, t:t + 1], None, ALU.mult)\
                        .then_inc(done.sem, 1)

            def gated(th, src, dst, done):
                nc.vector.scalar_tensor_tensor(out=dst, in0=th, scalar=1.0, in1=src, op0=ALU.add, op1=ALU.mult)\
                    .then_inc(done.sem, 1)

            def convolve(m, h):
                src = M[1 + h]
                dve.wait_ge(in_mm.sem, in_mm.by(m, h + 1))
                nc.vector.tensor_scalar(conv[h][:, :], src[:, :], conv_w[:, h, TAPS - 1:TAPS],
                                        cols[:, CONV_B + h:CONV_B + h + 1], ALU.mult, ALU.add)\
                    .then_inc(conv_done.sem, 1)
                for back in range(1, TAPS):
                    dve.wait_ge(conv_done.sem, conv_done.by(m, TAPS * h + back))
                    nc.vector.scalar_tensor_tensor(out=conv[h][:, back:], in0=src[:, 0:SEQ - back],
                                                   scalar=conv_w[:, h, TAPS - 1 - back:TAPS - back],
                                                   in1=conv[h][:, back:], op0=ALU.mult, op1=ALU.add)\
                        .then_inc(conv_done.sem, 1)

            def thirds(m, src, rem, parts, done):
                nc.vector.tensor_copy(parts(0), src).then_inc(done.sem, 1)
                dve.wait_ge(done.sem, done.by(m, 1))
                nc.vector.tensor_tensor(rem, src, parts(0), ALU.subtract).then_inc(done.sem, 1)
                dve.wait_ge(done.sem, done.by(m, 2))
                nc.vector.tensor_copy(parts(1), rem).then_inc(done.sem, 1)
                dve.wait_ge(done.sem, done.by(m, 3))
                nc.vector.tensor_tensor(parts(2), rem, parts(1), ALU.subtract).then_inc(done.sem, 1)

            def norm_of_x(m, at):
                counts = {d: count_of(d, m) for d in (ln1_st, ln2_st, probs_done, top_done)}
                dve.wait_ge(x_in.sem, x_in.by(m))
                norm_stats(m, counts[ln1_st], x_tm, stats, ln1_st, mv, ln1_mv, var1, ln1_var)
                return counts

            def row_stages(m, counts, at, scan_experts):
                at("a2")
                dve.wait_ge(mod_in.sem, mod_in.by(m))
                modulated(m, x_tm, mv, rstd1, ln1_rs, SC1, SH1, hs_tm, hs_done, h_tm, h_done)
                at("a3")
                at("a4")
                dve.wait_ge(ss1_done.sem, ss1_done.by(m))
                nc.vector.tensor_scalar(ms1[:, :], ss1[:, :], 1.0 / DM, EPS_RMS, ALU.mult, ALU.add)\
                    .then_inc(ms1_done.sem, 1)
                at("a5")
                at("a6")
                dve.wait_ge(r1_done.sem, r1_done.by(m))
                scaled(hn_tm, h_tm, r1, hn_done)
                at("a7")
                at("a8")
                convolve(m, 0)
                at("a9")
                convolve(m, 1)
                at("a10")
                for h in range(HALVES):
                    dve.wait_ge(convth_done.sem, convth_done.by(m, h + 1))
                    gated(conv_th[h][:, :], conv[h][:, :], x2[h][:, :], x2_done)
                dve.wait_ge(zth_done.sem, zth_done.by(m, 1))
                gated(z_th[0][:, :], M[0][:, :], z2[0][:, :], z2_done)
                at("a11")
                dve.wait_ge(zth_done.sem, zth_done.by(m, 2))
                gated(z_th[1][:, :], M[1][:, :], z2[1][:, :], z2_done)
                at("a12")
                at("a13")
                dve.wait_ge(sq3_done.sem, sq3_done.by(m))
                nc.vector.tensor_reduce(ss3[:, :, 0], proj_sq[:, :, 0:RANK], AX_X, ALU.add).then_inc(ss3_done.sem, 1)
                nc.vector.tensor_reduce(ss3[:, :, 1:3], proj_sq[:, :, RANK:].rearrange("p t (k n) -> p t k n", k=2),
                                        AX_X, ALU.add).then_inc(ss3_done.sem, 1)
                dve.wait_ge(ss3_done.sem, ss3_done.by(m))
                nc.vector.tensor_scalar(ms3[:, :, 0], ss3[:, :, 0], 1.0 / RANK, EPS_RMS, ALU.mult, ALU.add)\
                    .then_inc(ms3_done.sem, 1)
                nc.vector.tensor_scalar(ms3[:, :, 1:3], ss3[:, :, 1:3], 1.0 / NS, EPS_RMS, ALU.mult, ALU.add)\
                    .then_inc(ms3_done.sem, 1)
                for p in ("a14", "a15", "a16"):
                    at(p)
                dve.wait_ge(r3_done.sem, r3_done.by(m))
                proj = M[2][:, 0:TILES * PROJ].rearrange("p (t n) -> p t n", t=TILES)
                nc.vector.tensor_tensor(dtn_tm[:, :, :], proj[:, :, 0:RANK],
                                        r3[:, :, 0:1].to_broadcast([P, TILES, RANK]), ALU.mult).then_inc(dtn_done.sem, 1)
                nc.vector.tensor_tensor(bcn[:, :, :].rearrange("p t (k n) -> p t k n", k=2),
                                        proj[:, :, RANK:].rearrange("p t (k n) -> p t k n", k=2),
                                        r3[:, :, 1:3].rearrange("p t (k o) -> p t k o", o=1)
                                        .to_broadcast([P, TILES, 2, NS]), ALU.mult).then_inc(bcn_done.sem, 1)
                dve.wait_ge(bcn_done.sem, bcn_done.by(m))
                nc.vector.tensor_tensor(bcs[:, :, :], bcn[:, :, :],
                                        bc_w[:, :, :].rearrange("p (o k) n -> p o (k n)", o=1)
                                        .to_broadcast([P, TILES, 2 * NS]), ALU.mult).then_inc(bcs_done.sem, 1)
                dve.wait_ge(bcs_done.sem, bcs_done.by(m))
                thirds(m, bcs[:, :, :], bc_rem[:, :, :], lambda i: bc_parts[:, :, i, :], bcp_done)
                at("a17")
                for h in range(HALVES):
                    dve.wait_ge(dt_mm.sem, dt_mm.by(m, h + 1))
                    nc.vector.tensor_scalar(dt_min[h][:, :], M[2 * (1 - h)][:, :], cols[:, DT_B + h:DT_B + h + 1], 30.0,
                                            ALU.add, ALU.min).then_inc(dtmin_done.sem, 1)
                at("a18")
                for h in range(HALVES):
                    dve.wait_ge(dtln_done.sem, dtln_done.by(m, h + 1))
                    nc.vector.scalar_tensor_tensor(out=dt[h][:, :], in0=M[2 * (1 - h)][:, :],
                                                   scalar=cols[:, DT_B + h:DT_B + h + 1], in1=dt_ln[h][:, :],
                                                   op0=ALU.add, op1=ALU.max).then_inc(dt_done.sem, 1)
                for h in range(HALVES):
                    dve.wait_ge(dt_done.sem, dt_done.by(m, h + 1))
                    nc.vector.tensor_tensor(dtx[h][:, :], dt[h][:, :], x2[h][:, :], ALU.mult).then_inc(dtx_done.sem, 1)
                at("a19")
                at("a20")
                with dve.Fori(0, TURNS) as turn:
                    dve.wait_ge(dtx_done.sem, dtx_done.by(m))
                    for s in range(STATES_PER_TURN):
                        n = STATES_PER_TURN * turn + s
                        cut = TURN_SHARE[s], TURN_SHARE[s] + 1, TURN_SHARE[s + 1]
                        dve.wait_ge(b_mm.sem, b_mm.by(m, n + 1))
                        dve.wait_ge(scan_done.sem, scan_done.by(m, HALVES * n))
                        for h in range(HALVES):
                            nc.vector.tensor_tensor(dbx[h][:, :], dtx[h][:, :], b_bank[:, :], ALU.mult)\
                                .then_inc(dbx_done.sem, 1)
                        for h in range(HALVES):
                            k = HALVES * n + h
                            dve.wait_ge(dbx_done.sem, dbx_done.by(m, k + 1))
                            dve.wait_ge(da_done.sem, da_done.by(m, k + 1))
                            dve.wait_ge(read_done.sem, read_done.by(m, k - 3))
                            nc.vector.tensor_tensor_scan(state[s % 2][h][:, :], da_bank[:, :], dbx[h][:, :], 0.0,
                                                         ALU.mult, ALU.add).then_inc(scan_done.sem, 1)
                            for b in range(cut[h], cut[h + 1]):
                                scan_experts(turn, b)
                at("c1")
                at("c2")
                for h in range(HALVES):
                    dve.wait_ge(y_done.sem, y_done.by(m, 2 * NS - 1 + h))
                    nc.vector.tensor_tensor(yz[h][:, :], y[h][:, :], z2[h][:, :], ALU.mult).then_inc(yz_done.sem, 1)
                dve.wait_ge(outp_mm.sem, outp_mm.by(m))
                nc.vector.tensor_tensor(hid_tm[:, :, :], M[0][:, :].rearrange("p (t d) -> p t d", t=TILES),
                                        h_tm[:, :, :], ALU.add).then_inc(hid_done.sem, 1)
                at("c3")
                dve.wait_ge(ss2_done.sem, ss2_done.by(m))
                nc.vector.tensor_scalar(ms2[:, :], ss2[:, :], 1.0 / DM, EPS_RMS, ALU.mult, ALU.add)\
                    .then_inc(ms2_done.sem, 1)
                at("c4")
                dve.wait_ge(r2_done.sem, r2_done.by(m))
                scaled(hn_tm, hid_tm, r2, hn2_done)
                at("c5")
                at("c6")
                for f in range(FB):
                    g, u = FFN_BANKS[f]
                    dve.wait_ge(fth_done.sem, fth_done.by(m, f + 1))
                    gated(f_th[f % 2][:, :], M[g][:, :], f_v[f % 2][:, :], fv_done)
                    dve.wait_ge(fv_done.sem, fv_done.by(m, f + 1))
                    dve.wait_ge(fu_mm.sem, fu_mm.by(m, f + 1))
                    nc.vector.tensor_tensor(f_act[f][:, :], f_v[f % 2][:, :], M[u][:, :], ALU.mult)\
                        .then_inc(fa_done.sem, 1)
                    at(f"c{7 + f}")
                dve.wait_ge(down_mm.sem, down_mm.by(m))
                nc.vector.tensor_tensor(att_tm[:, :, :], M[1][:, :].rearrange("p (t d) -> p t d", t=TILES),
                                        hid_tm[:, :, :], ALU.add).then_inc(att_done.sem, 1)
                dve.wait_ge(att_done.sem, att_done.by(m))
                nc.vector.tensor_tensor(gat_tm[:, :, :], att_tm[:, :, :],
                                        mod[:, G1:G1 + 1, :].to_broadcast([P, TILES, DM]), ALU.mult)\
                    .then_inc(gat_done.sem, 1)
                at("c11")
                dve.wait_ge(gat_done.sem, gat_done.by(m))
                nc.vector.tensor_tensor(x1_tm[:, :, :], gat_tm[:, :, :], x_tm[:, :, :], ALU.add).then_inc(x1_done.sem, 1)
                at("c12")
                dve.wait_ge(x1_done.sem, x1_done.by(m))
                norm_stats(m, counts[ln2_st], x1_tm, stats2, ln2_st, mv2, ln2_mv, var2, ln2_var)
                at("c13")
                modulated(m, x1_tm, mv2, rstd2, ln2_rs, SC2, SH2, hs2_tm, hs2_done, h2_tm, h2_done)
                for p in ("c14", "c15", "c16"):
                    at(p)
                dve.wait_ge(rt_mm.sem, rt_mm.by(m))
                nc.vector.tensor_tensor(logits[:, 0:3, :], M[1][:, 0:3 * EXPERTS].rearrange("p (t e) -> p t e", t=3),
                                        bias_w[:, :].rearrange("p (o e) -> p o e", o=1)
                                        .to_broadcast([P, 3, EXPERTS]), ALU.add).then_inc(lg_done.sem, 1)
                nc.vector.tensor_tensor(logits[:, 3, :], M[2][:, 0:EXPERTS], bias_w[:, :], ALU.add)\
                    .then_inc(lg_done.sem, 1)
                at("c17")
                dve.wait_ge(lexp_done.sem, lexp_done.by(m))
                nc.vector.tensor_scalar(l_one[:, :, :], l_exp[:, :, :], 1.0, None, ALU.add).then_inc(lone_done.sem, 1)
                dve.wait_ge(lone_done.sem, lone_done.by(m))

                for t in range(TILES):
                    nc.vector.reciprocal(probs[:, t, :], l_one[:, t, :]).then_inc(probs_done.sem, 1)
                    if t == 1:
                        at("c18")
                wait_apart(probs_done, counts[probs_done])
                for t in range(TILES):
                    nc.vector.max(top[:, t, :], probs[:, t, :]).then_inc(top_done.sem, 1)
                at("c19")
                wait_apart(top_done, counts[top_done])
                for t in range(TILES):
                    nc.vector.match_replace(rest[:, t, :], in_to_replace=top[:, t, :], in_values=probs[:, t, :],
                                            imm_value=-1.0).then_inc(rest_done.sem, 1)
                at("c20")
                dve.wait_ge(rest_done.sem, rest_done.by(m))
                for t in range(TILES):
                    nc.vector.scalar_tensor_tensor(out=chosen[:, t, :], in0=rest[:, t, :], scalar=0.0,
                                                   in1=probs[:, t, :], op0=ALU.max, op1=ALU.subtract)\
                        .then_inc(chosen_done.sem, 1)
                at("c21")
                dve.wait_ge(live_h2.sem, live_h2.by(m))
                nc.vector.tensor_tensor(h2_live[1][:, :], h2_cm[:, :], h2_live[0][:, :].bitcast(F32), ALU.subtract)\
                    .then_inc(live_lo.sem, 1)
                nc.vector.tensor_reduce(top_sum[:, :], top[:, :, :], AX_X, ALU.add).then_inc(tops_done.sem, 1)
                dve.wait_ge(tops_done.sem, tops_done.by(m, 1))
                nc.vector.tensor_scalar(top_inv[:, :], top_sum[:, :], 1e-9, None, ALU.add).then_inc(tops_done.sem, 1)
                dve.wait_ge(tops_done.sem, tops_done.by(m, 2))
                nc.vector.reciprocal(top_fac[:, :], top_inv[:, :]).then_inc(tops_done.sem, 1)
                dve.wait_ge(tops_done.sem, tops_done.by(m, 3))
                dve.wait_ge(chosen_done.sem, chosen_done.by(m))
                for t in range(TILES):
                    nc.vector.tensor_scalar(comb[:, t, :], chosen[:, t, :], top_fac[:, t:t + 1], -SCALE / 2,
                                            ALU.mult, ALU.mult).then_inc(comb_done.sem, 1)
                dve.wait_ge(comb_done.sem, comb_done.by(m))
                as_groups = "p t (g e) -> p t g e"
                thirds(m, comb[:, :, :].rearrange(as_groups, g=GROUPS), comb_rem[:, :, :].rearrange(as_groups, g=GROUPS),
                       lambda i: comb_parts[:, :, :, i, :], combp_done)

            def take_live(m):
                gate(m, block_at(0))
                gate(m, block_at(1))
                dve.wait_ge(combT_mm.sem, combT_mm.by(m))
                for b in range(3):
                    g = min(2, GROUPS - 2 * b)
                    nc.vector.tensor_copy(comb_live[:, 2 * b:2 * b + g, :],
                                          Mb[b][0:96, 0:g * SEQ].rearrange("p (g t) -> p g t", g=g))\
                        .then_inc(live_comb.sem, 1)

            def take_residual(m):
                nc.vector.tensor_copy(x1_live[:, :, :], x1_tm[:, :, :]).then_inc(live_x1.sem, 1)

            def finish_row(row, first):
                dve.wait_ge(g2_in.sem, g2_in.by(row))
                dve.wait_ge(eT_mm.sem, eT_mm.by(row))
                nc.vector.tensor_tensor(e_gat[:, :, :], M[0][:, :].rearrange("p (t d) -> p t d", t=TILES),
                                        g2_live[:, :].rearrange("p (o d) -> p o d", o=1)
                                        .to_broadcast([P, TILES, DM]), ALU.mult).then_inc(eg_done.sem, 1)
                dve.wait_ge(eg_done.sem, eg_done.by(row))
                dve.wait_ge(o_out.sem, o_out.by(row, 0))
                nc.vector.tensor_tensor(o_tm[:, :, :], e_gat[:, :, :], x1_live[:, :, :], ALU.add)\
                    .then_inc(o_done.sem, 1)

            counts = norm_of_x(0, lambda p: None)
            dve.wait_ge(c_tanh.sem, 1)
            gated(c_th[:, :], c_cm[:, :], c_sl[:, :], c_silu)
            dve.wait_ge(mod_mm.sem, 1)
            flat = mod_all[:, :, :].rearrange("b s d -> b (s d)")
            nc.vector.tensor_scalar(flat[:, 0:512], M[0][0:rows, :], 0.5, None, ALU.mult).then_inc(mod_half.sem, 1)
            nc.vector.tensor_scalar(flat[:, 512:768], M[1][0:rows, 0:256], 0.5, None, ALU.mult).then_inc(mod_half.sem, 1)
            dve.wait_ge(mod_half.sem, 2)
            nc.vector.tensor_scalar(mod_all[:, SC1::3, :], mod_all[:, SC1::3, :], 1.0, None, ALU.add)\
                .then_inc(mod_done.sem, 1)
            for i, slot in enumerate((G1, G2)):
                nc.vector.scalar_tensor_tensor(out=mod_abs[:, i, :], in0=mod_all[:, slot, :], scalar=-1.0,
                                               in1=mod_all[:, slot, :], op0=ALU.mult, op1=ALU.max)\
                    .then_inc(mod_raw.sem, 1)
            nc.vector.tensor_scalar(mod_sgn[:, :, :], mod_all[:, G1::3, :], 0.0, 2.0, ALU.is_ge, ALU.mult)\
                .then_inc(mod_raw.sem, 1)
            dve.wait_ge(mod_raw.sem, 3)
            nc.vector.tensor_scalar(mod_abs[:, :, :], mod_abs[:, :, :], 0.25, None, ALU.max).then_inc(mod_raw.sem, 1)
            dve.wait_ge(mod_raw.sem, 4)
            for i, slot in enumerate((G1, G2)):
                nc.vector.scalar_tensor_tensor(out=mod_all[:, slot, :], in0=mod_sgn[:, i, :], scalar=-1.0,
                                               in1=mod_abs[:, i, :], op0=ALU.add, op1=ALU.mult)\
                    .then_inc(mod_done.sem, 1)
            dve.wait_ge(c_loaded[1].sem, N_LOADS[1])
            dve.wait_ge(c_loaded[2].sem, N_LOADS[2])
            dve.wait_ge(a_exp.sem, 1)
            for t, scale in ((in_w[:, :], cols[:, IN_LN:IN_LN + 1]), (gate_w[:, :], cols[:, PRE_LN:PRE_LN + 1]),
                             (up_w[:, :], cols[:, PRE_LN:PRE_LN + 1]),
                             (dtproj_w[:, :], cols[0:RANK, DT_LN:DT_LN + 1]), (xproj_w[:, :, :], 0.5),
                             (out_w[:, :, :], 0.5), (down_w[:, :, :], 0.5), (shared_down[:, :], 0.5),
                             (bc_w[:, 0, :], 0.5), (cols[:, D_HALF:D_HALF + 2], 0.5), (a_neg[:, :, :], -1.0)):
                nc.vector.tensor_scalar(t, t, scale, None, ALU.mult).then_inc(prep.sem, 1)
            dve.wait_ge(prep.sem, N_PREP)
            dve.wait_ge(shared_split.sem, 1)
            nc.vector.tensor_tensor(shared_parts[:, 1, :], shared_up[:, :], shared_parts[:, 0, :].bitcast(F32), ALU.subtract)\
                .then_inc(shared_split.sem, 1)

            def cut_lo(turn, k):
                dve.wait_ge(hi_done.sem, CUTS * turn + k + 1)
                at = slice(k % OUTS * SPLIT, (k % OUTS + 1) * SPLIT)
                nc.vector.tensor_tensor(up_exact[:, at, 1, :], raw_up[:, k, :, :], up_ring[:, at, 0, :], ALU.subtract)\
                    .then_inc(lo_done.sem, 1)

            row_stages(0, counts, lambda p: None, cut_lo)
            take_live(0)
            take_residual(0)
            with dve.Fori(0, rows - 1) as row:
                def at(p):
                    experts(row, block_at(POINTS[p]))
                counts = norm_of_x(row + 1, at)
                row_stages(row + 1, counts, at,
                           lambda turn, k: experts(row, block_in_turn(turn, k)))
                dve.wait_ge(e_c.sem, e_c.by(row))
                take_live(row + 1)
                finish_row(row, False)
                dve.wait_ge(o_done.sem, o_done.by(row))
                take_residual(row + 1)
            for k in range(RING):
                experts(rows - 1, block_at(k))
            with dve.Fori(1, PAIRS // RING) as lap:
                for k in range(RING):
                    experts(rows - 1, block_in_lap(lap, k))
            experts(rows - 1, block_at(PAIRS))
            finish_row(rows - 1, True)


def kernel(**inputs):
    import numpy as np
    import concourse.bacc as bacc
    from concourse.bass_utils import run_bass_kernel_spmd as run

    i = {k.replace("L0_", ""): np.asarray(v) for k, v in inputs.items()}
    rows = i["attn_hidden_states"].shape[0]

    def lay(a):
        return np.ascontiguousarray(a)

    up = i["ffn_w_gate"].reshape(GROUPS, GP, 2, INTER, DM).transpose(1, 0, 4, 2, 3).reshape(PAIRS, P, P)
    down = i["ffn_w_down"].reshape(GROUPS, GP, 2, DM, INTER).transpose(1, 0, 2, 4, 3).reshape(PAIRS, P, P)
    cols = np.zeros((P, 9), np.float32)
    for at, name in ((0, "attn_conv_b"), (2, "attn_dt_proj_b"), (4, "attn_D_skip"), (6, "attn_input_ln_w"),
                     (7, "attn_pre_moe_ln_w")):
        v = i[name].reshape(-1, P)
        cols[:, at:at + len(v)] = v.T
    cols[:RANK, 8] = i["attn_dt_ln_w"]
    arrays = {
        "x": np.concatenate([i["attn_hidden_states"], np.zeros((1, SEQ, DM), np.float32)]), "in_w": lay(i["attn_in_proj_w"]), "conv_w": lay(i["attn_conv_w"]),
        "cols": cols, "xproj_w": lay(i["attn_x_proj_w"]), "dtproj_w": lay(i["attn_dt_proj_w"]),
        "b_ln": lay(i["attn_b_ln_w"]),
        "c_ln": lay(i["attn_c_ln_w"]), "a_log": lay(i["attn_A_log"]),
        "out_w": lay(i["attn_out_proj_w"]),
        "gate_w": lay(i["attn_gate_w"]), "up_w": lay(i["attn_up_w"]), "down_w": lay(i["attn_down_w"]),
        "router_cm": lay(i["ffn_router_w"].T), "bias": lay(i["ffn_expert_bias"]),
        "up": lay(up), "down": lay(down),
        "shared_up": lay(i["ffn_w_gate_shared"].T), "shared_down": lay(i["ffn_w_down_shared"].T),
        "c_cm": lay(i["c"].T), "mod_w": lay(i["wmod"]),
    }
    nc = bacc.Bacc("TRN2", target_bir_lowering=False, num_devices=1)
    args = {n: nc.dram_tensor(f"in_{n}", a.shape, F32, kind="ExternalInput").ap() for n, a in arrays.items()}
    out = nc.dram_tensor("out_0", (rows, SEQ, DM), F32, kind="ExternalOutput").ap()
    build(nc, args, out, rows)
    r = run(nc, [{f"in_{n}": a for n, a in arrays.items()}], core_ids=[0])
    return r.results[0]["out_0"]
```

```python
from contextlib import ExitStack

import concourse.bass as bass
from concourse import mybir

ALU = mybir.AluOpType
ACT = mybir.ActivationFunctionType
BF16 = mybir.dt.bfloat16
F32 = mybir.dt.float32
F32R = mybir.dt.float32r
AX_X = mybir.AxisListType.X

P = 128
DM = 128
DI = 256
HALVES = DI // P
NS = 16
RANK = 64
TAPS = 4
FF = 512
FB = FF // P
EXPERTS = 160
TOPK = 8
INTER = 64
SCALE = 2.5
PROJ = RANK + 2 * NS
SEQ = 512
TILES = SEQ // P
TAKEN = -3e38
EPS_LN = 1e-5
EPS_RMS = 1e-6

PAIRS = EXPERTS // 2
GROUPS = EXPERTS // 32
GP = 16
RING = 10
HRING = 5
BLOCKS = PAIRS + 1
LAG = 3
LOOP_PAIRS = 8
BEFORE = 4
STATES_PER_TURN = 4
TURNS = NS // STATES_PER_TURN
PER_TURN = LOOP_PAIRS * GROUPS // TURNS
FIRST_LOOP = BEFORE * GROUPS
FIRST_AFTER = FIRST_LOOP + LOOP_PAIRS * GROUPS
SPLIT = 2
CUTS = PAIRS // SPLIT
SLOTS = RING // SPLIT
TURN_SHARE = [0, 3, 5, 8, 10]
FFN_BANKS = [(0, 2), (1, 0), (2, 1), (0, 2)]
assert PER_TURN == RING and RING % 2 == 0 and RING % HRING == 0 and FIRST_LOOP % HRING == 0
assert CUTS % SLOTS == 0 and SLOTS * SPLIT * P <= HRING * SEQ

A_POINTS = {f"a{i + 1}": i for i in range(FIRST_LOOP)}
C_POINTS = {f"c{i + 1}": FIRST_AFTER + i for i in range(BLOCKS - FIRST_AFTER)}
POINTS = {**A_POINTS, **C_POINTS}
EARLY = {"w9": A_POINTS["a9"], "w18": A_POINTS["a18"], "wc12": C_POINTS["c12"], "wc13": C_POINTS["c13"]}
POOL_IN_TURN, POOL_STATE = 3, 1
POOL_WEIGHS = range(PAIRS - 6, PAIRS)


class Block:

    def __init__(self, q, slot, pair, lap):
        self.q, self.slot, self.pair, self.lap = q, slot, pair, lap
        self.group, self.h_slot, self.two = slot % GROUPS, slot % HRING, slot % 2

    def before(self, n):
        return Block(self.q - n, (self.slot - n) % RING, None, None)


def block_at(q):
    return Block(q, q % RING, q // GROUPS if q < PAIRS else None, q // RING)


def block_in_turn(turn, k):
    at = FIRST_LOOP + k
    return Block(PER_TURN * turn + at, at % RING, PER_TURN // GROUPS * turn + at // GROUPS, turn + at // RING)


def block_in_lap(lap, k):
    return Block(RING * lap + k, k, RING // GROUPS * lap + k // GROUPS, lap)


class Signal:

    def __init__(self, sem, per_row, credit):
        self.sem, self.per_row, self.credit = sem, per_row, credit

    def by(self, row, k=None):
        return row * self.per_row + (self.per_row if k is None else k) + self.credit


def build(nc, A, out, rows):
    with ExitStack() as ctx:
        def sb(name, shape, dt=F32):
            return ctx.enter_context(nc.sbuf_tensor(name, shape, dt))

        def bank(name, dt=F32):
            return ctx.enter_context(nc.psum_tensor(name, [P, 2048 // (4 if dt == F32 else 2)], dt))

        def sig(name, per_row=1, credit=0):
            return Signal(ctx.enter_context(nc.semaphore(name)), per_row, credit)

        ident = sb("ident", [P, P])
        identb = sb("identb", [P, P], BF16)
        pair_sel = sb("pair_sel", [96, GP, P], BF16)
        row_sel = sb("row_sel", [96, 2 * NS, P], BF16)
        neg_half = sb("neg_half", [P, 16])
        raised = sb("raised", [1, 10 + SLOTS])
        in_w = sb("in_w", [P, 2 * DI])
        conv_w = sb("conv_w", [P, HALVES, TAPS])
        cols = sb("cols", [P, 9])
        xproj_w = sb("xproj_w", [P, HALVES, PROJ])
        dtproj_w = sb("dtproj_w", [RANK, DI])
        a_neg = sb("a_neg", [P, HALVES, NS])
        out_w = sb("out_w", [P, HALVES, DM])
        gate_w = sb("gate_w", [P, FF])
        up_w = sb("up_w", [P, FF])
        down_w = sb("down_w", [P, FB, DM])
        bc_w = sb("bc_w", [P, 2, NS])
        bias_w = sb("bias_w", [P, EXPERTS])
        router_w = sb("router_w", [P, EXPERTS])
        shared_up = sb("shared_up", [P, INTER])
        shared_parts = sb("shared_parts", [P, 2, INTER], F32R)
        shared_down = sb("shared_down", [INTER, DM])
        c_cm = sb("c_cm", [P, rows])
        c_th = sb("c_th", [P, rows])
        c_sl = sb("c_sl", [P, rows])
        mod_w = sb("mod_w", [P, 6 * DM])
        mod_all = sb("mod_all", [rows, 6, DM])
        mod_abs = sb("mod_abs", [rows, 2, DM])
        mod_sgn = sb("mod_sgn", [rows, 2, DM])
        CONV_B, DT_B, D_HALF, IN_LN, PRE_LN, DT_LN = 0, 2, 4, 6, 7, 8

        mod = sb("mod", [P, 5, DM])
        SH1, SC1, G1, SH2, SC2, G2 = range(6)
        x_tm = sb("x_tm", [P, TILES, DM])
        stats = sb("stats", [P, TILES, 6])
        mv = sb("mv", [P, TILES, 2])
        var1 = sb("var1", [P, TILES])
        rstd1 = sb("rstd1", [P, TILES])
        hs_tm = sb("hs_tm", [P, TILES, DM])
        h_tm = sb("h_tm", [P, TILES, DM])
        junk = sb("junk", [P, TILES, DM])
        ss1 = sb("ss1", [P, TILES])
        ms1 = sb("ms1", [P, TILES])
        r1 = sb("r1", [P, TILES])
        hn_tm = sb("hn_tm", [P, TILES, DM])
        h_cm = sb("h_cm", [P, SEQ])
        conv = [sb(f"conv{h}", [P, SEQ]) for h in range(HALVES)]
        conv_th = [sb(f"conv_th{h}", [P, SEQ]) for h in range(HALVES)]
        x2 = [sb(f"x2_{h}", [P, SEQ]) for h in range(HALVES)]
        z_th = [sb(f"z_th{h}", [P, SEQ]) for h in range(HALVES)]
        z2 = [sb(f"z2_{h}", [P, SEQ]) for h in range(HALVES)]
        proj_sq = sb("proj_sq", [P, TILES, PROJ])
        ss3 = sb("ss3", [P, TILES, 3])
        ms3 = sb("ms3", [P, TILES, 3])
        r3 = sb("r3", [P, TILES, 3])
        dtn_tm = sb("dtn_tm", [P, TILES, RANK])
        bcn = sb("bcn", [P, TILES, 2 * NS])
        bcs = sb("bcs", [P, TILES, 2 * NS])
        bc_rem = sb("bc_rem", [P, TILES, 2 * NS])
        bc_parts = sb("bc_parts", [P, TILES, 3, 2 * NS], BF16)
        dtn_cm = sb("dtn_cm", [RANK, SEQ])
        bc_cm = sb("bc_cm", [96, SEQ], BF16)
        dt_min = conv
        dt_exp = conv_th
        dt_ln = z_th
        dt = [sb(f"dt{h}", [P, SEQ]) for h in range(HALVES)]
        dtx = [sb(f"dtx{h}", [P, SEQ]) for h in range(HALVES)]
        c_sb = [sb(f"c_sb{i}", [P, SEQ]) for i in range(2)]
        dbx = [sb(f"dbx{h}", [P, SEQ]) for h in range(HALVES)]
        state = [[sb(f"state{i}{h}", [P, SEQ]) for h in range(HALVES)] for i in range(2)]
        read = [sb(f"read{h}", [P, SEQ]) for h in range(HALVES)]
        y = [sb(f"y{h}", [P, SEQ]) for h in range(HALVES)]
        yz = [sb(f"yz{h}", [P, SEQ]) for h in range(HALVES)]
        hid_tm = sb("hid_tm", [P, TILES, DM])
        ss2 = sb("ss2", [P, TILES])
        ms2 = sb("ms2", [P, TILES])
        r2 = sb("r2", [P, TILES])
        f_th, f_v, f_act = read, dbx, dt + dtx
        att_tm = sb("att_tm", [P, TILES, DM])
        gat_tm = sb("gat_tm", [P, TILES, DM])
        x1_tm = sb("x1_tm", [P, TILES, DM])
        stats2 = sb("stats2", [P, TILES, 6])
        mv2 = sb("mv2", [P, TILES, 2])
        var2 = sb("var2", [P, TILES])
        rstd2 = sb("rstd2", [P, TILES])
        hs2_tm = hs_tm
        h2_tm = sb("h2_tm", [P, TILES, DM])
        h2_cm = sb("h2_cm", [P, SEQ])
        logits = sb("logits", [P, TILES, EXPERTS])
        l_exp = sb("l_exp", [P, TILES, EXPERTS])
        minus_u = sb("minus_u", [P, TILES, EXPERTS])
        probs = sb("probs", [P, TILES, EXPERTS])
        top = sb("top", [P, TILES, TOPK])
        rest = sb("rest", [P, TILES, EXPERTS])
        chosen = sb("chosen", [P, TILES, EXPERTS])
        top_prob = sb("top_prob", [P, TILES, TOPK])
        top_sum = sb("top_sum", [P, TILES])
        top_inv = sb("top_inv", [P, TILES])
        top_fac = sb("top_fac", [P, TILES])
        comb = sb("comb", [P, TILES, EXPERTS])
        comb_rem = sb("comb_rem", [P, TILES, EXPERTS])
        comb_parts = sb("comb_parts", [P, TILES, GROUPS, 3, 32], BF16)

        h2_live = [sb(f"h2_live{i}", [P, SEQ], F32R) for i in range(2)]
        comb_live = sb("comb_live", [96, GROUPS, SEQ], BF16)
        x1_live = sb("x1_live", [P, TILES, DM])
        g2_live = sb("g2_live", [P, DM])
        up_ring = sb("up_ring", [P, RING, 2, P])
        up_exact = up_ring[:, :, :, :].bitcast(F32R)
        down_ring = sb("down_ring", [P, RING, P])
        comb_sb = [sb(f"comb_sb{i}", [P, SEQ]) for i in range(2)]
        e_th = [sb(f"e_th{i}", [P, SEQ]) for i in range(2)]
        e_h = sb("e_h", [P, HRING, SEQ])
        e_out = sb("e_out", [P, SEQ])
        raw_up = e_h[:, :, :].rearrange("p h s -> p (h s)").rearrange("p (k i n) -> p k i n", i=SPLIT, n=P)
        e_gat = sb("e_gat", [P, TILES, DM])
        o_tm = sb("o_tm", [P, TILES, DM])

        up_bank = [bank("up_bank0"), bank("up_bank1")]
        comb_bank = [bank("comb_bank0"), bank("comb_bank1")]
        acc_bank = bank("acc_bank")
        M = [bank("m0"), bank("m1"), bank("m2")]
        b_bank, c_bank, da_bank = M
        Mb = [b[:, :].bitcast(BF16) for b in M]

        c_loaded = [sig(f"c_loaded{i}") for i in range(3)]
        ident_zero, ident_done = sig("ident_zero"), sig("ident_done")
        sel_done, sel_copied = sig("sel_done"), sig("sel_copied")
        prep = sig("prep")
        c_tanh, c_silu, mod_mm, mod_raw, mod_half, mod_done, mod_out = (
            sig(n) for n in ("c_tanh", "c_silu", "mod_mm", "mod_raw", "mod_half", "mod_done", "mod_out"))
        a_exp = sig("a_exp")
        x_in, mod_in, g2_in = sig("x_in", 16), sig("mod_in", 16), sig("g2_in", 16)
        ln1_st, ln1_mv, ln1_var, ln1_rs = sig("ln1_st", 4), sig("ln1_mv", 4), sig("ln1_var"), sig("ln1_rs")
        hs_done, h_done = sig("hs_done", 4), sig("h_done", 4)
        ss1_done, ms1_done, r1_done, hn_done = sig("ss1_done", 4), sig("ms1_done"), sig("r1_done"), sig("hn_done", 4)
        hT_mm, hT_done = sig("hT_mm"), sig("hT_done")
        in_mm = sig("in_mm", 4)
        conv_done = sig("conv_done", 2 * TAPS)
        convth_done, x2_done = sig("convth_done", 2), sig("x2_done", 2)
        zth_done, z2_done = sig("zth_done", 2), sig("z2_done", 2)
        proj_mm, sq3_done, ss3_done, ms3_done, r3_done = (
            sig("proj_mm"), sig("sq3_done"), sig("ss3_done", 2), sig("ms3_done", 2), sig("r3_done", 2))
        dtn_done, bcn_done, bcs_done, bcp_done = sig("dtn_done"), sig("bcn_done"), sig("bcs_done"), sig("bcp_done", 4)
        dtT_mm, bcT_mm, dtT_done, bcT_done = sig("dtT_mm"), sig("bcT_mm"), sig("dtT_done"), sig("bcT_done")
        dt_mm, dtmin_done, dtexp_done, dtln_done, dt_done = (
            sig("dt_mm", 2), sig("dtmin_done", 2), sig("dtexp_done", 2), sig("dtln_done", 2), sig("dt_done", 2))
        dtx_done, y0_done = sig("dtx_done", 2), sig("y0_done", 2)
        b_mm, cn_mm, c_copied = sig("b_mm", NS), sig("cn_mm", NS), sig("c_copied", NS, credit=1)
        da_done, dbx_done, scan_done = sig("da_done", 2 * NS), sig("dbx_done", 2 * NS, credit=1), sig("scan_done", 2 * NS, credit=2)
        read_done, y_done = sig("read_done", 2 * NS, credit=4), sig("y_done", 2 * NS, credit=2)
        first_read, first_y = sig("first_read", NS, credit=2), sig("first_y", NS, credit=1)
        yz_done, outp_mm, hid_done = sig("yz_done", 2), sig("outp_mm"), sig("hid_done")
        ss2_done, ms2_done, r2_done, hn2_done = sig("ss2_done", 4), sig("ms2_done"), sig("r2_done"), sig("hn2_done", 4)
        hT2_mm, hT2_done = sig("hT2_mm"), sig("hT2_done")
        fg_mm, fu_mm, fth_done, fv_done, fa_done = (
            sig("fg_mm", FB), sig("fu_mm", FB), sig("fth_done", FB), sig("fv_done", FB), sig("fa_done", FB))
        down_mm, att_done, gat_done, x1_done = sig("down_mm"), sig("att_done"), sig("gat_done"), sig("x1_done")
        ln2_st, ln2_mv, ln2_var, ln2_rs = sig("ln2_st", 4), sig("ln2_mv", 4), sig("ln2_var"), sig("ln2_rs")
        hs2_done, h2_done = sig("hs2_done", 4), sig("h2_done", 4)
        h2T_mm, h2T_done = sig("h2T_mm"), sig("h2T_done")
        rt_mm, lg_done, lexp_done, lone_done, probs_done = (
            sig("rt_mm"), sig("lg_done", 2), sig("lexp_done"), sig("lone_done"), sig("probs_done"))
        top_done, rest_done, chosen_done = sig("top_done", 4), sig("rest_done", 4), sig("chosen_done")
        topp_done = sig("topp_done")
        tops_done, comb_done, combp_done = sig("tops_done", 3), sig("comb_done", 4), sig("combp_done", 4)
        combT_mm = sig("combT_mm", 3)
        live_h2, live_comb, live_x1 = sig("live_h2"), sig("live_comb", 3), sig("live_x1")
        raw_in = [sig(f"raw_in{k}") for k in range(SLOTS)]
        hi_done, lo_done = sig("hi_done"), sig("lo_done")
        split_out = [sig(f"split_out{k}", credit=16) for k in range(SLOTS)]
        shared_split, live_lo = sig("shared_split"), sig("live_lo")
        w_in = [sig(f"w_in{k}", 32 * PAIRS // RING) for k in range(RING)]
        e_up, e_c, e_tanh, e_vd, e_hd, e_down = (
            sig(n, BLOCKS) for n in ("e_up", "e_c", "e_tanh", "e_vd", "e_hd", "e_down"))
        e_c.per_row = e_hd.per_row = PAIRS
        e_cs = sig("e_cs", TURNS + len(POOL_WEIGHS))
        eo_done, eT_mm, eg_done, o_done, o_out = sig("eo_done", credit=1), sig("eT_mm"), sig("eg_done"), sig("o_done", credit=1), sig("o_out", 16, credit=1)

        up_parts = nc.dram_tensor("up_parts", (PAIRS, P, 2, P), F32, kind="Internal").ap()
        mod_dram = nc.dram_tensor("mod_rows", (rows + 1, 6 * DM), F32, kind="Internal").ap()
        x_dram = A["x"].rearrange("b (t p) d -> b p t d", p=P)
        out_dram = out.rearrange("b (t p) d -> b p t d", p=P)

        def tiles_of(ap, row):
            return ap[bass.ds(row, 1)].rearrange("o p t d -> p (o t) d")

        LOADS = [
            (0, c_cm[:, :], A["c_cm"]), (0, mod_w[:, :], A["mod_w"]),
            (1, in_w[:, :], A["in_w"]), (1, conv_w[:, :, :], A["conv_w"].rearrange("(h p) k -> p h k", p=P)),
            (1, cols[:, :], A["cols"]),
            (1, xproj_w[:, :, :], A["xproj_w"].rearrange("(h p) n -> p h n", p=P)),
            (1, dtproj_w[:, :], A["dtproj_w"]),
            (1, a_neg[:, :, :], A["a_log"].rearrange("(h p) n -> p h n", p=P)),
            (2, bc_w[:, 0, :], A["b_ln"].rearrange("(o n) -> o n", o=1).to_broadcast([P, NS])),
            (2, bc_w[:, 1, :], A["c_ln"].rearrange("(o n) -> o n", o=1).to_broadcast([P, NS])),
            (2, bias_w[:, :], A["bias"].rearrange("(o n) -> o n", o=1).to_broadcast([P, EXPERTS])),
            (2, out_w[:, :, :], A["out_w"].rearrange("(h p) n -> p h n", p=P)),
            (2, gate_w[:, :], A["gate_w"]), (2, up_w[:, :], A["up_w"]),
            (2, down_w[:, :, :], A["down_w"].rearrange("(f p) n -> p f n", p=P)),
            (2, router_w[:, :], A["router_cm"]), (2, shared_up[:, :], A["shared_up"]),
            (2, shared_down[:, :], A["shared_down"]),
        ]
        N_LOADS = [16 * sum(q == k for q, _, _ in LOADS) for k in range(3)]
        N_PREP = 11

        block = ctx.enter_context(nc.Block())

        @block.sync
        def _(sp):
            for q, dst, src in LOADS:
                if q:
                    sp.dma_start(dst, src).then_inc(c_loaded[q].sem, 16)
            def load_raw(k, cut):
                sp.dma_start(raw_up[:, k, :, :], A["up"][bass.ds(cut * SPLIT, SPLIT)].rearrange("i p n -> p i n"))\
                    .then_inc(raw_in[k].sem, 16)

            def store_parts(k, cut):
                sp.wait_ge(lo_done.sem, cut + 1)
                sp.dma_start(up_parts[bass.ds(cut * SPLIT, SPLIT)].rearrange("i p a n -> p i a n"),
                             up_ring[:, k * SPLIT:(k + 1) * SPLIT, :, :]).then_inc(split_out[k].sem, 16)

            def load(k, source):
                sp.dma_start(up_ring[:, k, :, :], up_parts[bass.ds(source, 1)].rearrange("o p a n -> p (o a) n"))\
                    .then_inc(w_in[k].sem, 16)
                sp.dma_start(down_ring[:, k, :], A["down"][bass.ds(source, 1)].rearrange("o p n -> p (o n)"))\
                    .then_inc(w_in[k].sem, 16)

            for k in range(SLOTS):
                load_raw(k, k)
            sp.wait_ge(sel_done.sem, 2)
            for sel in (row_sel, pair_sel):
                for part in (1, 2):
                    sp.dma_start(sel[32 * part:32 * (part + 1), :, :], sel[0:32, :, :]).then_inc(sel_copied.sem, 16)
            with sp.Fori(0, CUTS // SLOTS - 1) as lap:
                for k in range(SLOTS):
                    store_parts(k, SLOTS * lap + k)
                    load_raw(k, SLOTS * lap + k + SLOTS)
            for k in range(SLOTS):
                store_parts(k, CUTS - SLOTS + k)
            for k in range(SLOTS):
                sp.wait_ge(split_out[k].sem, split_out[k].credit + 16 * CUTS // SLOTS)
            for k in range(RING):
                load(k, k)

            def load_g2(m):
                sp.dma_start(g2_live[:, :], mod_dram[bass.ds(m, 1), 5 * DM:].to_broadcast([P, DM]))\
                    .then_inc(g2_in.sem, 16)

            def store(row):
                sp.wait_ge(o_done.sem, o_done.by(row))
                sp.dma_start(tiles_of(out_dram, row), o_tm[:, :, :]).then_inc(o_out.sem, 16)

            def refill(row, turn, source):
                for k in range(RING):
                    sp.wait_ge(e_down.sem, e_down.by(row, RING * turn + k + 1))
                    load(k, source + k)

            sp.wait_ge(mod_out.sem, 32)
            load_g2(0)
            with sp.Fori(0, rows - 1) as row:
                with sp.Fori(0, PAIRS // RING - 1) as turn:
                    refill(row, turn, RING * turn + RING)
                refill(row, PAIRS // RING - 1, 0)
                store(row)
                load_g2(row + 1)
            with sp.Fori(0, PAIRS // RING - 1) as turn:
                refill(rows - 1, turn, RING * turn + RING)
            store(rows - 1)
            sp.wait_ge(o_out.sem, o_out.by(rows - 1))

        @block.gpsimd
        def _(pool):
            def root(dst, src, n):
                return nc.gpsimd.tensor_tensor(dst, src, neg_half[:, 0:n], ALU.pow)

            def first_roots(m):
                pool.wait_ge(ln1_var.sem, ln1_var.by(m))
                root(rstd1[:, :], var1[:, :], TILES).then_inc(ln1_rs.sem, 1)
                pool.wait_ge(ms1_done.sem, ms1_done.by(m))
                root(r1[:, :], ms1[:, :], TILES).then_inc(r1_done.sem, 1)

            def cut(lap, k):
                come, gone = 16 * (lap + 1), split_out[k].credit + 16 * lap
                if not isinstance(lap, int):
                    come, gone = (pool.snap(pool.to_reg(v)) for v in (come, gone))
                pool.wait_ge(ident_done.sem, 2)
                pool.wait_ge(raw_in[k].sem, come)
                pool.wait_ge(split_out[k].sem, gone)
                at = slice(k * SPLIT, (k + 1) * SPLIT)
                nc.gpsimd.tensor_copy(up_exact[:, at, 0, :], raw_up[:, k, :, :]).then_inc(hi_done.sem, 1)
                pool.wait_ge(hi_done.sem, SLOTS * lap + k + 1)
                nc.gpsimd.tensor_tensor(up_exact[:, at, 1, :], raw_up[:, k, :, :], up_ring[:, at, 0, :], ALU.subtract)\
                    .then_inc(lo_done.sem, 1)

            nc.gpsimd.memset(ident[:, :], 0.0).then_inc(ident_zero.sem, 1)
            nc.gpsimd.memset(identb[:, :], 0.0).then_inc(ident_zero.sem, 1)
            nc.gpsimd.memset(neg_half[:, :], -0.5).then_inc(ident_zero.sem, 1)
            for i, s in enumerate((read_done, scan_done, dbx_done, c_copied, y_done, first_read, first_y, o_done, eo_done, o_out, *split_out)):
                nc.gpsimd.memset(raised[:, i:i + 1], 0.0).then_inc(s.sem, s.credit)
            pool.wait_ge(ident_zero.sem, 3)
            for t in (ident, identb):
                nc.gpsimd.affine_select(out=t[:, :], in_=t[:, :], compare_op=ALU.not_equal, fill=1.0, base=0,
                                        pattern=[[-1, P]], channel_multiplier=1).then_inc(ident_done.sem, 1)
            nc.gpsimd.memset(pair_sel[0:32, :, :], 0.0).then_inc(ident_zero.sem, 1)
            nc.gpsimd.memset(row_sel[0:32, :, :], 0.0).then_inc(ident_zero.sem, 1)
            first_roots(0)
            pool.wait_ge(ident_zero.sem, 5)
            sel_v = pair_sel[0:32, :, :].rearrange("p j (e i) -> p j e i", e=2)
            nc.gpsimd.affine_select(out=row_sel[0:32, :, :], in_=row_sel[0:32, :, :], compare_op=ALU.not_equal,
                                    fill=1.0, base=0, pattern=[[-1, 2 * NS], [0, P]], channel_multiplier=1)\
                .then_inc(sel_done.sem, 1)
            nc.gpsimd.affine_select(out=sel_v, in_=sel_v, compare_op=ALU.not_equal, fill=1.0, base=0,
                                    pattern=[[-2, GP], [-1, 2], [0, INTER]], channel_multiplier=1)\
                .then_inc(sel_done.sem, 1)

            def weigh(row, w, copies):
                pool.wait_ge(e_hd.sem, e_hd.by(row, w.q))
                pool.wait_ge(e_vd.sem, e_vd.by(row, w.q + 1))
                pool.wait_ge(e_cs.sem, e_cs.by(row, copies))
                nc.gpsimd.tensor_tensor(e_h[:, w.h_slot, :], e_h[:, w.h_slot, :], comb_sb[w.two][:, :], ALU.mult)\
                    .then_inc(e_hd.sem, 1)

            def add_residual(row):
                pool.wait_ge(live_x1.sem, live_x1.by(row))
                pool.wait_ge(eg_done.sem, eg_done.by(row))
                pool.wait_ge(o_out.sem, o_out.by(row, 0))
                nc.gpsimd.tensor_tensor(o_tm[:, :, :], e_gat[:, :, :], x1_live[:, :, :], ALU.add).then_inc(o_done.sem, 1)

            def row_stages(m, halves, cut, in_turn):
                if cut:
                    for k in range(SLOTS):
                        cut(0, k)
                pool.wait_ge(ms3_done.sem, ms3_done.by(m))
                root(r3[:, :, 0], ms3[:, :, 0], TILES).then_inc(r3_done.sem, 1)
                nc.gpsimd.tensor_tensor(r3[:, :, 1:3], ms3[:, :, 1:3],
                                        neg_half[:, 0:2 * TILES].rearrange("p (t k) -> p t k", k=2), ALU.pow)\
                    .then_inc(r3_done.sem, 1)
                pool.wait_ge(x2_done.sem, x2_done.by(m))
                for h in range(HALVES):
                    nc.gpsimd.tensor_tensor(y[h][:, :], x2[h][:, :], cols[:, D_HALF + h:D_HALF + h + 1]
                                            .to_broadcast([P, SEQ]), ALU.mult).then_inc(y0_done.sem, 1)
                if cut:
                    for k in range(SLOTS):
                        cut(1, k)
                with pool.Fori(0, TURNS) as turn:
                    pool.wait_ge(y0_done.sem, y0_done.by(m))
                    for s in range(STATES_PER_TURN):
                        for h in halves:
                            k = STATES_PER_TURN * HALVES * turn + HALVES * s + h
                            pool.wait_ge(scan_done.sem, scan_done.by(m, k + 1))
                            pool.wait_ge(y_done.sem, y_done.by(m, k - 1))
                            if h == 0:
                                pool.wait_ge(c_copied.sem, c_copied.by(m, STATES_PER_TURN * turn + s + 1))
                            nc.gpsimd.tensor_tensor(read[h][:, :], state[s % 2][h][:, :], c_sb[s % 2][:, :], ALU.mult)\
                                .then_inc(read_done.sem, HALVES // len(halves))
                        if s == POOL_STATE:
                            in_turn(turn)
                        for h in halves:
                            k = STATES_PER_TURN * HALVES * turn + HALVES * s + h
                            pool.wait_ge(read_done.sem, read_done.by(m, k + 1))
                            nc.gpsimd.tensor_tensor(y[h][:, :], y[h][:, :], read[h][:, :], ALU.add)\
                                .then_inc(y_done.sem, HALVES // len(halves))
                        if cut:
                            for k in range(SLOTS * s // STATES_PER_TURN, SLOTS * (s + 1) // STATES_PER_TURN):
                                cut(turn + 2, k)
                pool.wait_ge(ms2_done.sem, ms2_done.by(m))
                root(r2[:, :], ms2[:, :], TILES).then_inc(r2_done.sem, 1)
                if cut:
                    for k in range(SLOTS):
                        cut(2 + TURNS, k)
                pool.wait_ge(ln2_var.sem, ln2_var.by(m))
                root(rstd2[:, :], var2[:, :], TILES).then_inc(ln2_rs.sem, 1)
                if cut:
                    for lap in range(3 + TURNS, CUTS // SLOTS):
                        for k in range(SLOTS):
                            cut(lap, k)

            row_stages(0, [0], cut, lambda turn: None)
            with pool.Fori(0, rows - 1) as row:
                first_roots(row + 1)
                row_stages(row + 1, range(HALVES), None,
                           lambda turn: weigh(row, block_in_turn(turn, POOL_IN_TURN), turn + 1))
                for i, q in enumerate(POOL_WEIGHS):
                    weigh(row, block_at(q), TURNS + i + 1)
                add_residual(row)
            add_residual(rows - 1)

        @block.tensor
        def _(pe):
            def transposed(dst, src, width, idn):
                for t in range(TILES):
                    last = nc.tensor.transpose(dst[0:width, t * P:(t + 1) * P], src(t), idn[:, :])
                return last

            def up(row, e, steady):
                shared = e.pair is None
                if steady:
                    pe.wait_ge(e_vd.sem, e_vd.by(row, e.q - 1))
                if not shared:
                    pe.wait_ge(w_in[e.slot].sem, w_in[e.slot].by(row, 32 * (e.lap + 1)))
                for w, h in ((0, 0), (0, 1), (1, 0)):
                    last = nc.tensor.matmul(up_bank[e.two][0:INTER if shared else P, :],
                                            shared_parts[:, w, :] if shared else up_exact[:, e.slot, w, :],
                                            h2_live[h][:, :], start=(w + h == 0), stop=(w == 1))
                last.then_inc(e_up.sem, 1)

            def spread_weights(row, e, steady, copies=None):
                if e.pair is None:
                    return
                if copies is not None:
                    pe.wait_ge(e_cs.sem, e_cs.by(row, copies))
                elif steady:
                    pe.wait_ge(e_hd.sem, e_hd.by(row, e.q - 1))
                nc.tensor.matmul(comb_bank[e.two][:, :], pair_sel[:, e.pair, :] if isinstance(e.pair, int) else
                                 pair_sel[:, bass.ds(e.pair, 1), :].rearrange("p o n -> p (o n)"),
                                 comb_live[:, e.group, :], start=True, stop=True).then_inc(e_c.sem, 1)

            def down(row, e, first=False, shared=False):
                if shared:
                    pe.wait_ge(e_vd.sem, e_vd.by(row))
                    nc.tensor.matmul(acc_bank[:, :], shared_down[:, :], e_h[0:INTER, e.h_slot, :], start=False,
                                     stop=True).then_inc(e_down.sem, 1)
                else:
                    pe.wait_ge(e_hd.sem, e_hd.by(row, e.q + 1))
                    nc.tensor.matmul(acc_bank[:, :], down_ring[:, e.slot, :], e_h[:, e.h_slot, :], start=first,
                                     stop=False).then_inc(e_down.sem, 1)

            def experts(row, q):
                if q < 2:
                    return
                up(row, block_at(q), steady=True)
                if q == LAG:
                    pe.wait_ge(eo_done.sem, eo_done.by(row, 0))
                if q >= LAG:
                    down(row, block_at(q - LAG), first=q == LAG)
                spread_weights(row, block_at(q), steady=True,
                               copies=TURNS + q - 1 - POOL_WEIGHS[0] if q - 2 in POOL_WEIGHS else None)

            def first_ups(row):
                pe.wait_ge(live_h2.sem, live_h2.by(row))
                pe.wait_ge(live_lo.sem, live_lo.by(row))
                if not isinstance(row, int):
                    pe.wait_ge(e_vd.sem, e_vd.by(row - 1))
                for q in range(2):
                    up(row, block_at(q), steady=False)

            def first_weights(row):
                pe.wait_ge(live_comb.sem, live_comb.by(row))
                if not isinstance(row, int):
                    pe.wait_ge(e_hd.sem, e_hd.by(row - 1))
                for q in range(2):
                    spread_weights(row, block_at(q), steady=False)

            def finish_experts(row):
                for back in range(LAG - 1, 0, -1):
                    down(row, block_at(PAIRS - back))
                down(row, block_at(PAIRS), shared=True)

            def turn_out(row):
                pe.wait_ge(eo_done.sem, eo_done.by(row))
                transposed(M[0], lambda t: e_out[:, t * P:(t + 1) * P], P, ident).then_inc(eT_mm.sem, 1)

            def row_stages(m, at, scan_experts):
                for p in ("a1", "a2", "a3", "a4", "a5", "a6", "a7"):
                    at(p)
                pe.wait_ge(hn_done.sem, hn_done.by(m))
                transposed(M[0], lambda t: hn_tm[:, t, :], P, ident).then_inc(hT_mm.sem, 1)
                at("a8")
                pe.wait_ge(hT_done.sem, hT_done.by(m))
                for h in range(HALVES):
                    nc.tensor.matmul(M[1 + h][:, :], in_w[:, h * P:(h + 1) * P], h_cm[:, :], start=True, stop=True)\
                        .then_inc(in_mm.sem, 1)
                nc.tensor.matmul(M[0][:, :], in_w[:, DI:DI + P], h_cm[:, :], start=True, stop=True)\
                    .then_inc(in_mm.sem, 1)
                at("a9")
                at("a10")
                pe.wait_ge(conv_done.sem, conv_done.by(m, TAPS))
                nc.tensor.matmul(M[1][:, :], in_w[:, DI + P:], h_cm[:, :], start=True, stop=True)\
                    .then_inc(in_mm.sem, 1)
                at("a11")
                at("a12")
                pe.wait_ge(x2_done.sem, x2_done.by(m))
                for t in range(TILES):
                    for h in range(HALVES):
                        last = nc.tensor.matmul(M[2][:, t * PROJ:(t + 1) * PROJ], x2[h][:, t * P:(t + 1) * P],
                                                xproj_w[:, h, :], start=(h == 0), stop=(h == HALVES - 1))
                last.then_inc(proj_mm.sem, 1)
                for p in ("a13", "a14", "a15", "a16"):
                    at(p)
                pe.wait_ge(prep.sem, N_PREP)
                pe.wait_ge(z2_done.sem, z2_done.by(m))
                pe.wait_ge(dtn_done.sem, dtn_done.by(m))
                transposed(M[0], lambda t: dtn_tm[:, t, :], RANK, ident).then_inc(dtT_mm.sem, 1)
                at("a17")
                pe.wait_ge(dtT_done.sem, dtT_done.by(m))
                for h in range(HALVES):
                    if h:
                        pe.wait_ge(bcn_done.sem, bcn_done.by(m))
                    nc.tensor.matmul(M[2 * h][:, :], dtproj_w[:, h * P:(h + 1) * P], dtn_cm[:, :], start=True,
                                     stop=True).then_inc(dt_mm.sem, 1)
                pe.wait_ge(bcp_done.sem, bcp_done.by(m))
                transposed(Mb[1], lambda t: bc_parts[:, t, :, :].rearrange("p s n -> p (s n)"), 96, identb)\
                    .then_inc(bcT_mm.sem, 1)
                for p in ("a18", "a19", "a20"):
                    at(p)
                with pe.Fori(0, TURNS) as turn:
                    pe.wait_ge(sel_copied.sem, 64)
                    pe.wait_ge(bcT_done.sem, bcT_done.by(m))
                    pe.wait_ge(dt_done.sem, dt_done.by(m))
                    for s in range(STATES_PER_TURN):
                        n = STATES_PER_TURN * turn + s
                        pe.wait_ge(dbx_done.sem, dbx_done.by(m, HALVES * n))
                        nc.tensor.matmul(b_bank[:, :], row_sel[:, bass.ds(n, 1), :].rearrange("p o n -> p (o n)"),
                                         bc_cm[:, :], start=True, stop=True).then_inc(b_mm.sem, 1)
                        pe.wait_ge(c_copied.sem, c_copied.by(m, n))
                        nc.tensor.matmul(c_bank[:, :], row_sel[:, bass.ds(n + NS, 1), :].rearrange("p o n -> p (o n)"),
                                         bc_cm[:, :], start=True, stop=True).then_inc(cn_mm.sem, 1)
                        for k in range(TURN_SHARE[s], TURN_SHARE[s + 1]):
                            scan_experts(turn, k)
                for p in ("c1", "c2", "c3"):
                    at(p)
                pe.wait_ge(yz_done.sem, yz_done.by(m))
                for t in range(TILES):
                    for h in range(HALVES):
                        last = nc.tensor.matmul(M[0][:, t * P:(t + 1) * P], yz[h][:, t * P:(t + 1) * P], out_w[:, h, :],
                                                start=(h == 0), stop=(h == HALVES - 1))
                last.then_inc(outp_mm.sem, 1)
                for p in ("c4", "c5"):
                    at(p)
                pe.wait_ge(hn2_done.sem, hn2_done.by(m))
                transposed(M[1], lambda t: hn_tm[:, t, :], P, ident).then_inc(hT2_mm.sem, 1)
                at("c6")
                pe.wait_ge(hT2_done.sem, hT2_done.by(m))
                for f in range(FB):
                    g, u = FFN_BANKS[f]
                    if f:
                        pe.wait_ge(fv_done.sem, fv_done.by(m, f))
                    if f >= 2:
                        pe.wait_ge(fa_done.sem, fa_done.by(m, f - 1))
                    nc.tensor.matmul(M[g][:, :], gate_w[:, f * P:(f + 1) * P], h_cm[:, :], start=True, stop=True)\
                        .then_inc(fg_mm.sem, 1)
                    nc.tensor.matmul(M[u][:, :], up_w[:, f * P:(f + 1) * P], h_cm[:, :], start=True, stop=True)\
                        .then_inc(fu_mm.sem, 1)
                    at(f"c{7 + f}")
                pe.wait_ge(fa_done.sem, fa_done.by(m))
                for t in range(TILES):
                    for f in range(FB):
                        last = nc.tensor.matmul(M[1][:, t * P:(t + 1) * P], f_act[f][:, t * P:(t + 1) * P],
                                                down_w[:, f, :], start=(f == 0), stop=(f == FB - 1))
                last.then_inc(down_mm.sem, 1)
                for p in ("c11", "c12", "c13", "c14", "c15"):
                    at(p)
                pe.wait_ge(h2_done.sem, h2_done.by(m))
                transposed(M[0], lambda t: h2_tm[:, t, :], P, ident).then_inc(h2T_mm.sem, 1)
                at("c16")
                pe.wait_ge(h2T_done.sem, h2T_done.by(m))
                for t in range(TILES):
                    last = nc.tensor.matmul(M[1 + t // 3][:, t % 3 * EXPERTS:(t % 3 + 1) * EXPERTS],
                                            h2_cm[:, t * P:(t + 1) * P], router_w[:, :], start=True, stop=True)
                last.then_inc(rt_mm.sem, 1)
                for p in ("c17", "c18", "c19", "c20", "c21"):
                    at(p)

            def turn_weights(m):
                pe.wait_ge(combp_done.sem, combp_done.by(m))
                for g in range(GROUPS):
                    half = g % 2 * SEQ
                    last = transposed(Mb[g // 2][:, half:half + SEQ],
                                      lambda t: comb_parts[:, t, g, :, :].rearrange("p s e -> p (s e)"), 96, identb)
                    if g % 2 or g == GROUPS - 1:
                        last.then_inc(combT_mm.sem, 1)

            pe.wait_ge(c_silu.sem, 1)
            nc.tensor.matmul(M[0][0:rows, :], c_sl[:, :], mod_w[:, 0:512], start=True, stop=True)
            nc.tensor.matmul(M[1][0:rows, 0:256], c_sl[:, :], mod_w[:, 512:768], start=True, stop=True)\
                .then_inc(mod_mm.sem, 1)
            pe.wait_ge(ident_done.sem, 2)
            pe.wait_ge(prep.sem, N_PREP)
            pe.wait_ge(c_loaded[2].sem, N_LOADS[2])
            row_stages(0, lambda p: None, lambda turn, k: None)
            pe.wait_ge(shared_split.sem, 2)
            first_ups(0)
            turn_weights(0)
            first_weights(0)
            with pe.Fori(0, rows - 1) as row:
                def in_scan(turn, k):
                    e = block_in_turn(turn, k)
                    up(row, e, True)
                    down(row, e.before(LAG))
                    spread_weights(row, e, True, copies=turn + 1 if k == POOL_IN_TURN + 2 else None)
                row_stages(row + 1, lambda p: experts(row, POINTS[p]), in_scan)
                finish_experts(row)
                first_ups(row + 1)
                turn_weights(row + 1)
                first_weights(row + 1)
                turn_out(row)
            for q in range(RING):
                experts(rows - 1, q)
            with pe.Fori(1, PAIRS // RING) as lap:
                for k in range(RING):
                    e = block_in_lap(lap, k)
                    up(rows - 1, e, True)
                    down(rows - 1, e.before(LAG))
                    spread_weights(rows - 1, e, True)
            experts(rows - 1, PAIRS)
            finish_experts(rows - 1)
            turn_out(rows - 1)

        @block.scalar
        def _(act):
            for q, dst, src in LOADS:
                if q == 0:
                    act.dma_start(dst, src).then_inc(c_loaded[0].sem, 16)

            def load_x(m):
                act.dma_start(x_tm[:, :, :], tiles_of(x_dram, m)).then_inc(x_in.sem, 16)

            def load_mod(m):
                act.dma_start(mod[:, :, :].rearrange("p s d -> p (s d)"),
                              mod_dram[bass.ds(m, 1), 0:5 * DM].to_broadcast([P, 5 * DM])).then_inc(mod_in.sem, 16)

            def experts(row, e):
                act.wait_ge(e_up.sem, e_up.by(row, e.q + 1))
                n = INTER if e.pair is None else P
                nc.scalar.activation(e_th[e.two][0:n, :], up_bank[e.two][0:n, :], ACT.Tanh, scale=0.5)\
                    .then_inc(e_tanh.sem, 1)

            def scaled(dst, src, r, done):
                for t in range(TILES):
                    nc.scalar.activation(dst[:, t, :], src[:, t, :], ACT.Copy, scale=r[:, t:t + 1]).then_inc(done.sem, 1)

            def copy_weights(row, w, weighed):
                act.wait_ge(e_c.sem, e_c.by(row, w.q + 1))
                act.wait_ge(e_hd.sem, e_hd.by(row, weighed))
                nc.scalar.activation(comb_sb[w.two][:, :], comb_bank[w.two][:, :], ACT.Copy).then_inc(e_cs.sem, 1)

            def experts_and_weights(row, e):
                experts(row, e)
                if e.q - 1 in POOL_WEIGHS:
                    copy_weights(row, block_at(e.q - 1), e.q - 2 if e.q - 3 in POOL_WEIGHS else FIRST_AFTER)

            def in_scan(row, turn, k):
                e = block_in_turn(turn, k)
                experts(row, e)
                if k == POOL_IN_TURN + 1:
                    w = e.before(1)
                    copy_weights(row, w, w.q - PER_TURN + 1)

            def square_sums(src, dst, done):
                for t in range(TILES):
                    nc.scalar.activation(junk[:, t, :], src[:, t, :], ACT.Square, accum_out=dst[:, t:t + 1])\
                        .then_inc(done.sem, 1)

            def row_stages(m, at, scan_experts):
                at("a3")
                at("a4")
                act.wait_ge(h_done.sem, h_done.by(m))
                square_sums(h_tm, ss1, ss1_done)
                at("a5")
                act.wait_ge(r1_done.sem, r1_done.by(m))
                scaled(hn_tm, h_tm, r1, hn_done)
                at("a6")
                at("a7")
                act.wait_ge(hT_mm.sem, hT_mm.by(m))
                nc.scalar.activation(h_cm[:, :], M[0][:, :], ACT.Copy).then_inc(hT_done.sem, 1)
                at("a8")
                at("a9")
                for h in range(HALVES):
                    act.wait_ge(conv_done.sem, conv_done.by(m, TAPS * (h + 1)))
                    nc.scalar.activation(conv_th[h][:, :], conv[h][:, :], ACT.Tanh, scale=0.5)\
                        .then_inc(convth_done.sem, 1)
                    at(f"a{10 + h}")
                act.wait_ge(in_mm.sem, in_mm.by(m, 3))
                nc.scalar.activation(z_th[0][:, :], M[0][:, :], ACT.Tanh, scale=0.5).then_inc(zth_done.sem, 1)
                act.wait_ge(in_mm.sem, in_mm.by(m, 4))
                nc.scalar.activation(z_th[1][:, :], M[1][:, :], ACT.Tanh, scale=0.5).then_inc(zth_done.sem, 1)
                at("a12")
                act.wait_ge(proj_mm.sem, proj_mm.by(m))
                nc.scalar.activation(proj_sq[:, :, :].rearrange("p t n -> p (t n)"), M[2][:, 0:TILES * PROJ], ACT.Square)\
                    .then_inc(sq3_done.sem, 1)
                for p in ("a13", "a14", "a15", "a16"):
                    at(p)
                act.wait_ge(dtT_mm.sem, dtT_mm.by(m))
                nc.scalar.activation(dtn_cm[:, :], M[0][0:RANK, :], ACT.Copy).then_inc(dtT_done.sem, 1)
                at("a17")
                for h in range(HALVES):
                    act.wait_ge(dtmin_done.sem, dtmin_done.by(m, h + 1))
                    nc.scalar.activation(dt_exp[h][:, :], dt_min[h][:, :], ACT.Exp).then_inc(dtexp_done.sem, 1)
                act.wait_ge(bcT_mm.sem, bcT_mm.by(m))
                nc.scalar.activation(bc_cm[:, :], Mb[1][0:96, 0:SEQ], ACT.Copy).then_inc(bcT_done.sem, 1)
                at("a18")
                for h in range(HALVES):
                    act.wait_ge(dtexp_done.sem, dtexp_done.by(m, h + 1))
                    nc.scalar.activation(dt_ln[h][:, :], dt_exp[h][:, :], ACT.Ln, bias=1.0).then_inc(dtln_done.sem, 1)
                at("a19")
                at("a20")
                act.wait_ge(dt_done.sem, dt_done.by(m))
                with act.Fori(0, TURNS) as turn:
                    for s in range(STATES_PER_TURN):
                        n = STATES_PER_TURN * turn + s
                        k = HALVES * n
                        act.wait_ge(cn_mm.sem, cn_mm.by(m, n + 1))
                        act.wait_ge(read_done.sem, read_done.by(m, k - HALVES))
                        if isinstance(m, int):
                            act.wait_ge(first_read.sem, first_read.by(0, n - 1))
                        nc.scalar.activation(c_sb[s % 2][:, :], c_bank[:, :], ACT.Copy).then_inc(c_copied.sem, 1)
                        cut = TURN_SHARE[s], TURN_SHARE[s] + 1, TURN_SHARE[s + 1]
                        for h in range(HALVES):
                            act.wait_ge(scan_done.sem, scan_done.by(m, k + h))
                            nc.scalar.activation(da_bank[:, :], dt[h][:, :], ACT.Exp,
                                                 scale=a_neg[:, h, bass.ds(n, 1)]).then_inc(da_done.sem, 1)
                            for b in range(cut[h], cut[h + 1]):
                                scan_experts(turn, b)
                for p in ("c1", "c2", "c3"):
                    at(p)
                act.wait_ge(hid_done.sem, hid_done.by(m))
                square_sums(hid_tm, ss2, ss2_done)
                at("c4")
                act.wait_ge(r2_done.sem, r2_done.by(m))
                scaled(hn_tm, hid_tm, r2, hn2_done)
                at("c5")
                act.wait_ge(hT2_mm.sem, hT2_mm.by(m))
                nc.scalar.activation(h_cm[:, :], M[1][:, :], ACT.Copy).then_inc(hT2_done.sem, 1)
                at("c6")
                for f in range(FB):
                    act.wait_ge(fg_mm.sem, fg_mm.by(m, f + 1))
                    nc.scalar.activation(f_th[f % 2][:, :], M[FFN_BANKS[f][0]][:, :], ACT.Tanh, scale=0.5)\
                        .then_inc(fth_done.sem, 1)
                    at(f"c{7 + f}")
                for p in ("c11", "c12", "c13", "c14", "c15"):
                    at(p)
                act.wait_ge(h2T_mm.sem, h2T_mm.by(m))
                nc.scalar.activation(h2_cm[:, :], M[0][:, :], ACT.Copy).then_inc(h2T_done.sem, 1)
                act.wait_ge(x1_done.sem, x1_done.by(m))
                load_x(m + 1)
                act.wait_ge(h2_done.sem, h2_done.by(m))
                load_mod(m + 1)
                at("c16")
                act.wait_ge(lg_done.sem, lg_done.by(m))
                nc.scalar.activation(l_exp[:, :, :], logits[:, :, :], ACT.Exp, scale=-1.0).then_inc(lexp_done.sem, 1)
                at("c17")
                nc.scalar.activation(probs[:, :, :], logits[:, :, :], ACT.Sigmoid).then_inc(probs_done.sem, 1)
                for p in ("c18", "c19", "c20", "c21"):
                    at(p)

            def take_live(m):
                act.wait_ge(h2T_done.sem, h2T_done.by(m))
                nc.scalar.activation(h2_live[0][:, :], h2_cm[:, :], ACT.Copy).then_inc(live_h2.sem, 1)

            def first_tanhs(row):
                experts(row, block_at(0))
                experts(row, block_at(1))

            def take_routing(m):
                act.wait_ge(combT_mm.sem, combT_mm.by(m, 1))
                nc.scalar.activation(comb_live[:, 0:2, :], Mb[0][0:96, 0:2 * SEQ].rearrange("p (g t) -> p g t", g=2),
                                     ACT.Copy).then_inc(live_comb.sem, 1)

            def take_sum(row):
                act.wait_ge(e_down.sem, e_down.by(row))
                nc.scalar.activation(e_out[:, :], acc_bank[:, :], ACT.Copy).then_inc(eo_done.sem, 1)

            def take_residual(m):
                act.wait_ge(x1_done.sem, x1_done.by(m))
                act.wait_ge(o_done.sem, o_done.by(m, 0))
                nc.scalar.activation(x1_live[:, :, :], x1_tm[:, :, :], ACT.Copy).then_inc(live_x1.sem, 1)

            load_x(0)
            act.wait_ge(c_loaded[0].sem, N_LOADS[0])
            nc.scalar.activation(c_th[:, :], c_cm[:, :], ACT.Tanh, scale=0.5).then_inc(c_tanh.sem, 1)
            act.wait_ge(c_loaded[1].sem, N_LOADS[1])
            act.wait_ge(c_loaded[2].sem, N_LOADS[2])
            nc.scalar.activation(a_neg[:, :, :], a_neg[:, :, :], ACT.Exp).then_inc(a_exp.sem, 1)
            act.wait_ge(mod_done.sem, mod_done.by(0, 3))
            act.dma_start(mod_dram[0:rows], mod_all[:, :, :].rearrange("b s d -> b (s d)")).then_inc(mod_out.sem, 16)
            act.dma_start(mod_dram[rows:], mod_all[0:1, :, :].rearrange("b s d -> b (s d)")).then_inc(mod_out.sem, 16)
            act.wait_ge(mod_out.sem, 32)
            load_mod(0)
            nc.scalar.activation(shared_parts[:, 0, :], shared_up[:, :], ACT.Copy).then_inc(shared_split.sem, 1)

            row_stages(0, lambda p: None, lambda turn, k: None)
            take_live(0)
            first_tanhs(0)
            take_routing(0)
            with act.Fori(0, rows - 1) as row:
                def at(p):
                    experts_and_weights(row, block_at(POINTS[p]))
                    if p == "a5":
                        take_residual(row)
                row_stages(row + 1, at, lambda turn, k: in_scan(row, turn, k))
                act.wait_ge(e_up.sem, e_up.by(row))
                take_live(row + 1)
                first_tanhs(row + 1)
                take_sum(row)
                act.wait_ge(e_c.sem, e_c.by(row))
                take_routing(row + 1)
            take_residual(rows - 1)
            for k in range(2, RING):
                experts(rows - 1, block_at(k))
            with act.Fori(1, PAIRS // RING) as lap:
                for k in range(RING):
                    experts(rows - 1, block_in_lap(lap, k))
            experts(rows - 1, block_at(PAIRS))
            take_sum(rows - 1)
            act.wait_ge(x_in.sem, x_in.by(rows))
            act.wait_ge(mod_in.sem, mod_in.by(rows))

        @block.vector
        def _(dve):
            def gate(row, e):
                n = INTER if e.pair is None else P
                if not (isinstance(e.q, int) and e.q < HRING):
                    dve.wait_ge(e_down.sem, e_down.by(row, e.q - HRING + 1))
                dve.wait_ge(e_tanh.sem, e_tanh.by(row, e.q + 1))
                nc.vector.scalar_tensor_tensor(out=e_h[0:n, e.h_slot, :], in0=e_th[e.two][0:n, :], scalar=1.0,
                                               in1=up_bank[e.two][0:n, :], op0=ALU.add, op1=ALU.mult)\
                    .then_inc(e_vd.sem, 1)

            def weigh(row, w, behind_pool=False):
                if behind_pool:
                    dve.wait_ge(e_hd.sem, e_hd.by(row, w.q))
                dve.wait_ge(e_vd.sem, e_vd.by(row, w.q + 1))
                dve.wait_ge(e_c.sem, e_c.by(row, w.q + 1))
                nc.vector.tensor_tensor(e_h[:, w.h_slot, :], e_h[:, w.h_slot, :], comb_bank[w.two][:, :],
                                        ALU.mult).then_inc(e_hd.sem, 1)

            def experts(row, e, elsewhere=()):
                if isinstance(e.q, int) and e.q < 2:
                    if e.q == 1:
                        weigh(row, e)
                    return
                gate(row, e)
                if isinstance(e.q, int) and e.q == 2:
                    return
                if not (isinstance(e.q, int) and e.q - 1 in elsewhere):
                    weigh(row, e.before(1))

            def count_of(done, m):
                return done.by(m) if isinstance(m, int) else dve.snap(dve.to_reg(done.by(m)))

            def wait_apart(done, count):
                if not isinstance(count, int):
                    dve.wait_ge(prep.sem, N_PREP)
                dve.wait_ge(done.sem, count)

            def norm_stats(m, count, src, st, st_done, agg, agg_done, var, var_done,
                           between=lambda: None):
                for t in range(TILES):
                    nc.vector.bn_stats(st[:, t, :], src[:, t, :]).then_inc(st_done.sem, 1)
                between()
                wait_apart(st_done, count)
                for t in range(TILES):
                    nc.vector.bn_aggr(agg[:, t, :], st[:, t, :]).then_inc(agg_done.sem, 1)
                dve.wait_ge(agg_done.sem, agg_done.by(m))
                nc.vector.tensor_scalar(var[:, :], agg[:, :, 1], EPS_LN, None, ALU.add).then_inc(var_done.sem, 1)

            def modulated(m, src, agg, rs, rs_done, scale, shift, mid, mid_done, dst, done,
                          between=lambda: None):
                for t in range(TILES):
                    nc.vector.scalar_tensor_tensor(out=mid[:, t, :], in0=src[:, t, :], scalar=agg[:, t, 0:1],
                                                   in1=mod[:, scale, :], op0=ALU.subtract, op1=ALU.mult)\
                        .then_inc(mid_done.sem, 1)
                between()
                dve.wait_ge(mid_done.sem, mid_done.by(m))
                dve.wait_ge(rs_done.sem, rs_done.by(m))
                for t in range(TILES):
                    nc.vector.scalar_tensor_tensor(out=dst[:, t, :], in0=mid[:, t, :], scalar=rs[:, t:t + 1],
                                                   in1=mod[:, shift, :], op0=ALU.mult, op1=ALU.add)\
                        .then_inc(done.sem, 1)

            def gated(th, src, dst, done):
                nc.vector.scalar_tensor_tensor(out=dst, in0=th, scalar=1.0, in1=src, op0=ALU.add, op1=ALU.mult)\
                    .then_inc(done.sem, 1)

            def convolve(m, h, between=lambda: None):
                src = M[1 + h]
                dve.wait_ge(in_mm.sem, in_mm.by(m, h + 1))
                nc.vector.tensor_scalar(conv[h][:, :], src[:, :], conv_w[:, h, TAPS - 1:TAPS],
                                        cols[:, CONV_B + h:CONV_B + h + 1], ALU.mult, ALU.add)\
                    .then_inc(conv_done.sem, 1)
                between()
                for back in range(1, TAPS):
                    dve.wait_ge(conv_done.sem, conv_done.by(m, TAPS * h + back))
                    nc.vector.scalar_tensor_tensor(out=conv[h][:, back:], in0=src[:, 0:SEQ - back],
                                                   scalar=conv_w[:, h, TAPS - 1 - back:TAPS - back],
                                                   in1=conv[h][:, back:], op0=ALU.mult, op1=ALU.add)\
                        .then_inc(conv_done.sem, 1)

            def thirds(m, src, rem, parts, done):
                nc.vector.tensor_copy(parts(0), src).then_inc(done.sem, 1)
                dve.wait_ge(done.sem, done.by(m, 1))
                nc.vector.tensor_tensor(rem, src, parts(0), ALU.subtract).then_inc(done.sem, 1)
                dve.wait_ge(done.sem, done.by(m, 2))
                nc.vector.tensor_copy(parts(1), rem).then_inc(done.sem, 1)
                dve.wait_ge(done.sem, done.by(m, 3))
                nc.vector.tensor_tensor(parts(2), rem, parts(1), ALU.subtract).then_inc(done.sem, 1)

            def inputs_of(m, n, h):
                dve.wait_ge(b_mm.sem, b_mm.by(m, n + 1))
                dve.wait_ge(scan_done.sem, scan_done.by(m, HALVES * n - 1 + h))
                nc.vector.tensor_tensor(dbx[h][:, :], dtx[h][:, :], b_bank[:, :], ALU.mult).then_inc(dbx_done.sem, 1)

            def scan_state(m, n, s, h):
                k = HALVES * n + h
                dve.wait_ge(dbx_done.sem, dbx_done.by(m, k + 1))
                dve.wait_ge(da_done.sem, da_done.by(m, k + 1))
                dve.wait_ge(read_done.sem, read_done.by(m, k - 3))
                nc.vector.tensor_tensor_scan(state[s % 2][h][:, :], da_bank[:, :], dbx[h][:, :], 0.0,
                                             ALU.mult, ALU.add).then_inc(scan_done.sem, 1)

            def scan_beside_experts(row):
                m = row + 1
                with dve.Fori(0, TURNS) as turn:
                    dve.wait_ge(dtx_done.sem, dtx_done.by(m))
                    for s in range(STATES_PER_TURN):
                        n = STATES_PER_TURN * turn + s
                        cut = TURN_SHARE[s], TURN_SHARE[s] + 1, TURN_SHARE[s + 1]
                        for h in range(HALVES):
                            inputs_of(m, n, h)
                        for h in range(HALVES):
                            scan_state(m, n, s, h)
                            for b in range(cut[h], cut[h + 1]):
                                e = block_in_turn(turn, b)
                                gate(row, e)
                                if b != POOL_IN_TURN + 1:
                                    weigh(row, e.before(1), behind_pool=b == POOL_IN_TURN + 2)

            def first_scan():
                def read_out(n, s):
                    dve.wait_ge(scan_done.sem, scan_done.by(0, HALVES * (n + 1)))
                    dve.wait_ge(c_copied.sem, c_copied.by(0, n + 1))
                    dve.wait_ge(first_y.sem, first_y.by(0, n))
                    nc.vector.tensor_tensor(read[1][:, :], state[s % 2][1][:, :], c_sb[s % 2][:, :], ALU.mult)\
                        .then_inc(first_read.sem, 1)

                def add(n):
                    dve.wait_ge(first_read.sem, first_read.by(0, n + 1))
                    nc.vector.tensor_tensor(y[1][:, :], y[1][:, :], read[1][:, :], ALU.add).then_inc(first_y.sem, 1)

                with dve.Fori(0, TURNS) as turn:
                    dve.wait_ge(dtx_done.sem, dtx_done.by(0))
                    dve.wait_ge(y0_done.sem, y0_done.by(0))
                    for s in range(STATES_PER_TURN):
                        n = STATES_PER_TURN * turn + s
                        inputs_of(0, n, 0)
                        if s:
                            read_out(n - 1, s - 1)
                        scan_state(0, n, s, 0)
                        inputs_of(0, n, 1)
                        if s:
                            add(n - 1)
                        scan_state(0, n, s, 1)
                    read_out(n, s)
                    add(n)

            def norm_of_x(m, at):
                counts = {d: count_of(d, m) for d in (ln1_st, ln2_st, lone_done, top_done)}
                dve.wait_ge(x_in.sem, x_in.by(m))
                norm_stats(m, counts[ln1_st], x_tm, stats, ln1_st, mv, ln1_mv, var1, ln1_var)
                return counts

            def row_stages(m, counts, at, scan):
                at("a2")
                at("a3")
                dve.wait_ge(mod_in.sem, mod_in.by(m))
                modulated(m, x_tm, mv, rstd1, ln1_rs, SC1, SH1, hs_tm, hs_done, h_tm, h_done)
                at("a4")
                dve.wait_ge(ss1_done.sem, ss1_done.by(m))
                nc.vector.tensor_scalar(ms1[:, :], ss1[:, :], 1.0 / DM, EPS_RMS, ALU.mult, ALU.add)\
                    .then_inc(ms1_done.sem, 1)
                for p in ("a5", "a6", "a7"):
                    at(p)
                at("a8")
                convolve(m, 0)
                at("a9")
                convolve(m, 1, lambda: at("w9"))
                at("a10")
                for h in range(HALVES):
                    dve.wait_ge(convth_done.sem, convth_done.by(m, h + 1))
                    gated(conv_th[h][:, :], conv[h][:, :], x2[h][:, :], x2_done)
                at("a11")
                at("a12")
                dve.wait_ge(zth_done.sem, zth_done.by(m, 1))
                gated(z_th[0][:, :], M[0][:, :], z2[0][:, :], z2_done)
                dve.wait_ge(zth_done.sem, zth_done.by(m, 2))
                gated(z_th[1][:, :], M[1][:, :], z2[1][:, :], z2_done)
                at("a13")
                dve.wait_ge(sq3_done.sem, sq3_done.by(m))
                nc.vector.tensor_reduce(ss3[:, :, 0], proj_sq[:, :, 0:RANK], AX_X, ALU.add).then_inc(ss3_done.sem, 1)
                nc.vector.tensor_reduce(ss3[:, :, 1:3], proj_sq[:, :, RANK:].rearrange("p t (k n) -> p t k n", k=2),
                                        AX_X, ALU.add).then_inc(ss3_done.sem, 1)
                dve.wait_ge(ss3_done.sem, ss3_done.by(m))
                nc.vector.tensor_scalar(ms3[:, :, 0], ss3[:, :, 0], 1.0 / RANK, EPS_RMS, ALU.mult, ALU.add)\
                    .then_inc(ms3_done.sem, 1)
                nc.vector.tensor_scalar(ms3[:, :, 1:3], ss3[:, :, 1:3], 1.0 / NS, EPS_RMS, ALU.mult, ALU.add)\
                    .then_inc(ms3_done.sem, 1)
                at("a14")
                at("a15")
                dve.wait_ge(r3_done.sem, r3_done.by(m, 1))
                proj = M[2][:, 0:TILES * PROJ].rearrange("p (t n) -> p t n", t=TILES)
                nc.vector.tensor_tensor(dtn_tm[:, :, :], proj[:, :, 0:RANK],
                                        r3[:, :, 0:1].to_broadcast([P, TILES, RANK]), ALU.mult).then_inc(dtn_done.sem, 1)
                at("a16")
                dve.wait_ge(r3_done.sem, r3_done.by(m))
                nc.vector.tensor_tensor(bcn[:, :, :].rearrange("p t (k n) -> p t k n", k=2),
                                        proj[:, :, RANK:].rearrange("p t (k n) -> p t k n", k=2),
                                        r3[:, :, 1:3].rearrange("p t (k o) -> p t k o", o=1)
                                        .to_broadcast([P, TILES, 2, NS]), ALU.mult).then_inc(bcn_done.sem, 1)
                dve.wait_ge(bcn_done.sem, bcn_done.by(m))
                nc.vector.tensor_tensor(bcs[:, :, :], bcn[:, :, :],
                                        bc_w[:, :, :].rearrange("p (o k) n -> p o (k n)", o=1)
                                        .to_broadcast([P, TILES, 2 * NS]), ALU.mult).then_inc(bcs_done.sem, 1)
                dve.wait_ge(bcs_done.sem, bcs_done.by(m))
                thirds(m, bcs[:, :, :], bc_rem[:, :, :], lambda i: bc_parts[:, :, i, :], bcp_done)
                at("a17")
                for h in range(HALVES):
                    dve.wait_ge(dt_mm.sem, dt_mm.by(m, h + 1))
                    nc.vector.tensor_scalar(dt_min[h][:, :], M[2 * h][:, :], cols[:, DT_B + h:DT_B + h + 1], 30.0,
                                            ALU.add, ALU.min).then_inc(dtmin_done.sem, 1)
                at("a18")
                at("w18")
                for h in range(HALVES):
                    dve.wait_ge(dtln_done.sem, dtln_done.by(m, h + 1))
                    nc.vector.scalar_tensor_tensor(out=dt[h][:, :], in0=M[2 * h][:, :],
                                                   scalar=cols[:, DT_B + h:DT_B + h + 1], in1=dt_ln[h][:, :],
                                                   op0=ALU.add, op1=ALU.max).then_inc(dt_done.sem, 1)
                for h in range(HALVES):
                    dve.wait_ge(dt_done.sem, dt_done.by(m, h + 1))
                    nc.vector.tensor_tensor(dtx[h][:, :], dt[h][:, :], x2[h][:, :], ALU.mult).then_inc(dtx_done.sem, 1)
                at("a19")
                at("a20")
                scan()
                at("c1")
                at("c2")
                for h in range(HALVES):
                    dve.wait_ge(y_done.sem, y_done.by(m, 2 * NS - 1 + h))
                    if h and isinstance(m, int):
                        dve.wait_ge(first_y.sem, first_y.by(0))
                    nc.vector.tensor_tensor(yz[h][:, :], y[h][:, :], z2[h][:, :], ALU.mult).then_inc(yz_done.sem, 1)
                at("c3")
                dve.wait_ge(outp_mm.sem, outp_mm.by(m))
                nc.vector.tensor_tensor(hid_tm[:, :, :], M[0][:, :].rearrange("p (t d) -> p t d", t=TILES),
                                        h_tm[:, :, :], ALU.add).then_inc(hid_done.sem, 1)
                dve.wait_ge(ss2_done.sem, ss2_done.by(m))
                nc.vector.tensor_scalar(ms2[:, :], ss2[:, :], 1.0 / DM, EPS_RMS, ALU.mult, ALU.add)\
                    .then_inc(ms2_done.sem, 1)
                at("c4")
                at("c5")
                at("c6")
                for f in range(FB):
                    g, u = FFN_BANKS[f]
                    dve.wait_ge(fth_done.sem, fth_done.by(m, f + 1))
                    gated(f_th[f % 2][:, :], M[g][:, :], f_v[f % 2][:, :], fv_done)
                    dve.wait_ge(fv_done.sem, fv_done.by(m, f + 1))
                    dve.wait_ge(fu_mm.sem, fu_mm.by(m, f + 1))
                    nc.vector.tensor_tensor(f_act[f][:, :], f_v[f % 2][:, :], M[u][:, :], ALU.mult)\
                        .then_inc(fa_done.sem, 1)
                    at(f"c{7 + f}")
                dve.wait_ge(down_mm.sem, down_mm.by(m))
                nc.vector.tensor_tensor(att_tm[:, :, :], M[1][:, :].rearrange("p (t d) -> p t d", t=TILES),
                                        hid_tm[:, :, :], ALU.add).then_inc(att_done.sem, 1)
                dve.wait_ge(att_done.sem, att_done.by(m))
                nc.vector.tensor_tensor(gat_tm[:, :, :], att_tm[:, :, :],
                                        mod[:, G1:G1 + 1, :].to_broadcast([P, TILES, DM]), ALU.mult)\
                    .then_inc(gat_done.sem, 1)
                at("c11")
                dve.wait_ge(gat_done.sem, gat_done.by(m))
                nc.vector.tensor_tensor(x1_tm[:, :, :], gat_tm[:, :, :], x_tm[:, :, :], ALU.add).then_inc(x1_done.sem, 1)
                at("c12")
                dve.wait_ge(x1_done.sem, x1_done.by(m))
                norm_stats(m, counts[ln2_st], x1_tm, stats2, ln2_st, mv2, ln2_mv, var2, ln2_var, lambda: at("wc12"))
                at("c13")
                modulated(m, x1_tm, mv2, rstd2, ln2_rs, SC2, SH2, hs2_tm, hs2_done, h2_tm, h2_done,
                          lambda: at("wc13"))
                for p in ("c14", "c15", "c16"):
                    at(p)
                dve.wait_ge(rt_mm.sem, rt_mm.by(m))
                nc.vector.tensor_tensor(logits[:, 0:3, :], M[1][:, 0:3 * EXPERTS].rearrange("p (t e) -> p t e", t=3),
                                        bias_w[:, :].rearrange("p (o e) -> p o e", o=1)
                                        .to_broadcast([P, 3, EXPERTS]), ALU.add).then_inc(lg_done.sem, 1)
                nc.vector.tensor_tensor(logits[:, 3, :], M[2][:, 0:EXPERTS], bias_w[:, :], ALU.add)\
                    .then_inc(lg_done.sem, 1)
                at("c17")
                dve.wait_ge(lexp_done.sem, lexp_done.by(m))
                nc.vector.tensor_scalar(minus_u[:, :, :], l_exp[:, :, :], -1.0, -1.0, ALU.mult, ALU.add)\
                    .then_inc(lone_done.sem, 1)
                wait_apart(lone_done, counts[lone_done])
                for t in range(TILES):
                    nc.vector.max(top[:, t, :], minus_u[:, t, :]).then_inc(top_done.sem, 1)
                at("c18")
                at("c19")
                wait_apart(top_done, counts[top_done])
                for t in range(TILES):
                    nc.vector.match_replace(rest[:, t, :], in_to_replace=top[:, t, :], in_values=minus_u[:, t, :],
                                            imm_value=TAKEN).then_inc(rest_done.sem, 1)
                at("c20")
                dve.wait_ge(rest_done.sem, rest_done.by(m))
                dve.wait_ge(probs_done.sem, probs_done.by(m))
                nc.vector.scalar_tensor_tensor(out=chosen[:, :, :], in0=rest[:, :, :], scalar=TAKEN,
                                               in1=probs[:, :, :], op0=ALU.is_equal, op1=ALU.mult)\
                    .then_inc(chosen_done.sem, 1)
                nc.vector.reciprocal(top_prob[:, :, :], top[:, :, :]).then_inc(topp_done.sem, 1)
                at("c21")
                dve.wait_ge(live_h2.sem, live_h2.by(m))
                nc.vector.tensor_tensor(h2_live[1][:, :], h2_cm[:, :], h2_live[0][:, :].bitcast(F32), ALU.subtract)\
                    .then_inc(live_lo.sem, 1)
                dve.wait_ge(topp_done.sem, topp_done.by(m))
                nc.vector.tensor_reduce(top_sum[:, :], top_prob[:, :, :], AX_X, ALU.add).then_inc(tops_done.sem, 1)
                dve.wait_ge(tops_done.sem, tops_done.by(m, 1))
                nc.vector.tensor_scalar(top_inv[:, :], top_sum[:, :], -1.0, 1e-9, ALU.mult, ALU.add).then_inc(tops_done.sem, 1)
                dve.wait_ge(tops_done.sem, tops_done.by(m, 2))
                nc.vector.reciprocal(top_fac[:, :], top_inv[:, :]).then_inc(tops_done.sem, 1)
                dve.wait_ge(tops_done.sem, tops_done.by(m, 3))
                dve.wait_ge(chosen_done.sem, chosen_done.by(m))
                for t in range(TILES):
                    nc.vector.tensor_scalar(comb[:, t, :], chosen[:, t, :], top_fac[:, t:t + 1], SCALE / 2,
                                            ALU.mult, ALU.mult).then_inc(comb_done.sem, 1)
                dve.wait_ge(comb_done.sem, comb_done.by(m))
                as_groups = "p t (g e) -> p t g e"
                thirds(m, comb[:, :, :].rearrange(as_groups, g=GROUPS), comb_rem[:, :, :].rearrange(as_groups, g=GROUPS),
                       lambda i: comb_parts[:, :, :, i, :], combp_done)

            def take_live(m):
                gate(m, block_at(0))
                gate(m, block_at(1))
                dve.wait_ge(combT_mm.sem, combT_mm.by(m))
                for b in (1, 2):
                    g = min(2, GROUPS - 2 * b)
                    nc.vector.tensor_copy(comb_live[:, 2 * b:2 * b + g, :],
                                          Mb[b][0:96, 0:g * SEQ].rearrange("p (g t) -> p g t", g=g))\
                        .then_inc(live_comb.sem, 1)
                weigh(m, block_at(0))

            def finish_row(row, first):
                dve.wait_ge(g2_in.sem, g2_in.by(row))
                dve.wait_ge(eT_mm.sem, eT_mm.by(row))
                nc.vector.tensor_tensor(e_gat[:, :, :], M[0][:, :].rearrange("p (t d) -> p t d", t=TILES),
                                        g2_live[:, :].rearrange("p (o d) -> p o d", o=1)
                                        .to_broadcast([P, TILES, DM]), ALU.mult).then_inc(eg_done.sem, 1)

            counts = norm_of_x(0, lambda p: None)
            dve.wait_ge(c_tanh.sem, 1)
            gated(c_th[:, :], c_cm[:, :], c_sl[:, :], c_silu)
            dve.wait_ge(mod_mm.sem, 1)
            flat = mod_all[:, :, :].rearrange("b s d -> b (s d)")
            nc.vector.tensor_scalar(flat[:, 0:512], M[0][0:rows, :], 0.5, None, ALU.mult).then_inc(mod_half.sem, 1)
            nc.vector.tensor_scalar(flat[:, 512:768], M[1][0:rows, 0:256], 0.5, None, ALU.mult).then_inc(mod_half.sem, 1)
            dve.wait_ge(mod_half.sem, 2)
            nc.vector.tensor_scalar(mod_all[:, SC1::3, :], mod_all[:, SC1::3, :], 1.0, None, ALU.add)\
                .then_inc(mod_done.sem, 1)
            for i, slot in enumerate((G1, G2)):
                nc.vector.scalar_tensor_tensor(out=mod_abs[:, i, :], in0=mod_all[:, slot, :], scalar=-1.0,
                                               in1=mod_all[:, slot, :], op0=ALU.mult, op1=ALU.max)\
                    .then_inc(mod_raw.sem, 1)
            nc.vector.tensor_scalar(mod_sgn[:, :, :], mod_all[:, G1::3, :], 0.0, 2.0, ALU.is_ge, ALU.mult)\
                .then_inc(mod_raw.sem, 1)
            dve.wait_ge(mod_raw.sem, 3)
            nc.vector.tensor_scalar(mod_abs[:, :, :], mod_abs[:, :, :], 0.25, None, ALU.max).then_inc(mod_raw.sem, 1)
            dve.wait_ge(mod_raw.sem, 4)
            for i, slot in enumerate((G1, G2)):
                nc.vector.scalar_tensor_tensor(out=mod_all[:, slot, :], in0=mod_sgn[:, i, :], scalar=-1.0,
                                               in1=mod_abs[:, i, :], op0=ALU.add, op1=ALU.mult)\
                    .then_inc(mod_done.sem, 1)
            dve.wait_ge(c_loaded[1].sem, N_LOADS[1])
            dve.wait_ge(c_loaded[2].sem, N_LOADS[2])
            dve.wait_ge(a_exp.sem, 1)
            for t, scale in ((in_w[:, :], cols[:, IN_LN:IN_LN + 1]), (gate_w[:, :], cols[:, PRE_LN:PRE_LN + 1]),
                             (up_w[:, :], cols[:, PRE_LN:PRE_LN + 1]),
                             (dtproj_w[:, :], cols[0:RANK, DT_LN:DT_LN + 1]), (xproj_w[:, :, :], 0.5),
                             (out_w[:, :, :], 0.5), (down_w[:, :, :], 0.5), (shared_down[:, :], 0.5),
                             (bc_w[:, 0, :], 0.5), (cols[:, D_HALF:D_HALF + 2], 0.5), (a_neg[:, :, :], -1.0)):
                nc.vector.tensor_scalar(t, t, scale, None, ALU.mult).then_inc(prep.sem, 1)
            dve.wait_ge(prep.sem, N_PREP)
            dve.wait_ge(shared_split.sem, 1)
            nc.vector.tensor_tensor(shared_parts[:, 1, :], shared_up[:, :], shared_parts[:, 0, :].bitcast(F32), ALU.subtract)\
                .then_inc(shared_split.sem, 1)

            row_stages(0, counts, lambda p: None, first_scan)
            take_live(0)
            with dve.Fori(0, rows - 1) as row:
                def at(p):
                    if p in EARLY:
                        weigh(row, block_at(EARLY[p]))
                    else:
                        experts(row, block_at(POINTS[p]), elsewhere=(*POOL_WEIGHS, *EARLY.values()))
                counts = norm_of_x(row + 1, at)
                row_stages(row + 1, counts, at, lambda: scan_beside_experts(row))
                dve.wait_ge(e_c.sem, e_c.by(row))
                take_live(row + 1)
                finish_row(row, False)
            for k in range(RING):
                experts(rows - 1, block_at(k))
            with dve.Fori(1, PAIRS // RING) as lap:
                for k in range(RING):
                    experts(rows - 1, block_in_lap(lap, k))
            experts(rows - 1, block_at(PAIRS))
            finish_row(rows - 1, True)


def kernel(**inputs):
    import numpy as np
    import concourse.bacc as bacc
    from concourse.bass_utils import run_bass_kernel_spmd as run

    i = {k.replace("L0_", ""): np.asarray(v) for k, v in inputs.items()}
    rows = i["attn_hidden_states"].shape[0]

    def lay(a):
        return np.ascontiguousarray(a)

    up = i["ffn_w_gate"].reshape(GROUPS, GP, 2, INTER, DM).transpose(1, 0, 4, 2, 3).reshape(PAIRS, P, P)
    down = i["ffn_w_down"].reshape(GROUPS, GP, 2, DM, INTER).transpose(1, 0, 2, 4, 3).reshape(PAIRS, P, P)
    cols = np.zeros((P, 9), np.float32)
    for at, name in ((0, "attn_conv_b"), (2, "attn_dt_proj_b"), (4, "attn_D_skip"), (6, "attn_input_ln_w"),
                     (7, "attn_pre_moe_ln_w")):
        v = i[name].reshape(-1, P)
        cols[:, at:at + len(v)] = v.T
    cols[:RANK, 8] = i["attn_dt_ln_w"]
    arrays = {
        "x": np.concatenate([i["attn_hidden_states"], np.zeros((1, SEQ, DM), np.float32)]), "in_w": lay(i["attn_in_proj_w"]), "conv_w": lay(i["attn_conv_w"]),
        "cols": cols, "xproj_w": lay(i["attn_x_proj_w"]), "dtproj_w": lay(i["attn_dt_proj_w"]),
        "b_ln": lay(i["attn_b_ln_w"]),
        "c_ln": lay(i["attn_c_ln_w"]), "a_log": lay(i["attn_A_log"]),
        "out_w": lay(i["attn_out_proj_w"]),
        "gate_w": lay(i["attn_gate_w"]), "up_w": lay(i["attn_up_w"]), "down_w": lay(i["attn_down_w"]),
        "router_cm": lay(i["ffn_router_w"].T), "bias": lay(i["ffn_expert_bias"]),
        "up": lay(up), "down": lay(down),
        "shared_up": lay(i["ffn_w_gate_shared"].T), "shared_down": lay(i["ffn_w_down_shared"].T),
        "c_cm": lay(i["c"].T), "mod_w": lay(i["wmod"]),
    }
    nc = bacc.Bacc("TRN2", target_bir_lowering=False, num_devices=1)
    args = {n: nc.dram_tensor(f"in_{n}", a.shape, F32, kind="ExternalInput").ap() for n, a in arrays.items()}
    out = nc.dram_tensor("out_0", (rows, SEQ, DM), F32, kind="ExternalOutput").ap()
    build(nc, args, out, rows)
    r = run(nc, [{f"in_{n}": a for n, a in arrays.items()}], core_ids=[0])
    return r.results[0]["out_0"]
```
